# Optimizing a Trainium2 kernel written in Bass

```python
import numpy as np
import jax
import jax.numpy as jnp

def _softmax(x, axis=-1):
    return jax.nn.softmax(x, axis=axis)

def _gelu(x):
    return jax.nn.gelu(x, approximate=True)

def _silu(x):
    return jax.nn.silu(x)

def _sigmoid(x):
    return jax.nn.sigmoid(x)

def _layernorm(x, axis=-1, eps=1e-05):
    m = jnp.mean(x, axis=axis, keepdims=True)
    v = jnp.var(x, axis=axis, keepdims=True)
    return (x - m) / jnp.sqrt(v + eps)

def _scatter_add(tgt, idx, src, axis=0):
    return tgt.at[idx].add(src)

def _segment_sum(src, seg, n):
    return jax.ops.segment_sum(src, seg, n)
kernel_name = 'mk_macaron_d4_jaxref_r8_f64534'

def setup_inputs(seed: int=0):
    np.random.seed(seed)
    _w = jnp.asarray

    def _L0_attn_setup():
        import jax, jax.numpy as jnp
        import numpy as np
        B, S, D, H = (4, 256, 128, 16)
        HD = D // H
        LB = 0.0
        EPS = 1e-05
        key = jax.random.key(seed)
        ks = jax.random.split(key, 8)
        s = 1.0 / np.sqrt(D)
        W = lambda k: jax.random.normal(k, (D, D), jnp.float32) * s
        return {'x': jax.random.normal(ks[0], (B, S, D), jnp.float32), 'Wq': W(ks[1]), 'Wk': W(ks[2]), 'Wv': W(ks[3]), 'Wf': W(ks[4]), 'bf': jnp.zeros((D,), jnp.float32), 'Wg': W(ks[5]), 'Wout': W(ks[6]), 'gamma': jnp.ones((D,), jnp.float32), 'beta': jnp.zeros((D,), jnp.float32)}
    _L0_attn_in = _L0_attn_setup()

    def _L0_ffn_setup():
        import jax, jax.numpy as jnp
        import numpy as np
        EMB = 128
        FF = 4 * EMB

        def _ternary(w):
            scale = jnp.maximum(jnp.mean(jnp.abs(w)), 1e-08)
            w_t = jnp.clip(jnp.round(w / scale), -1.0, 1.0)
            return w + jax.lax.stop_gradient(w_t - w)
        key = jax.random.key(seed)
        kx, k1, k2, kb1, kb2 = jax.random.split(key, 5)
        x = jax.random.normal(kx, (4, 256, EMB), dtype=jnp.float32)
        lim1 = 1.0 / np.sqrt(EMB)
        lim2 = 1.0 / np.sqrt(FF)
        W1 = jax.random.uniform(k1, (FF, EMB), jnp.float32, -lim1, lim1)
        b1 = jax.random.uniform(kb1, (FF,), jnp.float32, -lim1, lim1)
        W2 = jax.random.uniform(k2, (EMB, FF), jnp.float32, -lim2, lim2)
        b2 = jax.random.uniform(kb2, (EMB,), jnp.float32, -lim2, lim2)
        return {'x': x, 'W1': W1, 'b1': b1, 'W2': W2, 'b2': b2}
    _L0_ffn_in = _L0_ffn_setup()

    def _L1_attn_setup():
        import jax, jax.numpy as jnp
        import numpy as np
        import math
        N_HEAD = 16

        def _causal_attn(q, k, v):
            d_k = q.shape[-1]
            s = jnp.einsum('bhqd,bhkd->bhqk', q, k) / math.sqrt(d_k)
            L, S = (q.shape[-2], k.shape[-2])
            mask = jnp.tril(jnp.ones((L, S), dtype=bool))
            s = jnp.where(mask, s, -jnp.inf)
            a = jax.nn.softmax(s, axis=-1)
            return jnp.einsum('bhqk,bhkd->bhqd', a, v)
        key = jax.random.key(seed)
        ks = jax.random.split(key, 8)
        B, T, C = (2, 256, 128)
        scale = 0.02
        return {'x': jax.random.normal(ks[0], (B, T, C), dtype=jnp.float32), 'W_attn': jax.random.normal(ks[1], (C, 2 * C), dtype=jnp.float32) * scale, 'b_attn': jnp.zeros((2 * C,), dtype=jnp.float32), 'W_k2': jax.random.normal(ks[2], (C, C), dtype=jnp.float32) * scale, 'b_k2': jnp.zeros((C,), dtype=jnp.float32), 'W_proj': jax.random.normal(ks[3], (C, C), dtype=jnp.float32) * scale, 'b_proj': jnp.zeros((C,), dtype=jnp.float32)}
    _L1_attn_in = _L1_attn_setup()

    def _L1_ffn_setup():
        import jax, jax.numpy as jnp
        import numpy as np
        D_MODEL, D_FF, N_EXP = (128, 512, 8)
        key = jax.random.key(seed)
        ks = jax.random.split(key, 8)
        s = lambda fan_in: 1.0 / np.sqrt(fan_in)
        x = jax.random.normal(ks[0], (4, 256, D_MODEL), dtype=jnp.float32)
        Wr = jax.random.uniform(ks[1], (N_EXP, D_MODEL), jnp.float32, -s(D_MODEL), s(D_MODEL))
        br = jax.random.uniform(ks[2], (N_EXP,), jnp.float32, -s(D_MODEL), s(D_MODEL))
        W1 = jax.random.uniform(ks[3], (N_EXP, D_FF, D_MODEL), jnp.float32, -s(D_MODEL), s(D_MODEL))
        b1 = jax.random.uniform(ks[4], (N_EXP, D_FF), jnp.float32, -s(D_MODEL), s(D_MODEL))
        W2 = jax.random.uniform(ks[5], (N_EXP, D_MODEL, D_FF), jnp.float32, -s(D_FF), s(D_FF))
        b2 = jax.random.uniform(ks[6], (N_EXP, D_MODEL), jnp.float32, -s(D_FF), s(D_FF))
        return {'x': x, 'Wr': Wr, 'br': br, 'W1': W1, 'b1': b1, 'W2': W2, 'b2': b2}
    _L1_ffn_in = _L1_ffn_setup()

    def _L2_attn_setup():
        import jax, jax.numpy as jnp
        import numpy as np
        DIM = 128
        DIM_HEAD = 64
        N_HEADS = 16
        INNER = DIM_HEAD * N_HEADS
        LN_EPS = 1e-05

        def layer_norm(x, gamma, beta):
            mu = jnp.mean(x, axis=-1, keepdims=True)
            var = jnp.var(x, axis=-1, keepdims=True)
            return (x - mu) * jax.lax.rsqrt(var + LN_EPS) * gamma + beta

        def alibi_bias(seq, n_heads):
            n_sequence = jnp.arange(n_heads, 0, -1).astype(jnp.float32)
            head_scalars = 2.0 ** (-8.0 / n_sequence)
            idx = jnp.arange(seq)
            dist = -jnp.abs(idx[:, None] - idx[None, :]).astype(jnp.float32)
            return head_scalars[:, None, None] * dist
        key = jax.random.key(seed)
        ks = jax.random.split(key, 6)
        B, S = (2, 256)
        scale = 0.02
        return {'x': jax.random.normal(ks[0], (B, S, DIM), dtype=jnp.float32), 'ln_gamma': jnp.ones((DIM,), dtype=jnp.float32), 'ln_beta': jnp.zeros((DIM,), dtype=jnp.float32), 'Wq': jax.random.normal(ks[1], (DIM, INNER), dtype=jnp.float32) * scale, 'Wk': jax.random.normal(ks[2], (DIM, INNER), dtype=jnp.float32) * scale, 'Wv': jax.random.normal(ks[3], (DIM, INNER), dtype=jnp.float32) * scale, 'Wo': jax.random.normal(ks[4], (INNER, DIM), dtype=jnp.float32) * scale}
    _L2_attn_in = _L2_attn_setup()

    def _L2_ffn_setup():
        import jax, jax.numpy as jnp
        import numpy as np
        EPS = 1e-08

        def _ternary_linear(x, w):
            alpha = jnp.mean(jnp.abs(w))
            w_t = jnp.sign(w) * (jnp.abs(w) > 0.5 * alpha).astype(w.dtype)
            w_q = w + jax.lax.stop_gradient(w_t - w)
            d = x.shape[-1]
            rms = jnp.sqrt(jnp.sum(x * x, axis=-1, keepdims=True)) / jnp.sqrt(jnp.asarray(d, x.dtype))
            x_norm = x / (rms + EPS)
            return jnp.einsum('bsd,fd->bsf', x_norm, w_q)
        key = jax.random.key(seed)
        k1, k2, k3 = jax.random.split(key, 3)
        d_model, d_ff = (128, 512)
        B, S = (4, 512)
        x = jax.random.normal(k1, (B, S, d_model), dtype=jnp.float32)
        w_up = jax.random.normal(k2, (d_ff, d_model), dtype=jnp.float32) * 0.02
        w_down = jax.random.normal(k3, (d_model, d_ff), dtype=jnp.float32) * 0.02
        return {'x': x, 'w_up': w_up, 'w_down': w_down}
    _L2_ffn_in = _L2_ffn_setup()

    def _L3_attn_setup():
        import jax, jax.numpy as jnp
        import numpy as np
        L, B, D = (512, 4, 128)
        key = jax.random.key(seed)
        k1, k2, k3, k4 = jax.random.split(key, 4)
        return {'x': jax.random.normal(k1, (L, B, D), dtype=jnp.float32), 'lmlg': jax.random.normal(k2, (D,), dtype=jnp.float32), 'theta': jax.random.normal(k3, (D,), dtype=jnp.float32), 'last_conv_init': jax.random.normal(k4, (D,), dtype=jnp.float32)}
    _L3_attn_in = _L3_attn_setup()

    def _L3_ffn_setup():
        import jax, jax.numpy as jnp
        import numpy as np
        B, N, D = (4, 512, 128)
        E, S, F = (16, 64, 256)
        DO = 128
        EPS = 1e-05

        def _layernorm(x, g, b):
            mu = jnp.mean(x, axis=-1, keepdims=True)
            var = jnp.mean(jnp.square(x - mu), axis=-1, keepdims=True)
            return (x - mu) * jax.lax.rsqrt(var + EPS) * g + b
        key = jax.random.key(seed)
        ks = jax.random.split(key, 8)
        d = {'x': jax.random.normal(ks[0], (B, N, D), dtype=jnp.float32), 'norm_g': jnp.ones((D,), jnp.float32), 'norm_b': jnp.zeros((D,), jnp.float32), 'slot_g': jnp.ones((D,), jnp.float32), 'slot_b': jnp.zeros((D,), jnp.float32), 'scale': jnp.ones((1,), jnp.float32), 'slot_embeds': jax.random.normal(ks[1], (E, S, D), jnp.float32) / np.sqrt(D), 'Wg': jax.random.normal(ks[2], (E, D, F), jnp.float32) * np.sqrt(2.0 / (D + F)), 'bg': jnp.zeros((E, F), jnp.float32), 'Wu': jax.random.normal(ks[3], (E, D, F), jnp.float32) * np.sqrt(2.0 / (D + F)), 'bu': jnp.zeros((E, F), jnp.float32), 'Wd': jax.random.normal(ks[4], (E, F, DO), jnp.float32) * np.sqrt(2.0 / (F + DO)), 'bd': jnp.zeros((E, DO), jnp.float32)}
        return d
    _L3_ffn_in = _L3_ffn_setup()
    _d = {'L0_attn_x': _L0_attn_in['x'], 'L0_attn_Wq': _L0_attn_in['Wq'], 'L0_attn_Wk': _L0_attn_in['Wk'], 'L0_attn_Wv': _L0_attn_in['Wv'], 'L0_attn_Wf': _L0_attn_in['Wf'], 'L0_attn_bf': _L0_attn_in['bf'], 'L0_attn_Wg': _L0_attn_in['Wg'], 'L0_attn_Wout': _L0_attn_in['Wout'], 'L0_attn_gamma': _L0_attn_in['gamma'], 'L0_attn_beta': _L0_attn_in['beta'], 'L0_ffn_W1': _L0_ffn_in['W1'], 'L0_ffn_b1': _L0_ffn_in['b1'], 'L0_ffn_W2': _L0_ffn_in['W2'], 'L0_ffn_b2': _L0_ffn_in['b2'], 'L1_attn_W_attn': _L1_attn_in['W_attn'], 'L1_attn_b_attn': _L1_attn_in['b_attn'], 'L1_attn_W_k2': _L1_attn_in['W_k2'], 'L1_attn_b_k2': _L1_attn_in['b_k2'], 'L1_attn_W_proj': _L1_attn_in['W_proj'], 'L1_attn_b_proj': _L1_attn_in['b_proj'], 'L1_ffn_Wr': _L1_ffn_in['Wr'], 'L1_ffn_br': _L1_ffn_in['br'], 'L1_ffn_W1': _L1_ffn_in['W1'], 'L1_ffn_b1': _L1_ffn_in['b1'], 'L1_ffn_W2': _L1_ffn_in['W2'], 'L1_ffn_b2': _L1_ffn_in['b2'], 'L2_attn_ln_gamma': _L2_attn_in['ln_gamma'], 'L2_attn_ln_beta': _L2_attn_in['ln_beta'], 'L2_attn_Wq': _L2_attn_in['Wq'], 'L2_attn_Wk': _L2_attn_in['Wk'], 'L2_attn_Wv': _L2_attn_in['Wv'], 'L2_attn_Wo': _L2_attn_in['Wo'], 'L2_ffn_w_up': _L2_ffn_in['w_up'], 'L2_ffn_w_down': _L2_ffn_in['w_down'], 'L3_attn_lmlg': _L3_attn_in['lmlg'], 'L3_attn_theta': _L3_attn_in['theta'], 'L3_attn_last_conv_init': _L3_attn_in['last_conv_init'], 'L3_ffn_norm_g': _L3_ffn_in['norm_g'], 'L3_ffn_norm_b': _L3_ffn_in['norm_b'], 'L3_ffn_slot_g': _L3_ffn_in['slot_g'], 'L3_ffn_slot_b': _L3_ffn_in['slot_b'], 'L3_ffn_scale': _L3_ffn_in['scale'], 'L3_ffn_slot_embeds': _L3_ffn_in['slot_embeds'], 'L3_ffn_Wg': _L3_ffn_in['Wg'], 'L3_ffn_bg': _L3_ffn_in['bg'], 'L3_ffn_Wu': _L3_ffn_in['Wu'], 'L3_ffn_bu': _L3_ffn_in['bu'], 'L3_ffn_Wd': _L3_ffn_in['Wd'], 'L3_ffn_bd': _L3_ffn_in['bd']}
    _x0 = _d['L0_attn_x']
    _d['L0_attn_x'] = jax.random.normal(jax.random.fold_in(jax.random.key(seed), 1), (2, 1024, 128), dtype=_x0.dtype)
    del _x0
    return _d

def reference(L0_attn_x, L0_attn_Wq, L0_attn_Wk, L0_attn_Wv, L0_attn_Wf, L0_attn_bf, L0_attn_Wg, L0_attn_Wout, L0_attn_gamma, L0_attn_beta, L0_ffn_W1, L0_ffn_b1, L0_ffn_W2, L0_ffn_b2, L1_attn_W_attn, L1_attn_b_attn, L1_attn_W_k2, L1_attn_b_k2, L1_attn_W_proj, L1_attn_b_proj, L1_ffn_Wr, L1_ffn_br, L1_ffn_W1, L1_ffn_b1, L1_ffn_W2, L1_ffn_b2, L2_attn_ln_gamma, L2_attn_ln_beta, L2_attn_Wq, L2_attn_Wk, L2_attn_Wv, L2_attn_Wo, L2_ffn_w_up, L2_ffn_w_down, L3_attn_lmlg, L3_attn_theta, L3_attn_last_conv_init, L3_ffn_norm_g, L3_ffn_norm_b, L3_ffn_slot_g, L3_ffn_slot_b, L3_ffn_scale, L3_ffn_slot_embeds, L3_ffn_Wg, L3_ffn_bg, L3_ffn_Wu, L3_ffn_bu, L3_ffn_Wd, L3_ffn_bd):

    def _L0_attn_ref(x, Wq, Wk, Wv, Wf, bf, Wg, Wout, gamma, beta):
        import jax, jax.numpy as jnp
        import numpy as np
        B, S, D, H = (4, 256, 128, 16)
        HD = D // H
        LB = 0.0
        EPS = 1e-05
        b, s, d = x.shape
        q = (x @ Wq).reshape(b, s, H, HD)
        k = (x @ Wk).reshape(b, s, H, HD)
        v = (x @ Wv).reshape(b, s, H, HD)
        fg = jax.nn.sigmoid(x @ Wf + bf).reshape(b, s, H, HD)
        fg = LB + (1.0 - LB) * fg
        qs, ks_, vs, gs = (jnp.moveaxis(t, 1, 0) for t in (q, k, v, fg))

        def step(state, inp):
            qt, kt, vt, gt = inp
            state = state * gt[..., None] + vt[..., None] * kt[..., None, :]
            out_t = jnp.einsum('bhij,bhj->bhi', state, qt)
            return (state, out_t)
        state0 = jnp.zeros((b, H, HD, HD), x.dtype)
        _, outs = jax.lax.scan(step, state0, (qs, ks_, vs, gs))
        out = jnp.moveaxis(outs, 0, 1).reshape(b, s, d)
        mu = out.mean(-1, keepdims=True)
        var = out.var(-1, keepdims=True)
        out = (out - mu) * jax.lax.rsqrt(var + EPS) * gamma + beta
        out = out * jax.nn.silu(x @ Wg)
        return out @ Wout

    def _L0_ffn_ref(x, W1, b1, W2, b2):
        import jax, jax.numpy as jnp
        import numpy as np
        EMB = 128
        FF = 4 * EMB

        def _ternary(w):
            scale = jnp.maximum(jnp.mean(jnp.abs(w)), 1e-08)
            w_t = jnp.clip(jnp.round(w / scale), -1.0, 1.0)
            return w + jax.lax.stop_gradient(w_t - w)
        h = jnp.einsum('bsd,fd->bsf', x, _ternary(W1)) + b1
        h = jax.nn.gelu(h, approximate=False)
        out = jnp.einsum('bsf,df->bsd', h, _ternary(W2)) + b2
        return out

    def _L1_attn_ref(x, W_attn, b_attn, W_k2, b_k2, W_proj, b_proj):
        import jax, jax.numpy as jnp
        import numpy as np
        import math
        N_HEAD = 16

        def _causal_attn(q, k, v):
            d_k = q.shape[-1]
            s = jnp.einsum('bhqd,bhkd->bhqk', q, k) / math.sqrt(d_k)
            L, S = (q.shape[-2], k.shape[-2])
            mask = jnp.tril(jnp.ones((L, S), dtype=bool))
            s = jnp.where(mask, s, -jnp.inf)
            a = jax.nn.softmax(s, axis=-1)
            return jnp.einsum('bhqk,bhkd->bhqd', a, v)
        B, T, C = x.shape
        H = N_HEAD
        d = C // H
        qk = x @ W_attn + b_attn
        q, k = (qk[..., :C], qk[..., C:])
        q = q.reshape(B, T, H, d).transpose(0, 2, 1, 3)
        k = k.reshape(B, T, H, d).transpose(0, 2, 1, 3)
        v = x.reshape(B, T, H, d).transpose(0, 2, 1, 3)
        y = _causal_attn(q, k, v)
        e = v[:, :, 1:, :] - y[:, :, :-1, :]
        k2 = (x[:, :-1] @ W_k2 + b_k2).reshape(B, T - 1, H, d).transpose(0, 2, 1, 3)
        q2 = q[:, :, 1:, :]
        y2 = _causal_attn(q2, k2, e)
        y2 = jnp.concatenate([jnp.zeros_like(y2[:, :, :1, :]), y2], axis=2)

        def proj(t):
            return t.transpose(0, 2, 1, 3).reshape(B, T, C) @ W_proj + b_proj
        return proj(y) + proj(y2)

    def _L1_ffn_ref(x, Wr, br, W1, b1, W2, b2):
        import jax, jax.numpy as jnp
        import numpy as np
        D_MODEL, D_FF, N_EXP = (128, 512, 8)
        B, S, D = x.shape
        xf = x.reshape(-1, D)
        logits = xf @ Wr.T + br
        expert_idx = jnp.argmax(logits, axis=-1)
        h = jax.nn.relu(jnp.einsum('td,efd->etf', xf, W1) + b1[:, None, :])
        y = jnp.einsum('etf,edf->etd', h, W2) + b2[:, None, :]
        out = y[expert_idx, jnp.arange(xf.shape[0])]
        return out.reshape(B, S, D)

    def _L2_attn_ref(x, ln_gamma, ln_beta, Wq, Wk, Wv, Wo):
        import jax, jax.numpy as jnp
        import numpy as np
        DIM = 128
        DIM_HEAD = 64
        N_HEADS = 16
        INNER = DIM_HEAD * N_HEADS
        LN_EPS = 1e-05

        def layer_norm(x, gamma, beta):
            mu = jnp.mean(x, axis=-1, keepdims=True)
            var = jnp.var(x, axis=-1, keepdims=True)
            return (x - mu) * jax.lax.rsqrt(var + LN_EPS) * gamma + beta

        def alibi_bias(seq, n_heads):
            n_sequence = jnp.arange(n_heads, 0, -1).astype(jnp.float32)
            head_scalars = 2.0 ** (-8.0 / n_sequence)
            idx = jnp.arange(seq)
            dist = -jnp.abs(idx[:, None] - idx[None, :]).astype(jnp.float32)
            return head_scalars[:, None, None] * dist
        B, S, _ = x.shape
        xn = layer_norm(x, ln_gamma, ln_beta)

        def heads(t):
            return t.reshape(B, S, N_HEADS, DIM_HEAD).transpose(0, 2, 1, 3)
        q = heads(xn @ Wq)
        k = heads(xn @ Wk)
        v = heads(xn @ Wv)
        att = jnp.einsum('bhid,bhjd->bhij', q, k) / DIM_HEAD ** 0.5
        att = att + alibi_bias(S, N_HEADS)[None]
        p = jax.nn.softmax(att, axis=-1)
        out = jnp.einsum('bhij,bhjd->bhid', p, v)
        out = out.transpose(0, 2, 1, 3).reshape(B, S, INNER)
        return out @ Wo

    def _L2_ffn_ref(x, w_up, w_down):
        import jax, jax.numpy as jnp
        import numpy as np
        EPS = 1e-08

        def _ternary_linear(x, w):
            alpha = jnp.mean(jnp.abs(w))
            w_t = jnp.sign(w) * (jnp.abs(w) > 0.5 * alpha).astype(w.dtype)
            w_q = w + jax.lax.stop_gradient(w_t - w)
            d = x.shape[-1]
            rms = jnp.sqrt(jnp.sum(x * x, axis=-1, keepdims=True)) / jnp.sqrt(jnp.asarray(d, x.dtype))
            x_norm = x / (rms + EPS)
            return jnp.einsum('bsd,fd->bsf', x_norm, w_q)
        h = jax.nn.gelu(_ternary_linear(x, w_up), approximate=False)
        return _ternary_linear(h, w_down)

    def _L3_attn_ref(x, lmlg, theta, last_conv_init):
        import jax, jax.numpy as jnp
        import numpy as np
        L, B, D = (512, 4, 128)
        seq_len, batch, dim = x.shape
        gamma = jnp.exp(-jnp.exp(lmlg))
        c = gamma * jnp.exp(1j * theta)
        n = jnp.arange(seq_len)[:, None]
        filt = c[None, :] ** n
        filt_fft = jnp.fft.fft(filt, n=2 * seq_len, axis=0)
        x_fft = jnp.fft.fft(x, n=2 * seq_len, axis=0)
        conv_filter_x = jnp.fft.ifft(filt_fft[:, None, :] * x_fft, axis=0)[:seq_len]
        last_conv = jax.lax.stop_gradient(jnp.broadcast_to(last_conv_init.astype(conv_filter_x.dtype), (batch, dim)))
        conv_with_past = conv_filter_x + last_conv[None, :, :] * filt[:, None, :] * c[None, None, :]
        return conv_with_past.real * x

    def _L3_ffn_ref(x, norm_g, norm_b, slot_g, slot_b, scale, slot_embeds, Wg, bg, Wu, bu, Wd, bd):
        import jax, jax.numpy as jnp
        import numpy as np
        B, N, D = (4, 512, 128)
        E, S, F = (16, 64, 256)
        DO = 128
        EPS = 1e-05

        def _layernorm(x, g, b):
            mu = jnp.mean(x, axis=-1, keepdims=True)
            var = jnp.mean(jnp.square(x - mu), axis=-1, keepdims=True)
            return (x - mu) * jax.lax.rsqrt(var + EPS) * g + b
        x = _layernorm(x, norm_g, norm_b)
        se = _layernorm(slot_embeds, slot_g, slot_b) * scale
        logits = jnp.einsum('bnd,esd->bnes', x, se)
        dispatch = jax.nn.softmax(logits, axis=1)
        combine = jax.nn.softmax(logits.reshape(x.shape[0], x.shape[1], -1), axis=-1)
        slots = jnp.einsum('bnd,bnes->besd', x, dispatch)
        gate = jax.nn.gelu(jnp.einsum('besd,edf->besf', slots, Wg) + bg[None, :, None, :], approximate=False)
        up = jnp.einsum('besd,edf->besf', slots, Wu) + bu[None, :, None, :]
        eout = jnp.einsum('besf,efo->beso', gate * up, Wd) + bd[None, :, None, :]
        eout = eout.reshape(eout.shape[0], -1, eout.shape[-1])
        return jnp.einsum('bns,bso->bno', combine, eout)
    x = L0_attn_x
    x = x + 0.5 * _L0_ffn_ref(_layernorm(x, axis=-1), L0_ffn_W1, L0_ffn_b1, L0_ffn_W2, L0_ffn_b2)
    x = x + _L0_attn_ref(_layernorm(x, axis=-1), L0_attn_Wq, L0_attn_Wk, L0_attn_Wv, L0_attn_Wf, L0_attn_bf, L0_attn_Wg, L0_attn_Wout, L0_attn_gamma, L0_attn_beta)
    x = x + 0.5 * _L0_ffn_ref(_layernorm(x, axis=-1), L0_ffn_W1, L0_ffn_b1, L0_ffn_W2, L0_ffn_b2)
    x = x + 0.5 * _L1_ffn_ref(_layernorm(x, axis=-1), L1_ffn_Wr, L1_ffn_br, L1_ffn_W1, L1_ffn_b1, L1_ffn_W2, L1_ffn_b2)
    x = x + _L1_attn_ref(_layernorm(x, axis=-1), L1_attn_W_attn, L1_attn_b_attn, L1_attn_W_k2, L1_attn_b_k2, L1_attn_W_proj, L1_attn_b_proj)
    x = x + 0.5 * _L1_ffn_ref(_layernorm(x, axis=-1), L1_ffn_Wr, L1_ffn_br, L1_ffn_W1, L1_ffn_b1, L1_ffn_W2, L1_ffn_b2)
    x = x + 0.5 * _L2_ffn_ref(_layernorm(x, axis=-1), L2_ffn_w_up, L2_ffn_w_down)
    x = x + _L2_attn_ref(_layernorm(x, axis=-1), L2_attn_ln_gamma, L2_attn_ln_beta, L2_attn_Wq, L2_attn_Wk, L2_attn_Wv, L2_attn_Wo)
    x = x + 0.5 * _L2_ffn_ref(_layernorm(x, axis=-1), L2_ffn_w_up, L2_ffn_w_down)
    x = x + 0.5 * _L3_ffn_ref(_layernorm(x, axis=-1), L3_ffn_norm_g, L3_ffn_norm_b, L3_ffn_slot_g, L3_ffn_slot_b, L3_ffn_scale, L3_ffn_slot_embeds, L3_ffn_Wg, L3_ffn_bg, L3_ffn_Wu, L3_ffn_bu, L3_ffn_Wd, L3_ffn_bd)
    x = x + _L3_attn_ref(_layernorm(x, axis=-1), L3_attn_lmlg, L3_attn_theta, L3_attn_last_conv_init)
    x = x + 0.5 * _L3_ffn_ref(_layernorm(x, axis=-1), L3_ffn_norm_g, L3_ffn_norm_b, L3_ffn_slot_g, L3_ffn_slot_b, L3_ffn_scale, L3_ffn_slot_embeds, L3_ffn_Wg, L3_ffn_bg, L3_ffn_Wu, L3_ffn_bu, L3_ffn_Wd, L3_ffn_bd)
    return x

_drawn_inputs = setup_inputs


def setup_inputs(seed=0):
    import zlib

    import numpy as np

    out = dict(_drawn_inputs(seed))
    spreads = {'L0_attn_bf': (0.0, 0.8),
     'L0_attn_gamma': (1.0, 0.6),
     'L0_attn_beta': (0.0, 0.8),
     'L1_attn_b_attn': (0.0, 0.8),
     'L1_attn_b_k2': (0.0, 0.8),
     'L1_attn_b_proj': (0.0, 0.8),
     'L2_attn_ln_gamma': (1.0, 0.6),
     'L2_attn_ln_beta': (0.0, 0.8),
     'L3_ffn_norm_g': (1.0, 0.6),
     'L3_ffn_norm_b': (0.0, 0.8),
     'L3_ffn_slot_g': (1.0, 0.6),
     'L3_ffn_slot_b': (0.0, 0.8),
     'L3_ffn_bg': (0.0, 0.8),
     'L3_ffn_bu': (0.0, 0.8),
     'L3_ffn_bd': (0.0, 0.8)}
    factors = {'L0_attn_Wq': 8.0,
     'L0_attn_Wk': 8.0,
     'L0_attn_Wv': 8.0,
     'L0_attn_Wf': 8.0,
     'L0_attn_Wg': 8.0,
     'L0_attn_Wout': 8.0,
     'L0_ffn_b1': 8.0,
     'L0_ffn_b2': 8.0,
     'L1_attn_W_attn': 8.0,
     'L1_attn_W_k2': 8.0,
     'L1_attn_W_proj': 8.0,
     'L1_ffn_Wr': 8.0,
     'L1_ffn_br': 8.0,
     'L1_ffn_W1': 8.0,
     'L1_ffn_b1': 8.0,
     'L1_ffn_W2': 8.0,
     'L1_ffn_b2': 8.0,
     'L2_attn_Wq': 8.0,
     'L2_attn_Wk': 8.0,
     'L2_attn_Wv': 8.0,
     'L2_attn_Wo': 8.0,
     'L3_attn_lmlg': 8.0,
     'L3_attn_theta': 8.0,
     'L3_attn_last_conv_init': 8.0,
     'L3_ffn_slot_embeds': 8.0,
     'L3_ffn_Wg': 8.0,
     'L3_ffn_Wu': 8.0,
     'L3_ffn_Wd': 8.0}
    for name, (base, spread) in spreads.items():
        noise = np.random.default_rng([zlib.crc32(name.encode()), seed]).standard_normal(out[name].shape)
        drawn = base * np.exp(spread * noise) if base else spread * noise
        out[name] = jnp.asarray(drawn.astype(out[name].dtype))
    for name, factor in factors.items():
        out[name] = (out[name] * factor).astype(out[name].dtype)
    return out
```

```python
from contextlib import ExitStack

import numpy as np

import concourse.bass as bass
from concourse import mybir

F32 = mybir.dt.float32
F32R = mybir.dt.float32r
BF16 = mybir.dt.bfloat16
ALU = mybir.AluOpType
ACT = mybir.ActivationFunctionType
AX = mybir.AxisListType.X

P = 128
D = 128
BATCH, SEQ = 2, 1024
TOK = BATCH * SEQ
NT = TOK // P
TPB = SEQ // P
CH = 512
NCH = TOK // CH
TPC = CH // P
DFF = 4 * D
MFF = DFF // P
LN_EPS = 1e-5
RMS_EPS = 1e-8
BIG = 1.0e30
ds = bass.ds


class Stage:

    def __init__(self, nc, name):
        self.nc, self.name, self.stack, self.sems = nc, name, ExitStack(), []

    def __enter__(self):
        return self

    def __exit__(self, *err):
        self.stack.close()
        if self.sems:
            self.nc.clear_and_free_semaphores(self.sems)
            self.nc.all_engine_barrier()

    def sb(self, name, shape, dt=F32):
        return self.stack.enter_context(self.nc.sbuf_tensor(f"{self.name}_{name}", shape, dt))

    def ps(self, name, shape, dt=F32):
        return self.stack.enter_context(self.nc.psum_tensor(f"{self.name}_{name}", shape, dt))

    def sem(self, name):
        self.sems.append(self.nc.alloc_semaphore(name=f"{self.name}_{name}"))
        return self.sems[-1]


class Chain:

    def __init__(self, eng, sem, first=0):
        self.eng, self.sem, self.first, self.n = eng, sem, first, 0

    def step(self, ins):
        ins.then_inc(self.sem, 1)
        self.n += 1
        self.eng.wait_ge(self.sem, self.first + self.n)


def per_token(col, width):
    n = col.shape[1]
    return col.unsqueeze(2).to_broadcast([P, n, width])


def per_feature(row, tiles):
    return row.unsqueeze(1).to_broadcast([P, tiles, row.shape[1]])


def constants(nc, C):
    with Stage(nc, "const") as S:
        made = S.sem("made")
        with nc.Block() as block:

            @block.gpsimd
            def _(pool):
                chain = Chain(pool, made)
                chain.step(pool.memset(C.ident[:, :], 0.0))
                chain.step(pool.affine_select(out=C.ident[:, :], in_=C.ident[:, :], compare_op=ALU.not_equal,
                                              fill=1.0, base=0, pattern=[[-1, P]], channel_multiplier=1))
                pool.memset(C.ones[:, :], 1.0)
                pool.memset(C.zeros[:, :], 0.0)
                pool.memset(C.rms_eps[:, :], RMS_EPS)
                pool.memset(C.neg_half[:, :], -0.5)
                pool.memset(C.half[:, :], 0.5)
                chain.step(pool.memset(C.neg_one[:, :], -1.0))


def normalise(nc, C, name, src, dst, dstT=None, kind="layer", gamma=None, beta=None, tiles=NT):
    G = 4
    TG = tiles // G
    with Stage(nc, name) as S:
        sums = S.sb("sums", [P, tiles])
        mean = S.sb("mean", [P, tiles])
        cent = S.sb("cent", [P, tiles, D])
        square = S.sb("square", [P, tiles, D])
        sumsq = S.sb("sumsq", [P, tiles])
        var = S.sb("var", [P, tiles])
        root = S.sb("root", [P, tiles])
        rstd = S.sb("rstd", [P, tiles])
        turned = S.ps("turned", [P, G, CH])
        own = S.sem("own")
        centred = S.sem("centred")
        squared = S.sem("squared")
        summed = S.sem("summed")
        own_pool = S.sem("own_pool")
        scaled = S.sem("scaled")
        normed = S.sem("normed")
        turned_ok = S.sem("turned_ok")
        stored = S.sem("stored")
        with nc.Block() as block:

            @block.vector
            def _(dve):
                chain = Chain(dve, own)
                for g in range(G):
                    t = slice(g * TG, (g + 1) * TG)
                    if kind == "layer":
                        chain.step(dve.tensor_reduce(sums[:, t], src[:, t, :], AX, ALU.add))
                        chain.step(dve.tensor_scalar(mean[:, t], sums[:, t], 1.0 / D, None, ALU.mult))
                        dve.tensor_tensor(cent[:, t, :], src[:, t, :], per_token(mean[:, t], D),
                                          ALU.subtract).then_inc(centred, 1)
                    if g >= 1:
                        dve.wait_ge(squared, g)
                        p = slice((g - 1) * TG, g * TG)
                        dve.tensor_reduce(sumsq[:, p], square[:, p, :], AX, ALU.add).then_inc(summed, 1)
                dve.wait_ge(squared, G)
                p = slice((G - 1) * TG, G * TG)
                dve.tensor_reduce(sumsq[:, p], square[:, p, :], AX, ALU.add).then_inc(summed, 1)
                for g in range(G):
                    t = slice(g * TG, (g + 1) * TG)
                    dve.wait_ge(scaled, g + 1)
                    if kind == "layer":
                        dve.wait_ge(centred, g + 1)
                    x = cent if kind == "layer" else src
                    last = dve.tensor_tensor(dst[:, t, :], x[:, t, :], per_token(rstd[:, t], D), ALU.mult)
                    if gamma is not None:
                        chain.step(last)
                        chain.step(dve.tensor_tensor(dst[:, t, :], dst[:, t, :], per_feature(gamma, TG), ALU.mult))
                        last = dve.tensor_tensor(dst[:, t, :], dst[:, t, :], per_feature(beta, TG), ALU.add)
                    last.then_inc(normed, 1)

            @block.scalar
            def _(act):
                for g in range(G):
                    t = slice(g * TG, (g + 1) * TG)
                    if kind == "layer":
                        act.wait_ge(centred, g + 1)
                    x = cent if kind == "layer" else src
                    act.activation(square[:, t, :], x[:, t, :], ACT.Square).then_inc(squared, 1)
                if dstT is not None:
                    for g in range(G):
                        act.wait_ge(turned_ok, g + 1)
                        act.copy(dstT[:, g * TG * P:(g + 1) * TG * P], turned[:, g, 0:TG * P]).then_inc(stored, 1)

            @block.gpsimd
            def _(pool):
                chain = Chain(pool, own_pool)
                for g in range(G):
                    t = slice(g * TG, (g + 1) * TG)
                    pool.wait_ge(summed, g + 1)
                    if kind == "layer":
                        chain.step(pool.tensor_scalar(var[:, t], sumsq[:, t], 1.0 / D, LN_EPS, ALU.mult, ALU.add))
                        pool.tensor_tensor(rstd[:, t], var[:, t], C.neg_half[:, 0:TG], ALU.pow).then_inc(scaled, 1)
                    else:
                        chain.step(pool.tensor_scalar(var[:, t], sumsq[:, t], 1.0 / D, None, ALU.mult))
                        chain.step(pool.tensor_tensor(root[:, t], var[:, t], C.half[:, 0:TG], ALU.pow))
                        chain.step(pool.tensor_scalar(var[:, t], root[:, t], RMS_EPS, None, ALU.add))
                        pool.tensor_tensor(rstd[:, t], var[:, t], C.neg_one[:, 0:TG], ALU.pow).then_inc(scaled, 1)

            if dstT is not None:
                @block.tensor
                def _(pe):
                    for g in range(G):
                        pe.wait_ge(normed, g + 1)
                        for k in range(TG):
                            mm = pe.transpose(turned[:, g, k * P:(k + 1) * P], dst[:, g * TG + k, :], C.ident[:, :])
                        mm.then_inc(turned_ok, 1)


def ternary_weights(nc, C, name, W1, W2, floor, up, down):
    with Stage(nc, name) as S:
        raw = S.sb("raw", [P, 2, DFF])
        sign = S.sb("sign", [P, 2, DFF])
        below = S.sb("below", [P, 2, DFF])
        rows = S.sb("rows", [P, 2])
        cut = S.sb("cut", [P, 2])
        neg_cut = S.sb("neg_cut", [P, 2])
        total = S.ps("total", [P, CH])
        turned = S.ps("turned", [P, 2, DFF])
        loaded = S.sem("loaded")
        own = S.sem("own")
        summed = S.sem("summed")
        totalled = S.sem("totalled")
        turned_ok = S.sem("turned_ok")
        with nc.Block() as block:

            @block.sync
            def _(sp):
                sp.dma_start(raw[:, 0, :].rearrange("p (m d) -> p m d", m=MFF),
                             W1.rearrange("(m p) d -> p m d", p=P)).then_inc(loaded, 16)
                sp.dma_start(raw[:, 1, :], W2).then_inc(loaded, 16)

            @block.vector
            def _(dve):
                chain = Chain(dve, own)
                dve.wait_ge(loaded, 32)
                for w in range(2):
                    dve.tensor_reduce(rows[:, w:w + 1], raw[:, w, :], AX, ALU.add,
                                      apply_absolute_value=True).then_inc(summed, 1)
                dve.wait_ge(totalled, 1)
                chain.step(dve.tensor_scalar(cut[:, :], total[:, 0:2], 1.0 / (D * DFF), floor, ALU.mult, ALU.max))
                chain.step(dve.tensor_scalar(cut[:, :], cut[:, :], 0.5, None, ALU.mult))
                chain.step(dve.tensor_scalar(neg_cut[:, :], cut[:, :], -1.0, None, ALU.mult))
                for w in range(2):
                    dve.tensor_scalar(below[:, w, :], raw[:, w, :], neg_cut[:, w:w + 1], None, ALU.is_lt)
                    chain.step(dve.tensor_scalar(sign[:, w, :], raw[:, w, :], cut[:, w:w + 1], None, ALU.is_gt))
                    chain.step(dve.tensor_tensor(sign[:, w, :], sign[:, w, :], below[:, w, :], ALU.subtract))
                dve.wait_ge(turned_ok, 1)
                dve.tensor_copy(up[:, :], turned[:, 0, :])
                dve.tensor_copy(down[:, :, :], turned[:, 1, :].rearrange("p (m d) -> p m d", m=MFF))

            @block.tensor
            def _(pe):
                pe.wait_ge(summed, 2)
                pe.matmul(total[:, 0:2], C.ones[:, :], rows[:, :], start=True, stop=True).then_inc(totalled, 1)
                pe.wait_ge(own, 7)
                for w in range(2):
                    for m in range(MFF):
                        mm = pe.transpose(turned[:, w, m * P:(m + 1) * P], sign[:, w, m * P:(m + 1) * P], C.ident[:, :])
                mm.then_inc(turned_ok, 1)


def ffn(nc, C, name, X, xnT, up, down, b1=None, b2=None, rms=False):
    with Stage(nc, name) as S:
        hidden = [S.sb(f"hidden{k}", [P, MFF, CH]) for k in range(2)]
        square = [S.sb(f"square{k}", [P, MFF, CH]) for k in range(2)] if rms else None
        hidden_out = S.sb("hidden_out", [P, 2, TPC, D]) if rms else None
        mean_sq = S.sb("mean_sq", [P, 2, TPC])
        root = S.sb("root", [P, 2, TPC])
        scale = S.sb("scale", [P, 2, TPC])
        p_up = S.ps("p_up", [P, MFF, CH])
        p_down = S.ps("p_down", [P, 2, CH])
        p_sq = S.ps("p_sq", [P, 2, CH]) if rms else None
        up_ready = S.sem("up_ready")
        gelu_done = S.sem("gelu_done")
        square_done = S.sem("square_done")
        down_ready = S.sem("down_ready")
        sums_ready = S.sem("sums_ready")
        scale_ready = S.sem("scale_ready")
        own_pool = S.sem("own_pool")
        copied = S.sem("copied")
        added = S.sem("added")
        with nc.Block() as block:

            @block.tensor
            def _(pe):
                with pe.Fori(0, NCH // 2) as i:
                    for k in range(2):
                        for m in range(MFF):
                            if k:
                                pe.wait_ge(gelu_done, i * 2 * MFF + m + 1)
                            else:
                                pe.wait_ge(gelu_done, i * 2 * MFF)
                            pe.matmul(p_up[:, m, :], up[:, m * P:(m + 1) * P], xnT[:, ds((i * 2 + k) * CH, CH)],
                                      start=True, stop=True).then_inc(up_ready, 1)
                    for k in range(2):
                        pe.wait_ge(gelu_done, i * 2 * MFF + (k + 1) * MFF)
                        pe.wait_ge(added, i * 2)
                        for t in range(TPC):
                            if b2 is not None:
                                pe.matmul(p_down[:, k, t * D:(t + 1) * D], C.ones[0:1, :], b2, start=True, stop=False)
                            for m in range(MFF):
                                mm = pe.matmul(p_down[:, k, t * D:(t + 1) * D], hidden[k][:, m, t * P:(t + 1) * P],
                                               down[:, m, :], start=(m == 0 and b2 is None), stop=(m == MFF - 1))
                        mm.then_inc(down_ready, 1)
                        if rms:
                            pe.wait_ge(square_done, i * 2 + k + 1)
                            for t in range(TPC):
                                for m in range(MFF):
                                    mm = pe.matmul(p_sq[:, k, t:t + 1], square[k][:, m, t * P:(t + 1) * P],
                                                   C.ones[:, 0:1], start=(m == 0), stop=(m == MFF - 1))
                            mm.then_inc(sums_ready, 1)

            @block.scalar
            def _(act):
                with act.Fori(0, NCH // 2) as i:
                    for k in range(2):
                        act.wait_ge(down_ready, i * 2)
                        for m in range(MFF):
                            act.wait_ge(up_ready, i * 2 * MFF + k * MFF + m + 1)
                            bias = b1[:, m:m + 1] if b1 is not None else 0.0
                            act.activation(hidden[k][:, m, :], p_up[:, m, :], ACT.Gelu, bias=bias).then_inc(gelu_done, 1)

                        if rms:
                            act.wait_ge(gelu_done, i * 2 * MFF + (k + 1) * MFF)
                            act.wait_ge(sums_ready, i * 2)
                            act.activation(square[k][:, :, :], hidden[k][:, :, :], ACT.Square).then_inc(square_done, 1)

            if rms:
                @block.gpsimd
                def _(pool):
                    with pool.Fori(0, NCH // 2) as i:
                        for k in range(2):
                            chain = Chain(pool, own_pool, i * 4 + k * 2)
                            pool.wait_ge(copied, i * 2 + k + 1)
                            chain.step(pool.tensor_tensor(root[:, k, :], mean_sq[:, k, :], C.half[:, 0:TPC], ALU.pow))
                            chain.step(pool.tensor_tensor(root[:, k, :], root[:, k, :], C.rms_eps[:, 0:TPC], ALU.add))
                            pool.wait_ge(added, i * 2)
                            pool.tensor_tensor(scale[:, k, :], root[:, k, :], C.neg_one[:, 0:TPC],
                                               ALU.pow).then_inc(scale_ready, 1)

            @block.vector
            def _(dve):
                with dve.Fori(0, NCH // 2) as i:
                    for k in range(2):
                        tiles = ds((i * 2 + k) * TPC, TPC)
                        if rms:
                            dve.wait_ge(sums_ready, i * 2 + k + 1)
                            dve.tensor_scalar(mean_sq[:, k, :], p_sq[:, k, 0:TPC], 1.0 / DFF, None,
                                              ALU.mult).then_inc(copied, 1)
                    for k in range(2):
                        dve.wait_ge(down_ready, i * 2 + k + 1)
                        if not rms:
                            tiles = ds((i * 2 + k) * TPC, TPC)
                            dve.scalar_tensor_tensor(
                                out=X[:, tiles, :], in0=p_down[:, k, :].rearrange("p (t d) -> p t d", d=D), scalar=0.5,
                                in1=X[:, tiles, :], op0=ALU.mult, op1=ALU.add).then_inc(added, 1)
                        else:
                            dve.wait_ge(scale_ready, i * 2 + k + 1)
                            for t in range(TPC):
                                row = ds((i * 2 + k) * TPC + t, 1)
                                last = dve.tensor_scalar(hidden_out[:, k, t, :], p_down[:, k, t * D:(t + 1) * D],
                                                         scale[:, k, t:t + 1], 0.5, ALU.mult, ALU.mult)
                            last.then_inc(added, 1)
                            dve.wait_ge(added, i * 2 + k + 1)
                            tiles = ds((i * 2 + k) * TPC, TPC)
                            dve.tensor_tensor(X[:, tiles, :], X[:, tiles, :], hidden_out[:, k, :, :], ALU.add)



H, HD = 16, 8


def gated_scan_mixer(nc, C, I, X, xn, xnT):
    with Stage(nc, "mix0") as M:
        mixed = M.sb("mixed", [P, NT, D])
        gamma = M.sb("gamma", [P, D])
        beta = M.sb("beta", [P, D])
        Wg = M.sb("Wg", [P, D])
        Wout = M.sb("Wout", [P, D])
        with Stage(nc, "scan") as S:
            W = {n: S.sb(n, [P, D]) for n in ("Wq", "Wk", "Wv", "Wf")}
            bf = S.sb("bf", [P, 1])
            load(nc, "mix0_load", [(W[n][:, :], I[f"L0_attn_{n}"]) for n in W] + [
                (Wg[:, :], I["L0_attn_Wg"]), (Wout[:, :], I["L0_attn_Wout"]), (bf[:, :], I["L0_attn_bf"].unsqueeze(1)),
                (gamma[:, :], I["L0_attn_gamma"].partition_broadcast(P)),
                (beta[:, :], I["L0_attn_beta"].partition_broadcast(P))])
            krep_w = S.sb("krep_w", [P, HD, D])
            qrep_w = S.sb("qrep_w", [P, HD, D])
            with nc.Block() as block:

                @block.vector
                def _(dve):
                    for j in range(HD):
                        for rep, w in ((krep_w, W["Wk"]), (qrep_w, W["Wq"])):
                            dve.tensor_copy(rep[:, j, :].rearrange("p (h i) -> p h i", i=HD),
                                            w[:, j:D:HD].unsqueeze(2).to_broadcast([P, H, HD]))

            scan_over_tokens(nc, C, S, W, bf, krep_w, qrep_w, xnT, mixed)
        normalise(nc, C, "mix0_norm", mixed, mixed, gamma=gamma[:, :], beta=beta[:, :])
        gate_and_project(nc, C, X, xnT, mixed, Wg, Wout)


def scan_over_tokens(nc, C, S, W, bf, krep_w, qrep_w, xnT, mixed):
    vT = S.sb("vT", [P, SEQ])
    gT = S.sb("gT", [P, SEQ])
    vk = S.sb("vk", [P, SEQ])
    state = S.sb("state", [P, SEQ])
    sq = [S.sb(f"sq{k}", [P, SEQ]) for k in range(2)]
    p_k = [S.ps(f"p_k{k}", [P, SEQ]) for k in range(2)]
    p_q = S.ps("p_q", [P, SEQ])
    p_out = S.ps("p_out", [P, SEQ])
    v_ready, f_ready = S.sem("v_ready"), S.sem("f_ready")
    v_stored, g_stored = S.sem("v_stored"), S.sem("g_stored")
    k_ready, q_ready = S.sem("k_ready"), S.sem("q_ready")
    vk_done = S.sem("vk_done")
    sq_done = S.sem("sq_done")
    summed = S.sem("summed")
    out_stored = S.sem("out_stored")
    own = S.sem("own")
    with nc.Block() as block:

        @block.tensor
        def _(pe):
            with pe.Fori(0, BATCH) as b:
                def product(dst, w):
                    for c in range(SEQ // CH):
                        mm = pe.matmul(dst[:, c * CH:(c + 1) * CH], w, xnT[:, ds(b * SEQ + c * CH, CH)],
                                       start=True, stop=True)
                    return mm

                def k_of(j):
                    if j == 0:
                        pe.wait_ge(v_stored, b + 1)
                    else:
                        pe.wait_ge(vk_done, b * HD + j - 1)
                    product(p_k[j % 2], krep_w[:, j, :]).then_inc(k_ready, 1)

                def q_of(j):
                    if j == 0:
                        pe.wait_ge(g_stored, b + 1)
                    else:
                        pe.wait_ge(sq_done, b * HD + j)
                    product(p_q, qrep_w[:, j, :]).then_inc(q_ready, 1)

                pe.wait_ge(sq_done, b * HD)
                product(p_k[0], W["Wv"][:, :]).then_inc(v_ready, 1)
                product(p_q, W["Wf"][:, :]).then_inc(f_ready, 1)
                k_of(0)
                q_of(0)
                for j in range(HD):
                    if j + 1 < HD:
                        k_of(j + 1)
                        q_of(j + 1)
                    if j == 0:
                        pe.wait_ge(out_stored, b)
                    pe.wait_ge(sq_done, b * HD + j + 1)
                    for t in range(TPB):
                        mm = pe.matmul(p_out[:, t * D:(t + 1) * D], sq[j % 2][:, t * P:(t + 1) * P], C.ident[:, :],
                                       start=(j == 0 and t % TPC == 0), stop=(j == HD - 1), skip_group_check=True)
                    mm.then_inc(summed, 1)

        @block.scalar
        def _(act):
            with act.Fori(0, BATCH) as b:
                act.wait_ge(vk_done, b * HD)
                act.wait_ge(v_ready, b + 1)
                act.copy(vT[:, :], p_k[0][:, :]).then_inc(v_stored, 1)
                act.wait_ge(f_ready, b + 1)
                act.activation(gT[:, :], p_q[:, :], ACT.Sigmoid, bias=bf[:, 0:1]).then_inc(g_stored, 1)
                act.wait_ge(summed, (b + 1) * HD)
                act.copy(mixed[:, ds(b * TPB, TPB), :], p_out[:, :].rearrange("p (t d) -> p t d", d=D)
                         ).then_inc(out_stored, 1)

        @block.vector
        def _(dve):
            with dve.Fori(0, BATCH) as b:
                chain = Chain(dve, own, b * HD * 2)
                dve.wait_ge(v_stored, b + 1)
                dve.wait_ge(g_stored, b + 1)
                for j in range(HD):
                    dve.wait_ge(k_ready, b * HD + j + 1)
                    dve.tensor_tensor(vk[:, :], vT[:, :], p_k[j % 2][:, :], ALU.mult).then_inc(vk_done, 1)
                    dve.wait_ge(vk_done, b * HD + j + 1)
                    dve.tensor_tensor_scan(state[:, :], gT[:, :], vk[:, :], 0.0, ALU.mult, ALU.add).then_inc(own, 1)
                    dve.wait_ge(own, b * HD + j + 1)
                    dve.wait_ge(q_ready, b * HD + j + 1)
                    if j >= 2:
                        dve.wait_ge(summed, b * HD + j - 1)
                    else:
                        dve.wait_ge(summed, b * HD)
                    dve.tensor_tensor(sq[j % 2][:, :], state[:, :], p_q[:, :], ALU.mult).then_inc(sq_done, 1)


def gate_and_project(nc, C, X, xnT, mixed, Wg, Wout):
    G = NT // TPC
    with Stage(nc, "gate") as S:
        gate = S.sb("gate", [P, NT, D])
        gated = S.sb("gated", [P, NT, D])
        gatedT = S.sb("gatedT", [P, TOK])
        p_gate = S.ps("p_gate", [P, 2, CH])
        p_turn = S.ps("p_turn", [P, 2, CH])
        p_proj = S.ps("p_proj", [P, 2, CH])
        gate_ready, gate_done = S.sem("gate_ready"), S.sem("gate_done")
        gated_done, turned, turned_stored = S.sem("gated_done"), S.sem("turned"), S.sem("turned_stored")
        projected, added = S.sem("projected"), S.sem("added")
        with nc.Block() as block:

            @block.tensor
            def _(pe):
                def gates(g):
                    if g >= 2:
                        pe.wait_ge(gate_done, g - 1)
                    for k in range(TPC):
                        t = g * TPC + k
                        mm = pe.matmul(p_gate[:, g % 2, k * D:(k + 1) * D], xnT[:, t * P:(t + 1) * P], Wg[:, :],
                                       start=True, stop=True)
                    mm.then_inc(gate_ready, 1)

                gates(0)
                for g in range(G):
                    if g + 1 < G:
                        gates(g + 1)
                    pe.wait_ge(gated_done, g + 1)
                    if g >= 2:
                        pe.wait_ge(turned_stored, g - 1)
                    for k in range(TPC):
                        mm = pe.transpose(p_turn[:, g % 2, k * P:(k + 1) * P], gated[:, g * TPC + k, :], C.ident[:, :])
                    mm.then_inc(turned, 1)
                    pe.wait_ge(turned_stored, g + 1)
                    if g >= 2:
                        pe.wait_ge(added, g - 1)
                    for k in range(TPC):
                        t = g * TPC + k
                        mm = pe.matmul(p_proj[:, g % 2, k * D:(k + 1) * D], gatedT[:, t * P:(t + 1) * P], Wout[:, :],
                                       start=True, stop=True)
                    mm.then_inc(projected, 1)

            @block.scalar
            def _(act):
                for g in range(G):
                    act.wait_ge(gate_ready, g + 1)
                    act.activation(gate[:, g * TPC:(g + 1) * TPC, :],
                                   p_gate[:, g % 2, :].rearrange("p (t d) -> p t d", d=D), ACT.Silu).then_inc(gate_done, 1)
                    act.wait_ge(turned, g + 1)
                    act.copy(gatedT[:, g * CH:(g + 1) * CH], p_turn[:, g % 2, :]).then_inc(turned_stored, 1)

            @block.vector
            def _(dve):
                for g in range(G):
                    t = slice(g * TPC, (g + 1) * TPC)
                    dve.wait_ge(gate_done, g + 1)
                    dve.tensor_tensor(gated[:, t, :], gate[:, t, :], mixed[:, t, :], ALU.mult).then_inc(gated_done, 1)
                    dve.wait_ge(projected, g + 1)
                    dve.tensor_tensor(X[:, t, :], X[:, t, :], p_proj[:, g % 2, :].rearrange("p (t d) -> p t d", d=D),
                                      ALU.add).then_inc(added, 1)


NEXP = 8


def moe_ffn(nc, C, I, name, X, xnT):
    with Stage(nc, name) as M:
        pick = M.sb("pick", [P, NT, NEXP])
        b1T = M.sb("b1T", [P, NEXP * MFF])
        route(nc, C, I, name, X, xnT, pick, b1T)
        experts(nc, C, I, name, X, xnT, pick, b1T)


def route(nc, C, I, name, X, xnT, pick, b1T):
    with Stage(nc, name + "_route") as S:
        WrT = S.sb("WrT", [P, NEXP])
        br = S.sb("br", [P, NEXP])
        b1 = S.sb("b1", [NEXP * MFF, P])
        b2 = S.sb("b2", [NEXP, D])
        rank = S.sb("rank", [P, NEXP])
        logits = S.sb("logits", [P, NT, NEXP])
        best = S.sb("best", [P, NT])
        tied = S.sb("tied", [P, NT, NEXP])
        first = S.sb("first", [P, NT])
        pickT = S.sb("pickT", [NEXP, TOK])
        p_logits = S.ps("p_logits", [P, CH])
        p_b1T = S.ps("p_b1T", [P, CH])
        p_pickT = S.ps("p_pickT", [P, TOK])
        loaded, ranked = S.sem("loaded"), S.sem("ranked")
        logits_ready, own, picked = S.sem("logits_ready"), S.sem("own"), S.sem("picked")
        turned, stored = S.sem("turned"), S.sem("stored")
        bias_ready, b1_ready, bias_added = S.sem("bias_ready"), S.sem("b1_ready"), S.sem("bias_added")
        with nc.Block() as block:

            @block.sync
            def _(sp):
                sp.dma_start(WrT[:, :], I["L1_ffn_Wr"].rearrange("e d -> d e"),
                             allow_slow_non_contiguous=True).then_inc(loaded, 16)
                sp.dma_start(br[:, :], I["L1_ffn_br"].partition_broadcast(P)).then_inc(loaded, 16)
                sp.dma_start(b1[:, :], I["L1_ffn_b1"].rearrange("e (m p) -> (e m) p", p=P)).then_inc(loaded, 16)
                sp.dma_start(b2[:, :], I["L1_ffn_b2"]).then_inc(loaded, 16)

            @block.gpsimd
            def _(pool):
                for e in range(NEXP):
                    pool.memset(rank[:, e:e + 1], float(NEXP - e)).then_inc(ranked, 1)

            @block.tensor
            def _(pe):
                pe.wait_ge(loaded, 64)
                for t in range(NT):
                    mm = pe.matmul(p_logits[:, t * NEXP:(t + 1) * NEXP], xnT[:, t * P:(t + 1) * P], WrT[:, :],
                                   start=True, stop=True)
                mm.then_inc(logits_ready, 1)
                pe.transpose(p_b1T[:, 0:NEXP * MFF], b1[:, :], C.ident[0:NEXP * MFF, 0:NEXP * MFF]).then_inc(b1_ready, 1)
                pe.wait_ge(picked, 1)
                for t in range(NT):
                    mm = pe.transpose(p_pickT[0:NEXP, t * P:(t + 1) * P], pick[:, t, :], C.ident[:, :])
                mm.then_inc(turned, 1)
                pe.wait_ge(stored, 1)
                for t in range(NT):
                    mm = pe.matmul(p_pickT[:, t * D:(t + 1) * D], pickT[:, t * P:(t + 1) * P], b2[:, :],
                                   start=True, stop=True)
                mm.then_inc(bias_ready, 1)

            @block.scalar
            def _(act):
                act.wait_ge(b1_ready, 1)
                act.copy(b1T[:, :], p_b1T[:, 0:NEXP * MFF])
                act.wait_ge(turned, 1)
                act.copy(pickT[:, :], p_pickT[0:NEXP, :]).then_inc(stored, 1)

            @block.vector
            def _(dve):
                chain = Chain(dve, own)
                dve.wait_ge(loaded, 64)
                dve.wait_ge(ranked, NEXP)
                dve.wait_ge(logits_ready, 1)
                chain.step(dve.tensor_tensor(logits[:, :, :], p_logits[:, 0:NT * NEXP].rearrange("p (t e) -> p t e", e=NEXP),
                                             per_feature(br[:, :], NT), ALU.add))
                chain.step(dve.tensor_reduce(best[:, :], logits[:, :, :], AX, ALU.max))
                chain.step(dve.tensor_tensor(tied[:, :, :], logits[:, :, :], per_token(best[:, :], NEXP), ALU.is_equal))
                chain.step(dve.tensor_tensor(tied[:, :, :], tied[:, :, :], per_feature(rank[:, :], NT), ALU.mult))
                chain.step(dve.tensor_reduce(first[:, :], tied[:, :, :], AX, ALU.max))
                chain.step(dve.tensor_tensor(tied[:, :, :], tied[:, :, :], per_token(first[:, :], NEXP), ALU.is_equal))
                dve.tensor_scalar(pick[:, :, :], tied[:, :, :], 0.5, None, ALU.mult).then_inc(picked, 1)
                dve.wait_ge(bias_ready, 1)
                dve.tensor_tensor(X[:, :, :], X[:, :, :], p_pickT[:, :].rearrange("p (t d) -> p t d", d=D), ALU.add)


def experts(nc, C, I, name, X, xnT, pick, b1T):
    W1 = I["L1_ffn_W1"]
    W2 = I["L1_ffn_W2"]
    with Stage(nc, name + "_experts") as S:
        raw1 = [S.sb(f"raw1_{k}", [P, MFF, D]) for k in range(2)]
        raw2 = [S.sb(f"raw2_{k}", [P, DFF]) for k in range(2)]
        up = [S.sb(f"up{k}", [P, DFF]) for k in range(2)]
        down = [S.sb(f"down{k}", [P, MFF, D]) for k in range(2)]
        b1 = [S.sb(f"b1_{k}", [P, MFF]) for k in range(2)]
        hidden = [S.sb(f"hidden{k}", [P, MFF, CH]) for k in range(2)]
        p_up = S.ps("p_up", [P, MFF, CH])
        p_down = S.ps("p_down", [P, 2, CH])
        p_turn = S.ps("p_turn", [P, 2, DFF])
        loaded = [S.sem(f"loaded{k}") for k in range(2)]
        turned = S.sem("turned")
        up_stored, down_stored = S.sem("up_stored"), S.sem("down_stored")
        up_ready, relu_done = S.sem("up_ready"), S.sem("relu_done")
        down_ready, added = S.sem("down_ready"), S.sem("added")
        PAIRS = NEXP // 2

        with nc.Block() as block:

            @block.sync
            def _(sp):
                def fetch(e, k):
                    sp.dma_start(raw1[k][:, :, :], W1[ds(e, 1)].rearrange("e (m p) d -> p (e m) d", p=P)
                                 ).then_inc(loaded[k], 16)
                    sp.dma_start(raw2[k][:, :], W2[ds(e, 1)].rearrange("e d f -> d (e f)")).then_inc(loaded[k], 16)

                fetch(0, 0)
                fetch(1, 1)
                with sp.Fori(0, PAIRS - 1) as i:
                    for k in range(2):
                        sp.wait_ge(turned, i * 2 + k + 1)
                        fetch(i * 2 + k + 2, k)

            @block.tensor
            def _(pe):
                def turn(k, pair):
                    pe.wait_ge(loaded[k], pair * 32 + 32)
                    for m in range(MFF):
                        pe.transpose(p_turn[:, 0, m * P:(m + 1) * P], raw1[k][:, m, :], C.ident[:, :])
                    for m in range(MFF):
                        mm = pe.transpose(p_turn[:, 1, m * P:(m + 1) * P], raw2[k][:, m * P:(m + 1) * P], C.ident[:, :])
                    mm.then_inc(turned, 1)

                def up_products(i, k, c):
                    before = i * 8 * MFF + (k * NCH + c) * MFF
                    for m in range(MFF):
                        if k or c:
                            pe.wait_ge(relu_done, before - MFF + m + 1)
                        else:
                            pe.wait_ge(relu_done, before)
                        pe.matmul(p_up[:, m, :], up[k][:, m * P:(m + 1) * P], xnT[:, c * CH:(c + 1) * CH],
                                  start=True, stop=True).then_inc(up_ready, 1)

                def down_products(i, k, c):
                    n = i * 8 + k * NCH + c
                    pe.wait_ge(relu_done, (n + 1) * MFF)
                    pe.wait_ge(added, n - 1 if k or c else n)
                    for t in range(TPC):
                        for m in range(MFF):
                            mm = pe.matmul(p_down[:, c % 2, t * D:(t + 1) * D], hidden[c % 2][:, m, t * P:(t + 1) * P],
                                           down[k][:, m, :], start=(m == 0), stop=(m == MFF - 1))
                    mm.then_inc(down_ready, 1)

                def pair(i, last):
                    for k in range(2):
                        pe.wait_ge(up_stored, i * 2 + k + 1)
                        pe.wait_ge(down_stored, i * 2 + k + 1)
                        up_products(i, k, 0)
                        for c in range(NCH):
                            if c + 1 < NCH:
                                up_products(i, k, c + 1)
                            down_products(i, k, c)
                            if c == 1 and not (last and k):
                                turn(1 - k, i + k)

                turn(0, 0)
                with pe.Fori(0, PAIRS - 1) as i:
                    pair(i, False)
                pair(PAIRS - 1, True)

            @block.scalar
            def _(act):
                def pair(i, last):
                    for k in range(2):
                        for c in range(NCH):
                            n = i * 8 + k * NCH + c
                            act.wait_ge(down_ready, n - 1 if k or c else n)
                            for m in range(MFF):
                                act.wait_ge(up_ready, n * MFF + m + 1)
                                act.activation(hidden[c % 2][:, m, :], p_up[:, m, :], ACT.Relu,
                                               bias=b1[k][:, m:m + 1]).then_inc(relu_done, 1)
                        if not (last and k):
                            act.wait_ge(turned, i * 2 + k + 2)
                            act.copy(up[1 - k][:, :], p_turn[:, 0, :]).then_inc(up_stored, 1)

                act.wait_ge(turned, 1)
                act.copy(up[0][:, :], p_turn[:, 0, :]).then_inc(up_stored, 1)
                with act.Fori(0, PAIRS - 1) as i:
                    pair(i, False)
                pair(PAIRS - 1, True)

            @block.vector
            def _(dve):
                def pair(i, last):
                    for k in range(2):
                        for c in range(NCH):
                            n = i * 8 + k * NCH + c
                            dve.wait_ge(down_ready, n + 1)
                            dve.wait_ge(added, n)
                            for t in range(TPC):
                                tile = c * TPC + t
                                last_add = dve.scalar_tensor_tensor(
                                    out=X[:, tile, :], in0=p_down[:, c % 2, t * D:(t + 1) * D],
                                    scalar=pick[:, tile, ds(i * 2 + k, 1)], in1=X[:, tile, :], op0=ALU.mult, op1=ALU.add)
                            last_add.then_inc(added, 1)
                        if not (last and k):
                            dve.wait_ge(turned, i * 2 + k + 2)
                            dve.tensor_copy(down[1 - k][:, :, :], p_turn[:, 1, :].rearrange("p (m d) -> p m d", d=D))
                            dve.tensor_copy(b1[1 - k][:, :], b1T[:, ds((i * 2 + k + 1) * MFF, MFF)]).then_inc(down_stored, 1)

                dve.wait_ge(turned, 1)
                dve.tensor_copy(down[0][:, :, :], p_turn[:, 1, :].rearrange("p (m d) -> p m d", d=D))
                dve.tensor_copy(b1[0][:, :], b1T[:, 0:MFF]).then_inc(down_stored, 1)
                with dve.Fori(0, PAIRS - 1) as i:
                    pair(i, False)
                pair(PAIRS - 1, True)


UNITS = BATCH * H
KR = 4 * HD
KM = KR + 2
VW = HD + 1


def stacked_attention_mixer(nc, C, I, X, xn, xnT):
    with Stage(nc, "mix1") as M:
        parts = {n: nc.dram_tensor(f"mix1_{n}", [2, UNITS * HD, SEQ], F32, kind="Internal") for n in ("q", "k", "k2")}
        V = M.sb("V", [P, UNITS, TPB, VW])
        shifted = M.sb("shifted", [P, NT, D])
        Y = [M.sb(f"Y{n}", [P, UNITS, TPB, HD]) for n in range(2)]
        mask_q = M.sb("mask_q", [P, 2, 2, P], BF16)
        mask_k = M.sb("mask_k", [P, 2, 2, P], BF16)
        ident16 = M.sb("ident16", [P, P], BF16)
        project_and_split(nc, C, I, xn, xnT, parts, V, shifted, mask_q, mask_k, ident16)
        causal_attention(nc, C, "mix1_a", parts["q"], parts["k"], V, Y[0], mask_q[:, 0], mask_k[:, 0], ident16)
        errors(nc, V, shifted, Y[0])
        causal_attention(nc, C, "mix1_b", parts["q"], parts["k2"], V, Y[1], mask_q[:, 1], mask_k[:, 1], ident16)
        project_out(nc, C, I, X, Y)


def tokens_of(V, b):
    return V[:, b * H:(b + 1) * H, :, 0:HD].rearrange("p h t d -> p t h d")


def project_and_split(nc, C, I, xn, xnT, parts, V, shifted, mask_q, mask_k, ident16):
    SCALE = float(HD) ** -0.5
    with Stage(nc, "mix1_proj") as S:
        W = S.sb("W", [P, 3, D])
        bias = S.sb("bias", [P, 3])
        bias_s = S.sb("bias_s", [P, 3])
        full = [S.sb(f"full{k}", [P, CH]) for k in range(2)]
        high = S.sb("high", [P, 3, TOK], F32R)
        low = S.sb("low", [P, 3, TOK], F32R)
        p = S.ps("p", [P, 2, CH])
        loaded, biased, shifted_ok, cleared = S.sem("loaded"), S.sem("biased"), S.sem("shifted_ok"), S.sem("cleared")
        ready, stored, split_high, split = S.sem("ready"), S.sem("stored"), S.sem("split_high"), S.sem("split")
        sent, masks = S.sem("sent"), S.sem("masks")
        N = 3 * NCH
        with nc.Block() as block:

            @block.sync
            def _(sp):
                sp.dma_start(W[:, 0:2, :].rearrange("p a d -> p (a d)"), I["L1_attn_W_attn"]).then_inc(loaded, 16)
                sp.dma_start(W[:, 2, :], I["L1_attn_W_k2"]).then_inc(loaded, 16)
                sp.dma_start(bias[:, 0:2], I["L1_attn_b_attn"].rearrange("(a p) -> p a", p=P),
                             allow_slow_non_contiguous=True).then_inc(loaded, 16)
                sp.dma_start(bias[:, 2:3], I["L1_attn_b_k2"].unsqueeze(1)).then_inc(loaded, 16)
                sp.dma_start(shifted[0:112, :, :], xn[1:113, :, :]).then_inc(shifted_ok, 16)
                sp.dma_start(shifted[112:127, :, :], xn[113:128, :, :]).then_inc(shifted_ok, 16)
                sp.dma_start(shifted[127:128, 0:NT - 1, :], xn[0:1, 1:NT, :]).then_inc(shifted_ok, 16)
                sp.dma_start(shifted[127:128, NT - 1, :], xn[0:1, 0, :]).then_inc(shifted_ok, 16)
                for n, name in enumerate(("q", "k", "k2")):
                    sp.wait_ge(split, NCH * (n + 1))
                    for a, part in enumerate((high, low)):
                        for b in range(BATCH):
                            sp.dma_start(parts[name][a, b * P:(b + 1) * P, :],
                                         part[:, n, b * SEQ:(b + 1) * SEQ].bitcast(F32)).then_inc(sent, 16)
                sp.wait_ge(sent, 16 * 3 * 2 * BATCH)
                sp.wait_ge(shifted_ok, 64)

            @block.tensor
            def _(pe):
                pe.wait_ge(loaded, 64)
                for n in range(3):
                    for c in range(NCH):
                        i = n * NCH + c
                        if i >= 2:
                            pe.wait_ge(stored, i - 1)
                        pe.matmul(p[:, i % 2, :], W[:, n, :], xnT[:, c * CH:(c + 1) * CH],
                                  start=True, stop=True).then_inc(ready, 1)

            @block.scalar
            def _(act):
                act.wait_ge(biased, 1)
                for i in range(N):
                    n = i // NCH
                    act.wait_ge(ready, i + 1)
                    if i >= 2:
                        act.wait_ge(split, i - 1)
                    act.activation(full[i % 2][:, :], p[:, i % 2, :], ACT.Identity, bias=bias_s[:, n:n + 1],
                                   scale=SCALE if n == 0 else 1.0).then_inc(stored, 1)

            @block.vector
            def _(dve):
                dve.wait_ge(loaded, 64)
                dve.tensor_scalar(bias_s[:, 0:1], bias[:, 0:1], SCALE, None, ALU.mult)
                dve.tensor_copy(bias_s[:, 1:3], bias[:, 1:3]).then_inc(biased, 1)
                for i in range(N):
                    n, c = i // NCH, i % NCH
                    col = slice(c * CH, (c + 1) * CH)
                    dve.wait_ge(stored, i + 1)
                    dve.tensor_copy(high[:, n, col], full[i % 2][:, :]).then_inc(split_high, 1)
                    dve.wait_ge(split_high, i + 1)
                    dve.tensor_tensor(low[:, n, col], full[i % 2][:, :], high[:, n, col].bitcast(F32),
                                      ALU.subtract).then_inc(split, 1)
                for b in range(BATCH):
                    for h in range(H):
                        dve.tensor_copy(V[:, b * H + h, :, 0:HD], xn[:, b * TPB:(b + 1) * TPB, h * HD:(h + 1) * HD])
                dve.memset(V[:, :, :, HD:VW], 1.0)
                dve.tensor_copy(ident16[:, :], C.ident[:, :])

            @block.gpsimd
            def _(pool):
                pool.memset(mask_q[:, :, :, :], 0.0)
                pool.memset(mask_k[:, :, :, :], 0.0).then_inc(cleared, 1)
                pool.wait_ge(cleared, 1)
                for strict in range(2):
                    for tile in range(2):
                        pool.affine_select(out=mask_q[:, strict, tile, :], in_=mask_q[:, strict, tile, :],
                                           compare_op=ALU.is_ge, fill=-BIG, base=-strict, pattern=[[-1, P]],
                                           channel_multiplier=1)
                        pool.affine_select(out=mask_k[:, strict, tile, :], in_=mask_k[:, strict, tile, :],
                                           compare_op=ALU.is_ge, fill=-BIG, base=-strict, pattern=[[1, P]],
                                           channel_multiplier=-1).then_inc(masks, 1)
                pool.wait_ge(masks, 4)
                pool.memset(mask_q[0:1, 1, 0, 0:1], 0.0)
                pool.memset(mask_k[0:1, 1, 0, 0:1], 0.0)


def causal_attention(nc, C, name, q_parts, k_parts, V, Y, mask_q, mask_k, ident16):
    SLOTS = 4
    GROUPS = [(qc, kt) for qc in range(SEQ // CH) for kt in range((qc + 1) * TPC)]
    NG = len(GROUPS)
    MAX_AFTER = [0, 2, 3, 5, 6, 8, 9, 11]
    with Stage(nc, name) as S:
        q = [S.sb(f"q{k}", [KM, SEQ], F32R) for k in range(SLOTS)]
        k_ = [S.sb(f"k{k}", [KM, SEQ], F32R) for k in range(SLOTS)]
        neg_max = S.sb("neg_max", [P, TPB])
        max_high = S.sb("max_high", [P, 2 * TPB])
        max_rows = S.sb("max_rows", [2 * TPB, P])
        e = [S.sb(f"e{k}", [P, CH]) for k in range(2)]
        recip = S.sb("recip", [P, TPB])
        p_s = [S.ps(f"p_s{k}", [P, SEQ]) for k in range(2)]
        p_e = [S.ps(f"p_e{k}", [P, CH]) for k in range(2)]
        p_y = S.ps("p_y", [P, TPB, VW])
        p_m = S.ps("p_m", [2 * TPB, P])
        ones_set = S.sem("ones_set")
        loaded = [S.sem(f"loaded{k}") for k in range(SLOTS)]
        s_ready, s_read = S.sem("s_ready"), S.sem("s_read")
        m_own, m_split = S.sem("m_own"), S.sem("m_split")
        m_turned, m_copied, m_sent = S.sem("m_turned"), S.sem("m_copied"), S.sem("m_sent")
        e_scores, e_done, pv_done = S.sem("e_scores"), S.sem("e_done"), S.sem("pv_done")
        y_own, y_read = S.sem("y_own"), S.sem("y_read")
        FULL = UNITS // SLOTS - 1

        with nc.Block() as block:

            @block.sync
            def _(sp):
                def fetch(u, k):
                    rows = ds(u * HD, HD)
                    for half in range(2):
                        at = slice(half * 2 * HD, (half + 1) * 2 * HD)
                        sp.dma_start(q[k][at, :].bitcast(F32), q_parts[half, rows, :].unsqueeze(0).to_broadcast([2, HD, SEQ])
                                     ).then_inc(loaded[k], 16)
                        sp.dma_start(k_[k][at, :].bitcast(F32), k_parts[:, rows, :]).then_inc(loaded[k], 16)

                def send(u, k):
                    sp.wait_ge(m_copied, u + 1)
                    for a in range(2):
                        sp.dma_start(q[k][KR + a:KR + a + 1, :].bitcast(F32), max_rows[a * TPB:(a + 1) * TPB, :]
                                     ).then_inc(m_sent, 16)

                def body(i, last):
                    for k in range(SLOTS):
                        if not (last and k > 0):
                            if k:
                                sp.wait_ge(pv_done, (i * SLOTS + k) * NG)
                            else:
                                sp.wait_ge(pv_done, i * SLOTS * NG)
                            fetch(i * SLOTS + k + 3, (k + 3) % SLOTS)
                        if not (last and k == SLOTS - 1):
                            send(i * SLOTS + k + 1, (k + 1) % SLOTS)

                sp.wait_ge(ones_set, 1)
                for u in range(3):
                    fetch(u, u)
                send(0, 0)
                with sp.Fori(0, FULL) as i:
                    body(i, False)
                body(FULL, True)

            @block.tensor
            def _(pe):
                def scores(u, k, g, first=False):
                    if g == 0:
                        pe.wait_ge(loaded[k % SLOTS], (u - k) * (64 // SLOTS) + 64 * (k // SLOTS + 1))
                    if not (first and g < 2):
                        pe.wait_ge(s_read, u * TPB + g - 1)
                    k = k % SLOTS
                    n = (g + 1) * P
                    for c in range(0, n, CH):
                        w = min(CH, n - c)
                        pe.matmul(p_s[g % 2][:, c:c + w], q[k][0:KR, g * P:(g + 1) * P], k_[k][0:KR, c:c + w],
                                  start=True, stop=(c + w < n), skip_group_check=True)
                    pe.matmul(p_s[g % 2][:, n - P:n], ident16[:, :], mask_q[:, min(g, 1), :], start=False, stop=True,
                              skip_group_check=True).then_inc(s_ready, 1)

                def turn_max(u):
                    pe.wait_ge(m_split, u + 1)
                    pe.transpose(p_m[:, :], max_high[:, :], C.ident[:, :]).then_inc(m_turned, 1)

                def exp_scores(u, k, n):
                    qc, kt = GROUPS[n]
                    q0 = max(kt * P, qc * CH)
                    w = (qc + 1) * CH - q0
                    if n == 0:
                        pe.wait_ge(m_sent, u * 32 + 32)
                    if k or n:
                        if not (n < 2 and isinstance(u, int) and u == 0):
                            pe.wait_ge(e_done, u * NG + n - 1)
                    else:
                        pe.wait_ge(e_done, u * NG)
                    diag = kt * P >= qc * CH
                    mm = pe.matmul(p_e[n % 2][:, 0:w], k_[k][:, kt * P:(kt + 1) * P], q[k][:, q0:q0 + w],
                                   start=True, stop=not diag, skip_group_check=True)
                    if diag:
                        mm = pe.matmul(p_e[n % 2][:, 0:P], ident16[:, :], mask_k[:, min(kt, 1), :], start=False, stop=True,
                                       skip_group_check=True)
                    mm.then_inc(e_scores, 1)

                def times_values(u, k, n):
                    qc, kt = GROUPS[n]
                    q0 = max(kt, qc * TPC)
                    pe.wait_ge(e_done, u * NG + n + 1)
                    if n == 0:
                        pe.wait_ge(y_read, u)
                    for t in range(q0, (qc + 1) * TPC):
                        mm = pe.matmul(p_y[:, t, :], e[n % 2][:, (t - q0) * P:(t - q0 + 1) * P],
                                       V[:, ds(u, 1), kt, :].rearrange("p u w -> p (u w)"),
                                       start=(n == 0 and t == q0), stop=(kt == t), skip_group_check=True)
                    mm.then_inc(pv_done, 1)

                def body(i, last):
                    for k in range(SLOTS):
                        u = i * SLOTS + k
                        for n in range(NG):
                            exp_scores(u, k, n)
                            if n == 1 and not (last and k == SLOTS - 1):
                                turn_max(u + 1)
                            if n:
                                times_values(u, k, n - 1)
                            if n in MAX_AFTER and not (last and k >= 2):
                                scores(u + 2, k + 2, MAX_AFTER.index(n))
                        times_values(u, k, NG - 1)

                for u in range(2):
                    for g in range(TPB):
                        scores(u, u, g, first=(u == 0))
                    if u == 0:
                        turn_max(0)
                with pe.Fori(0, FULL) as i:
                    body(i, False)
                body(FULL, True)

            @block.scalar
            def _(act):
                def copy_max(u):
                    act.wait_ge(m_turned, u + 1)
                    act.wait_ge(m_sent, u * 32)
                    act.copy(max_rows[:, :], p_m[:, :]).then_inc(m_copied, 1)

                def body(i, last):
                    for k in range(SLOTS):
                        u = i * SLOTS + k
                        for n in range(NG):
                            qc, kt = GROUPS[n]
                            w = (qc + 1) * CH - max(kt * P, qc * CH)
                            act.wait_ge(e_scores, u * NG + n + 1)
                            if k or n:
                                if not (isinstance(u, int) and u * NG + n < 1):
                                    act.wait_ge(pv_done, u * NG + n - 1)
                            else:
                                act.wait_ge(pv_done, u * NG)
                            act.activation(e[n % 2][:, 0:w], p_e[n % 2][:, 0:w], ACT.Exp).then_inc(e_done, 1)
                            if n == 1 and not (last and k == SLOTS - 1):
                                copy_max(u + 1)

                copy_max(0)
                with act.Fori(0, FULL) as i:
                    body(i, False)
                body(FULL, True)

            @block.vector
            def _(dve):
                def maxima(u):
                    dve.wait_ge(m_split, u)
                    for g in range(TPB):
                        dve.wait_ge(s_ready, u * TPB + g + 1)
                        dve.tensor_reduce(neg_max[:, g:g + 1], p_s[g % 2][:, 0:(g + 1) * P], AX, ALU.max, negate=True
                                          ).then_inc(s_read, 1)
                    dve.wait_ge(s_read, (u + 1) * TPB)
                    dve.wait_ge(m_turned, u)
                    dve.tensor_copy(max_high[:, 0:TPB].bitcast(F32R), neg_max[:, :]).then_inc(m_own, 1)
                    dve.wait_ge(m_own, u + 1)
                    dve.tensor_tensor(max_high[:, TPB:2 * TPB].bitcast(F32R), neg_max[:, :], max_high[:, 0:TPB],
                                      ALU.subtract).then_inc(m_split, 1)

                def body(i, last):
                    for k in range(SLOTS):
                        u = i * SLOTS + k
                        if not (last and k >= 2):
                            maxima(u + 2)
                        dve.wait_ge(pv_done, (u + 1) * NG)
                        dve.reciprocal(recip[:, :], p_y[:, :, HD]).then_inc(y_own, 1)
                        dve.wait_ge(y_own, u + 1)
                        dve.tensor_tensor(Y[:, ds(u, 1), :, :].rearrange("p u t d -> p (u t) d"), p_y[:, :, 0:HD],
                                          per_token(recip[:, :], HD), ALU.mult).then_inc(y_read, 1)

                for k in range(SLOTS):
                    last = dve.memset(k_[k][KR:KM, :].bitcast(F32), 1.0)
                last.then_inc(ones_set, 1)
                maxima(0)
                maxima(1)
                with dve.Fori(0, FULL) as i:
                    body(i, False)
                body(FULL, True)


def errors(nc, V, shifted, Y):
    with nc.Block() as block:

        @block.vector
        def _(dve):
            for b in range(BATCH):
                for h in range(H):
                    dve.tensor_tensor(V[:, b * H + h, :, 0:HD], shifted[:, b * TPB:(b + 1) * TPB, h * HD:(h + 1) * HD],
                                      Y[:, b * H + h, :, :], ALU.subtract)


def project_out(nc, C, I, X, Y):
    G = NT // TPC
    with Stage(nc, "mix1_out") as S:
        W = S.sb("W", [P, D])
        bias = S.sb("bias", [1, D])
        bias2 = S.sb("bias2", [1, D])
        total = S.sb("total", [P, NT, D])
        totalT = S.sb("totalT", [P, TOK])
        p_turn = S.ps("p_turn", [P, 2, CH])
        p_out = S.ps("p_out", [P, 2, CH])
        loaded, own, summed = S.sem("loaded"), S.sem("own"), S.sem("summed")
        turned, stored, ready, added, bias_ok = (S.sem("turned"), S.sem("stored"), S.sem("ready"), S.sem("added"),
                                                 S.sem("bias_ok"))
        with nc.Block() as block:

            @block.sync
            def _(sp):
                sp.dma_start(W[:, :], I["L1_attn_W_proj"]).then_inc(loaded, 16)
                sp.dma_start(bias[:, :], I["L1_attn_b_proj"].unsqueeze(0)).then_inc(loaded, 16)

            @block.vector
            def _(dve):
                chain = Chain(dve, own)
                for b in range(BATCH):
                    chain.step(dve.memset(Y[1][0:1, b * H:(b + 1) * H, 0, :], 0.0))
                for b in range(BATCH):
                    for h in range(H):
                        last = dve.tensor_tensor(total[:, b * TPB:(b + 1) * TPB, h * HD:(h + 1) * HD], Y[0][:, b * H + h, :, :],
                                                 Y[1][:, b * H + h, :, :], ALU.add)
                    last.then_inc(summed, 1)
                dve.wait_ge(loaded, 32)
                dve.tensor_scalar(bias2[:, :], bias[:, :], 2.0, None, ALU.mult).then_inc(bias_ok, 1)
                for g in range(G):
                    t = slice(g * TPC, (g + 1) * TPC)
                    dve.wait_ge(ready, g + 1)
                    dve.tensor_tensor(X[:, t, :], X[:, t, :], p_out[:, g % 2, :].rearrange("p (t d) -> p t d", d=D),
                                      ALU.add).then_inc(added, 1)

            @block.tensor
            def _(pe):
                def turn(g):
                    pe.wait_ge(summed, g * TPC // TPB + 1)
                    if g >= 2:
                        pe.wait_ge(stored, g - 1)
                    for k in range(TPC):
                        mm = pe.transpose(p_turn[:, g % 2, k * P:(k + 1) * P], total[:, g * TPC + k, :], C.ident[:, :])
                    mm.then_inc(turned, 1)

                turn(0)
                pe.wait_ge(bias_ok, 1)
                for g in range(G):
                    if g + 1 < G:
                        turn(g + 1)
                    pe.wait_ge(stored, g + 1)
                    if g >= 2:
                        pe.wait_ge(added, g - 1)
                    for k in range(TPC):
                        t = g * TPC + k
                        pe.matmul(p_out[:, g % 2, k * D:(k + 1) * D], C.ones[0:1, :], bias2[:, :], start=True, stop=False)
                        mm = pe.matmul(p_out[:, g % 2, k * D:(k + 1) * D], totalT[:, t * P:(t + 1) * P], W[:, :],
                                       start=False, stop=True)
                    mm.then_inc(ready, 1)

            @block.scalar
            def _(act):
                for g in range(G):
                    act.wait_ge(turned, g + 1)
                    act.copy(totalT[:, g * CH:(g + 1) * CH], p_turn[:, g % 2, :]).then_inc(stored, 1)


AH, AD = 16, 64
DIST0 = SEQ - P


def wait(eng, sem, value):
    if not (isinstance(value, int) and value <= 0):
        eng.wait_ge(sem, value)


def alibi_attention_mixer(nc, C, I, X, xn, xnT):
    with Stage(nc, "mix2") as M:
        gamma = M.sb("gamma", [P, D])
        beta = M.sb("beta", [P, D])
        dist = M.sb("dist", [P, DIST0 + SEQ])
        slopes = M.sb("slopes", [P, AH])
        load(nc, "mix2_load", [(gamma[:, :], I["L2_attn_ln_gamma"].partition_broadcast(P)),
                               (beta[:, :], I["L2_attn_ln_beta"].partition_broadcast(P))])
        normalise(nc, C, "mix2_norm", xn, xn, xnT, gamma=gamma[:, :], beta=beta[:, :])
        with Stage(nc, "mix2_tables") as S:
            steps = S.sb("steps", [P, DIST0 + SEQ], mybir.dt.int32)
            signed = S.sb("signed", [P, DIST0 + SEQ])
            made, own = S.sem("made"), S.sem("own")
            with nc.Block() as block:

                @block.gpsimd
                def _(pool):
                    pool.iota(steps[:, :], pattern=[[-1, DIST0 + SEQ]], base=DIST0, channel_multiplier=1).then_inc(made, 1)
                    for h in range(AH):
                        pool.memset(slopes[:, h:h + 1], -float(np.float32(2.0 ** (-8.0 / (AH - h)))))

                @block.vector
                def _(dve):
                    chain = Chain(dve, own)
                    dve.wait_ge(made, 1)
                    chain.step(dve.tensor_copy(signed[:, :], steps[:, :]))
                    chain.step(dve.tensor_scalar(dist[:, :], signed[:, :], -1.0, None, ALU.mult))
                    chain.step(dve.tensor_tensor(dist[:, :], dist[:, :], signed[:, :], ALU.max))

        for b in range(BATCH):
            with Stage(nc, f"mix2_{b}") as S:
                V = S.sb("V", [P, AH, TPB, AD + 1])
                outT = S.sb("outT", [P, SEQ])
                head_values(nc, C, I, f"mix2_v{b}", b, xnT, V)
                alibi_heads(nc, C, I, f"mix2_h{b}", b, xnT, V, dist, slopes, outT)
                add_turned(nc, C, f"mix2_o{b}", X, outT, b)


def head_values(nc, C, I, name, b, xnT, V):
    with Stage(nc, name) as S:
        Wv = S.sb("Wv", [P, AH * AD])
        p = S.ps("p", [P, 4, CH])
        loaded, ready, stored = S.sem("loaded"), S.sem("ready"), S.sem("stored")
        HC = CH // AD
        with nc.Block() as block:

            @block.sync
            def _(sp):
                sp.dma_start(Wv[:, :], I["L2_attn_Wv"]).then_inc(loaded, 16)

            @block.tensor
            def _(pe):
                pe.wait_ge(loaded, 16)
                for t in range(TPB):
                    for c in range(2):
                        i = t * 2 + c
                        if i >= 4:
                            pe.wait_ge(stored, i - 3)
                        pe.matmul(p[:, i % 4, :], xnT[:, b * SEQ + t * P:b * SEQ + (t + 1) * P], Wv[:, c * CH:(c + 1) * CH],
                                  start=True, stop=True).then_inc(ready, 1)

            @block.scalar
            def _(act):
                for t in range(TPB):
                    for c in range(2):
                        i = t * 2 + c
                        act.wait_ge(ready, i + 1)
                        act.copy(V[:, c * HC:(c + 1) * HC, t, 0:AD], p[:, i % 4, :].rearrange("p (h d) -> p h d", d=AD)
                                 ).then_inc(stored, 1)

            @block.vector
            def _(dve):
                dve.memset(V[:, :, :, AD:AD + 1], 1.0)


def alibi_heads(nc, C, I, name, b, xnT, V, dist, slopes, outT):
    NE = 16
    SLOTS = 4
    SCHEDULE = []
    taken = 0
    for n in range(NE):
        SCHEDULE.append(("E", n))
        if n:
            SCHEDULE.append(("V", n - 1))
        while taken < min(NE, NE * (n + 1) // 12):
            SCHEDULE.append(("S", taken))
            taken += 1
        SCHEDULE += {1: [("P", 0), ("b", 0)], 3: [("o", 0)], 4: [("P", 1), ("b", 1)], 6: [("o", 1)], 7: [("P", 2)],
                     10: [("P", 3)], 12: [("M", 0)], 14: [("T", 0)]}.get(n, [])
    SCHEDULE += [("V", NE - 1), ("Y", 0)]

    with Stage(nc, name) as S:
        wq = [S.sb(f"wq{k}", [P, 2 * AD]) for k in range(SLOTS)]
        wk = [S.sb(f"wk{k}", [P, 2 * AD]) for k in range(SLOTS)]
        wo = [S.sb(f"wo{k}", [AD, D]) for k in range(SLOTS)]
        q1 = [S.sb(f"q1_{k}", [P, SEQ], F32R) for k in range(SLOTS)]
        k1 = [S.sb(f"k1_{k}", [P, SEQ], F32R) for k in range(SLOTS)]
        q2 = [S.sb(f"q2_{k}", [AD + 2, SEQ], F32R) for k in range(SLOTS)]
        k2 = [S.sb(f"k2_{k}", [AD + 2, SEQ], F32R) for k in range(SLOTS)]
        bias = [S.sb(f"bias{k}", [P, DIST0 + SEQ]) for k in range(SLOTS)]
        slope = [S.sb(f"slope{k}", [P, 1]) for k in range(SLOTS)]
        vals = [S.sb(f"vals{k}", [P, TPB, AD + 1]) for k in range(SLOTS)]
        junk = S.sb("junk", [P, CH])
        start, zero = S.sb("start", [1, 1]), C.zeros[0:1, 0:1]
        half_max = S.sb("half_max", [P, TPB, 2])
        neg_max = S.sb("neg_max", [P, TPB])
        max_parts = S.sb("max_parts", [P, 2 * TPB])
        max_rows = S.sb("max_rows", [2 * TPB, P])
        biased = [S.sb(f"biased{k}", [P, CH]) for k in range(2)]
        e = [S.sb(f"e{k}", [P, CH]) for k in range(2)]
        y = S.sb("y", [AD + 1, SEQ])
        recip = S.sb("recip", [AD + 1, SEQ])
        y_norm = S.sb("y_norm", [AD, SEQ])
        p_p = S.ps("p_p", [P, CH])
        p_s = [S.ps(f"p_s{k}", [P, CH]) for k in range(2)]
        p_e = [S.ps(f"p_e{k}", [P, CH]) for k in range(2)]
        p_y = S.ps("p_y", [P, SEQ])
        p_x = S.ps("p_x", [P, CH])
        loaded = [S.sem(f"loaded{k}") for k in range(SLOTS)]
        ones_set, cleared, sloped, prepared = S.sem("ones_set"), S.sem("cleared"), S.sem("sloped"), S.sem("prepared")
        p_ready, high_done, low_done, q2_done = S.sem("p_ready"), S.sem("high_done"), S.sem("low_done"), S.sem("q2_done")
        s_ready, s_read = S.sem("s_ready"), S.sem("s_read")
        m_own, m_split, m_turned, m_copied, m_sent = (S.sem("m_own"), S.sem("m_split"), S.sem("m_turned"),
                                                      S.sem("m_copied"), S.sem("m_sent"))
        e_scores, e_biased, e_done, pv_done = S.sem("e_scores"), S.sem("e_biased"), S.sem("e_done"), S.sem("pv_done")
        y_copied, y_recip, y_spread, y_done = S.sem("y_copied"), S.sem("y_recip"), S.sem("y_spread"), S.sem("y_done")
        o_ready, o_added = S.sem("o_ready"), S.sem("o_added")

        def slot_of(k, ahead=0):
            return (k + ahead) % SLOTS

        def steps(eng, step):
            step(0, 0)
            with eng.Fori(0, AH // SLOTS - 1) as i:
                for k in range(1, SLOTS + 1):
                    step(i * SLOTS + k, k % SLOTS)
            for u in range(AH - SLOTS + 1, AH):
                step(u, u % SLOTS)

        def exists(u, ahead):
            return not isinstance(u, int) or 0 <= u + ahead < AH

        def loop_turn(u, k):
            return u // SLOTS + 1 if isinstance(u, int) else None

        with nc.Block() as block:

            @block.sync
            def _(sp):
                def fetch(u, k):
                    for half in range(2):
                        cols = slice(half * AD, (half + 1) * AD)
                        sp.dma_start(wq[k][:, cols], I["L2_attn_Wq"][:, ds(u * AD, AD)]).then_inc(loaded[k], 16)
                        sp.dma_start(wk[k][:, cols], I["L2_attn_Wk"][:, ds(u * AD, AD)]).then_inc(loaded[k], 16)
                    sp.dma_start(wo[k][:, :], I["L2_attn_Wo"][ds(u * AD, AD), :]).then_inc(loaded[k], 16)

                def send(u, k):
                    sp.wait_ge(m_copied, u + 1)
                    for a in range(2):
                        sp.dma_start(q2[k][AD + a:AD + a + 1, :].bitcast(F32), max_rows[a * TPB:(a + 1) * TPB, :]
                                     ).then_inc(m_sent, 16)

                def step(u, k):
                    if exists(u, 1):
                        send(u + 1, slot_of(k, 1))
                    if exists(u, 3):
                        wait(sp, o_added, u * 2)
                        fetch(u + 3, slot_of(k, 3))

                for u in range(3):
                    fetch(u, u)
                send(0, 0)
                steps(sp, step)

            @block.gpsimd
            def _(pool):
                def prepare(u, k):
                    pool.tensor_copy(slope[k][:, :], slopes[:, ds(u, 1)]).then_inc(sloped, 1)
                    pool.tensor_copy(vals[k][:, :, :], V[:, ds(u, 1), :, :].rearrange("p u t d -> p (u t) d"))
                    pool.wait_ge(sloped, u + 1)
                    pool.tensor_tensor(bias[k][:, :], dist[:, :], slope[k][:, 0:1].to_broadcast([P, DIST0 + SEQ]), ALU.mult
                                       ).then_inc(prepared, 1)

                def step(u, k):
                    if exists(u, 2):
                        wait(pool, pv_done, (u - 1) * NE)
                        pool.nop()
                        prepare(u + 2, slot_of(k, 2))

                prepare(0, 0)
                prepare(1, 1)
                steps(pool, step)

            @block.tensor
            def _(pe):
                def project(u, k, j):
                    if j == 0:
                        pe.wait_ge(loaded[k], (u - k) * (80 // SLOTS) + 80)
                    wait(pe, low_done, u * 4 + j)
                    c = j % 2
                    pe.matmul(p_p[:, :], (wq if j < 2 else wk)[k][:, :], xnT[:, b * SEQ + c * CH:b * SEQ + (c + 1) * CH],
                              start=True, stop=True).then_inc(p_ready, 1)

                def scores(u, k, g):
                    t, c = g // 2, g % 2
                    if g == 0:
                        pe.wait_ge(low_done, u * 4 + 4)
                        pe.wait_ge(q2_done, u * 2 + 2)
                    wait(pe, s_read, u * NE + g - 1)
                    keys = slice(c * CH, (c + 1) * CH)
                    queries = slice(t * P, (t + 1) * P)
                    pe.matmul(p_s[g % 2][:, :], q1[k][:, queries], k1[k][:, keys], start=True, stop=False)
                    pe.matmul(p_s[g % 2][:, :], q2[k][0:AD, queries], k2[k][0:AD, keys], start=False, stop=True
                              ).then_inc(s_ready, 1)

                def exp_scores(u, k, n):
                    t, c = n // 2, n % 2
                    if n == 0:
                        pe.wait_ge(m_sent, u * 32 + 32)
                    wait(pe, e_biased, u * NE + n - 1)
                    keys = slice(t * P, (t + 1) * P)
                    queries = slice(c * CH, (c + 1) * CH)
                    pe.matmul(p_e[n % 2][:, :], k1[k][:, keys], q1[k][:, queries], start=True, stop=False)
                    pe.matmul(p_e[n % 2][:, :], k2[k][:, keys], q2[k][:, queries], start=False, stop=True
                              ).then_inc(e_scores, 1)

                def times_values(u, k, n):
                    t, c = n // 2, n % 2
                    if n == 0:
                        pe.wait_ge(prepared, u + 1)
                        wait(pe, y_copied, u)
                    pe.wait_ge(e_done, u * NE + n + 1)
                    pe.matmul(p_y[0:AD + 1, c * CH:(c + 1) * CH], vals[k][:, t, :], e[n % 2][:, :], start=(t == 0),
                              stop=(t == TPB - 1), skip_group_check=True).then_inc(pv_done, 1)

                def spread(u, c):
                    if c == 0:
                        pe.wait_ge(y_recip, u + 1)
                        pe.wait_ge(m_copied, u + 2 if exists(u, 1) else AH)
                    else:
                        pe.wait_ge(o_added, u * 2 + 1)
                    pe.matmul(p_x[0:AD, :], C.ones[AD:AD + 1, 0:AD], recip[AD:AD + 1, c * CH:(c + 1) * CH],
                              start=True, stop=True).then_inc(y_spread, 1)

                def output(u, k, c):
                    pe.wait_ge(y_done, u * 2 + c + 1)
                    pe.matmul(p_x[:, :], wo[k][:, :], y_norm[:, c * CH:(c + 1) * CH], start=True, stop=True
                              ).then_inc(o_ready, 1)

                def turn_max(u):
                    pe.wait_ge(m_split, u + 1)
                    wait(pe, o_added, u * 2 - 2)
                    pe.transpose(p_x[0:2 * TPB, 0:P], max_parts[:, :], C.ident[:, :]).then_inc(m_turned, 1)

                def step(u, k):
                    for what, n in SCHEDULE:
                        if what == "E":
                            exp_scores(u, k, n)
                        elif what == "V":
                            times_values(u, k, n)
                        elif what == "P" and exists(u, 2):
                            project(u + 2, slot_of(k, 2), n)
                        elif what == "S" and exists(u, 1):
                            scores(u + 1, slot_of(k, 1), n)
                        elif what == "T" and exists(u, 1):
                            turn_max(u + 1)
                        elif what == "b" and exists(u, -1):
                            spread(u - 1, n)
                        elif what == "o" and exists(u, -1):
                            output(u - 1, slot_of(k, 3), n)

                for u in range(2):
                    for j in range(4):
                        project(u, u, j)
                for g in range(NE):
                    scores(0, 0, g)
                turn_max(0)
                steps(pe, step)
                for c in range(2):
                    spread(AH - 1, c)
                    output(AH - 1, (AH - 1) % SLOTS, c)

            @block.scalar
            def _(act):
                def high_parts(u, k, j):
                    c = slice(j % 2 * CH, (j % 2 + 1) * CH)
                    act.wait_ge(p_ready, u * 4 + j + 1)
                    if j == 0:
                        wait(act, pv_done, (u - 3) * NE)
                    if j < 2:
                        act.activation(q1[k][:, c], p_p[:, :], ACT.Copy, scale=AD ** -0.5).then_inc(high_done, 1)
                        act.wait_ge(high_done, u * 4 + j + 1)
                        act.copy(q2[k][0:AD, c], q1[k][0:AD, c].bitcast(F32)).then_inc(q2_done, 1)
                    else:
                        act.copy(k1[k][:, c], p_p[:, :]).then_inc(high_done, 1)

                def step(u, k):
                    for what, n in SCHEDULE:
                        if what == "E":
                            act.wait_ge(e_biased, u * NE + n + 1)
                            wait(act, pv_done, u * NE + n - 1)
                            act.activation(e[n % 2][:, :], biased[n % 2][:, :], ACT.Exp).then_inc(e_done, 1)
                        elif what == "P" and exists(u, 2):
                            high_parts(u + 2, slot_of(k, 2), n)
                        elif what == "T" and exists(u, 1):
                            copy_max(u + 1)
                        elif what == "Y":
                            act.wait_ge(pv_done, (u + 1) * NE)
                            wait(act, y_done, u * 2)
                            act.copy(y[:, :], p_y[0:AD + 1, :]).then_inc(y_copied, 1)

                def copy_max(u):
                    act.wait_ge(m_turned, u + 1)
                    wait(act, m_sent, u * 32)
                    act.copy(max_rows[:, :], p_x[0:2 * TPB, 0:P]).then_inc(m_copied, 1)

                for u in range(2):
                    for j in range(4):
                        high_parts(u, u, j)
                copy_max(0)
                steps(act, step)

            @block.vector
            def _(dve):
                def low_parts(u, k, j):
                    c = slice(j % 2 * CH, (j % 2 + 1) * CH)
                    dve.wait_ge(high_done, u * 4 + j + 1)
                    if j < 2:
                        dve.scalar_tensor_tensor(out=q1[k][AD:P, c], in0=p_p[AD:P, :], scalar=AD ** -0.5,
                                                 in1=q1[k][AD:P, c].bitcast(F32), op0=ALU.mult, op1=ALU.subtract
                                                 ).then_inc(low_done, 1)
                    else:
                        dve.tensor_tensor(k2[k][0:AD, c], p_p[0:AD, :], k1[k][0:AD, c].bitcast(F32), ALU.subtract
                                          ).then_inc(low_done, 1)

                def max_of(u, k, g):
                    t, c = g // 2, g % 2
                    if g == 0:
                        dve.wait_ge(prepared, u + 1)
                        wait(dve, m_own, u * 2)
                    dve.wait_ge(s_ready, u * NE + g + 1)
                    wait(dve, s_read, u * NE + g)
                    dve.tensor_copy(start[:, :], zero[:, :])
                    at = DIST0 - t * P + c * CH
                    dve.tensor_tensor_reduce(junk[:, :], p_s[g % 2][:, :], bias[k][:, at:at + CH], 1.0, -3.0e38, ALU.add,
                                             ALU.max, half_max[:, t, c:c + 1]).then_inc(s_read, 1)

                def split_max(u):
                    dve.wait_ge(s_read, (u + 1) * NE)
                    wait(dve, m_split, u)
                    dve.tensor_reduce(neg_max[:, :], half_max[:, :, :], AX, ALU.max, negate=True).then_inc(m_own, 1)
                    dve.wait_ge(m_own, u * 2 + 1)
                    wait(dve, m_turned, u)
                    dve.tensor_copy(max_parts[:, 0:TPB].bitcast(F32R), neg_max[:, :]).then_inc(m_own, 1)
                    dve.wait_ge(m_own, u * 2 + 2)
                    dve.tensor_tensor(max_parts[:, TPB:2 * TPB].bitcast(F32R), neg_max[:, :], max_parts[:, 0:TPB],
                                      ALU.subtract).then_inc(m_split, 1)

                def normalised(u, c):
                    if c == 0:
                        wait(dve, o_ready, u * 2)
                    dve.wait_ge(y_spread, u * 2 + c + 1)
                    dve.tensor_tensor(y_norm[:, c * CH:(c + 1) * CH], y[0:AD, c * CH:(c + 1) * CH], p_x[0:AD, :], ALU.mult
                                      ).then_inc(y_done, 1)

                def add_output(u, c):
                    dve.wait_ge(o_ready, u * 2 + c + 1)
                    wait(dve, o_added, u * 2 + c)
                    dve.tensor_tensor(outT[:, c * CH:(c + 1) * CH], outT[:, c * CH:(c + 1) * CH], p_x[:, :], ALU.add
                                      ).then_inc(o_added, 1)

                def step(u, k):
                    for what, n in SCHEDULE:
                        if what == "E":
                            t, c = n // 2, n % 2
                            at = DIST0 - t * P + c * CH
                            dve.wait_ge(e_scores, u * NE + n + 1)
                            wait(dve, e_done, u * NE + n - 1)
                            dve.tensor_tensor(biased[n % 2][:, :], p_e[n % 2][:, :], bias[k][:, at:at + CH], ALU.add
                                              ).then_inc(e_biased, 1)
                        elif what == "P" and exists(u, 2):
                            low_parts(u + 2, slot_of(k, 2), n)
                        elif what == "S" and exists(u, 1):
                            max_of(u + 1, slot_of(k, 1), n)
                        elif what == "M" and exists(u, 1):
                            split_max(u + 1)
                        elif what == "b" and exists(u, -1):
                            normalised(u - 1, n)
                        elif what == "o" and exists(u, -1):
                            add_output(u - 1, n)
                        elif what == "Y":
                            dve.wait_ge(y_copied, u + 1)
                            wait(dve, y_spread, u * 2)
                            dve.reciprocal(recip[AD:AD + 1, :], y[AD:AD + 1, :]).then_inc(y_recip, 1)

                for k in range(SLOTS):
                    last = dve.memset(k2[k][AD:AD + 2, :].bitcast(F32), 1.0)
                dve.memset(outT[:, :], 0.0).then_inc(ones_set, 1)
                dve.wait_ge(ones_set, 1)
                for u in range(2):
                    for j in range(4):
                        low_parts(u, u, j)
                for g in range(NE):
                    max_of(0, 0, g)
                split_max(0)
                steps(dve, step)
                for c in range(2):
                    normalised(AH - 1, c)
                    add_output(AH - 1, c)


def add_turned(nc, C, name, X, outT, b):
    with Stage(nc, name) as S:
        p = S.ps("p", [P, TPB // TPC, CH])
        ready = S.sem("ready")
        with nc.Block() as block:

            @block.tensor
            def _(pe):
                for g in range(TPB // TPC):
                    for k in range(TPC):
                        t = g * TPC + k
                        mm = pe.transpose(p[:, g, k * P:(k + 1) * P], outT[:, t * P:(t + 1) * P], C.ident[:, :])
                    mm.then_inc(ready, 1)

            @block.vector
            def _(dve):
                for g in range(TPB // TPC):
                    t = slice(b * TPB + g * TPC, b * TPB + (g + 1) * TPC)
                    dve.wait_ge(ready, g + 1)
                    dve.tensor_tensor(X[:, t, :], X[:, t, :], p[:, g, :].rearrange("p (t d) -> p t d", d=D), ALU.add)


TWO_PI = (6.28125, 0.0019350051879882812, 3.0199159819567e-07)
ROUND = 1.5 * 2.0 ** 23


def resonant_mixer(nc, C, I, X, xn):
    with Stage(nc, "mix3") as S:
        rows = S.sb("rows", [P, 3, D])
        gamma = S.sb("gamma", [P, D])
        turns = S.sb("turns", [P, D])
        angle = S.sb("angle", [P, D])
        re_c = S.sb("re_c", [P, D])
        past0 = S.sb("past0", [P, D])
        past1 = S.sb("past1", [P, D])
        y0 = S.sb("y0", [P, TPB, D])
        y1 = S.sb("y1", [P, TPB, D])
        loaded, own, own_act, own_pool = S.sem("loaded"), S.sem("own"), S.sem("own_act"), S.sem("own_pool")
        decayed, reduced, cos_done, past_done = S.sem("decayed"), S.sem("reduced"), S.sem("cos_done"), S.sem("past_done")
        x0, x1 = xn[:, 0:TPB, :], xn[:, TPB:NT, :]
        with nc.Block() as block:

            @block.sync
            def _(sp):
                for j, row in enumerate(("lmlg", "theta", "last_conv_init")):
                    sp.dma_start(rows[:, j, :], I["L3_attn_" + row].partition_broadcast(P)).then_inc(loaded, 16)

            @block.scalar
            def _(act):
                chain = Chain(act, own_act)
                act.wait_ge(loaded, 48)
                chain.step(act.activation(gamma[:, :], rows[:, 0, :], ACT.Exp))
                act.activation(gamma[:, :], gamma[:, :], ACT.Exp, scale=-1.0).then_inc(decayed, 1)
                act.wait_ge(reduced, 1)
                act.activation(re_c[:, :], angle[:, :], ACT.Sin).then_inc(cos_done, 1)

            @block.vector
            def _(dve):
                chain = Chain(dve, own)
                dve.wait_ge(loaded, 48)
                chain.step(dve.tensor_scalar(turns[:, :], rows[:, 1, :], float(1.0 / (2 * np.pi)), None, ALU.mult))
                chain.step(dve.tensor_scalar(turns[:, :], turns[:, :], ROUND, None, ALU.add))
                chain.step(dve.tensor_scalar(turns[:, :], turns[:, :], -ROUND, None, ALU.add))
                chain.step(dve.tensor_copy(angle[:, :], rows[:, 1, :]))
                for part in TWO_PI:
                    chain.step(dve.scalar_tensor_tensor(out=angle[:, :], in0=turns[:, :], scalar=-part, in1=angle[:, :],
                                                        op0=ALU.mult, op1=ALU.add))
                chain.step(dve.tensor_scalar(turns[:, :], angle[:, :], -1.0, None, ALU.mult))
                chain.step(dve.tensor_tensor(angle[:, :], angle[:, :], turns[:, :], ALU.max))
                dve.tensor_scalar(angle[:, :], angle[:, :], -1.0, float(np.pi / 2), ALU.mult, ALU.add).then_inc(reduced, 1)
                dve.wait_ge(decayed, 1)
                dve.wait_ge(cos_done, 1)
                chain.step(dve.tensor_tensor(re_c[:, :], re_c[:, :], gamma[:, :], ALU.mult))
                chain.step(dve.tensor_tensor(past0[:, :], re_c[:, :], rows[:, 2, :], ALU.mult))
                chain.step(dve.tensor_tensor(past1[:, :], re_c[:, :], re_c[:, :], ALU.mult))
                chain.step(dve.tensor_tensor(gamma[:, :], gamma[:, :], gamma[:, :], ALU.mult))
                chain.step(dve.scalar_tensor_tensor(out=past1[:, :], in0=past1[:, :], scalar=2.0, in1=gamma[:, :],
                                                    op0=ALU.mult, op1=ALU.subtract))
                dve.tensor_tensor(past1[:, :], past1[:, :], rows[:, 2, :], ALU.mult).then_inc(past_done, 1)
                dve.wait_ge(past_done, 1)
                chain.step(dve.tensor_tensor(y1[:, :, :], x0, per_feature(re_c[:, :], TPB), ALU.mult))
                chain.step(dve.tensor_tensor(y1[:, :, :], y1[:, :, :], per_feature(past1[:, :], TPB), ALU.add))
                chain.step(dve.tensor_tensor(y1[:, :, :], y1[:, :, :], x1, ALU.add))
                chain.step(dve.tensor_tensor(y1[:, :, :], y1[:, :, :], x1, ALU.mult))
                dve.tensor_tensor(X[:, TPB:NT, :], X[:, TPB:NT, :], y1[:, :, :], ALU.add)

            @block.gpsimd
            def _(pool):
                chain = Chain(pool, own_pool)
                pool.wait_ge(past_done, 1)
                chain.step(pool.tensor_tensor(y0[:, :, :], x0, per_feature(past0[:, :], TPB), ALU.add))
                chain.step(pool.tensor_tensor(y0[:, :, :], y0[:, :, :], x0, ALU.mult))
                pool.tensor_tensor(X[:, 0:TPB, :], X[:, 0:TPB, :], y0[:, :, :], ALU.add)


SE = 16
SLOT = 64
NSLOT = SE * SLOT
ST = NSLOT // P
SFF = 256
MSF = SFF // P


def slot_directions(nc, C, I, seT):
    with Stage(nc, "slots") as S:
        raw = S.sb("raw", [P, ST, D])
        gamma, beta, scale = S.sb("gamma", [P, D]), S.sb("beta", [P, D]), S.sb("scale", [P, 1])
        load(nc, "slots_load", [(raw[:, :, :], I["L3_ffn_slot_embeds"].rearrange("e s d -> (e s) d").rearrange(
                                    "(t p) d -> p t d", p=P)),
                                (gamma[:, :], I["L3_ffn_slot_g"].partition_broadcast(P)),
                                (beta[:, :], I["L3_ffn_slot_b"].partition_broadcast(P)),
                                (scale[:, :], I["L3_ffn_scale"].partition_broadcast(P))])
        with nc.Block() as block:

            @block.vector
            def _(dve):
                dve.tensor_scalar(gamma[:, :], gamma[:, :], scale[:, 0:1], None, ALU.mult)
                dve.tensor_scalar(beta[:, :], beta[:, :], scale[:, 0:1], None, ALU.mult)

        normalise(nc, C, "slots_norm", raw, raw, seT, gamma=gamma[:, :], beta=beta[:, :], tiles=ST)


def soft_moe_ffn(nc, C, I, name, X, xn, xnT, seT):
    with Stage(nc, name) as M:
        gamma, beta = M.sb("gamma", [P, D]), M.sb("beta", [P, D])
        slotsT = M.sb("slotsT", [P, SE, BATCH, SLOT])
        eout = M.sb("eout", [P, BATCH, ST, D])
        outT = M.sb("outT", [P, SEQ])
        load(nc, name + "_load", [(gamma[:, :], I["L3_ffn_norm_g"].partition_broadcast(P)),
                                  (beta[:, :], I["L3_ffn_norm_b"].partition_broadcast(P))])
        normalise(nc, C, name + "_norm", xn, xn, xnT, gamma=gamma[:, :], beta=beta[:, :])
        for b in range(BATCH):
            softmax_apply(nc, C, f"{name}_in{b}", seT, xnT[:, b * SEQ:(b + 1) * SEQ], xn[:, b * TPB:(b + 1) * TPB, :],
                          slotsT[:, :, b, :], 1.0)
        slot_experts(nc, C, I, name + "_exp", slotsT, eout)
        for b in range(BATCH):
            softmax_apply(nc, C, f"{name}_out{b}", xnT[:, b * SEQ:(b + 1) * SEQ], seT, eout[:, b, :, :],
                          outT[:, :].rearrange("p (e s) -> p e s", s=SLOT), 0.5)
            add_turned(nc, C, f"{name}_add{b}", X, outT, b)


def softmax_apply(nc, C, name, A, B, W, dst, factor):
    TILES = SEQ // P
    HALF = TILES // 2
    with Stage(nc, name) as S:
        stat = [S.sb(f"stat{k}", [P, P]) for k in range(2)]
        neg_max = [S.sb(f"neg_max{k}", [P, 1]) for k in range(2)]
        total = [S.sb(f"total{k}", [P, 1]) for k in range(2)]
        recip = [S.sb(f"recip{k}", [P, 1]) for k in range(2)]
        e = [S.sb(f"e{k}", [P, SEQ]) for k in range(2)]
        turned = S.sb("turned", [P, TILES, CH])
        p_s = [S.ps(f"p_s{k}", [P, SEQ]) for k in range(2)]
        p_t = [S.ps(f"p_t{k}", [P, CH]) for k in range(2)]
        p_w = S.ps("p_w", [P, CH])
        staged, s_ready, max_done, exp_done = S.sem("staged"), S.sem("s_ready"), S.sem("max_done"), S.sem("exp_done")
        recip_done, e_ready = S.sem("recip_done"), S.sem("e_ready")
        t_ready = [S.sem(f"t_ready{h}") for h in range(2)]
        t_stored = [S.sem(f"t_stored{h}") for h in range(2)]
        w_ready, w_stored = S.sem("w_ready"), S.sem("w_stored")
        with nc.Block() as block:

            @block.gpsimd
            def _(pool):
                with pool.Fori(0, 2) as g:
                    for k in range(HALF):
                        i = g * HALF + k
                        pool.wait_ge(s_ready, i - 1 if k > 1 else g * HALF)
                        pool.tensor_tensor(stat[k % 2][:, :], A[:, ds(i * P, P)], C.zeros[:, :], ALU.add
                                           ).then_inc(staged, 1)

            @block.tensor
            def _(pe):
                def scores(g, k):
                    i = g * HALF + k
                    pe.wait_ge(staged, i + 1)
                    pe.wait_ge(exp_done, i - 1 if k > 1 else g * HALF)
                    for c in range(2):
                        mm = pe.matmul(p_s[k % 2][:, c * CH:(c + 1) * CH], stat[k % 2][:, :], B[:, c * CH:(c + 1) * CH],
                                       start=True, stop=True)
                    mm.then_inc(s_ready, 1)

                def turn(g, k):
                    i = g * HALF + k
                    pe.wait_ge(e_ready, i + 1)
                    for h in range(2):
                        pe.wait_ge(t_stored[h], i)
                        for j in range(4):
                            b = (h * 4 + j) * P
                            mm = pe.transpose(p_t[h][:, j * P:(j + 1) * P], e[k % 2][:, b:b + P], C.ident[:, :])
                        mm.then_inc(t_ready[h], 1)

                with pe.Fori(0, 2) as g:
                    scores(g, 0)
                    for k in range(HALF):
                        if k + 1 < HALF:
                            scores(g, k + 1)
                        turn(g, k)
                    pe.wait_ge(w_stored, g)
                    for h in range(2):
                        pe.wait_ge(t_stored[h], (g + 1) * HALF)
                        for j in range(4):
                            t = h * 4 + j
                            mm = pe.matmul(p_w[:, :], W[:, t, :], turned[:, t, :], start=(t == 0), stop=(t == TILES - 1))
                    mm.then_inc(w_ready, 1)

            @block.scalar
            def _(act):
                with act.Fori(0, 2) as g:
                    for k in range(HALF):
                        i = g * HALF + k
                        act.wait_ge(max_done, i + 1)
                        act.wait_ge(t_ready[1], i - 1 if k > 1 else g * HALF)
                        act.activation(e[k % 2][:, :], p_s[k % 2][:, :], ACT.Exp, bias=neg_max[k % 2][:, 0:1],
                                       accum_out=total[k % 2][:, 0:1]).then_inc(exp_done, 1)
                        for h in range(1, 2):
                            act.wait_ge(t_ready[h], i + 1)
                            if k == 0:
                                act.wait_ge(w_ready, g)
                            act.copy(turned[:, h * 4:h * 4 + 4, k * P:(k + 1) * P],
                                     p_t[h][:, :].rearrange("p (t a) -> p t a", a=P)).then_inc(t_stored[h], 1)

            @block.vector
            def _(dve):
                def maximum(g, k):
                    i = g * HALF + k
                    dve.wait_ge(s_ready, i + 1)
                    dve.tensor_reduce(neg_max[k % 2][:, 0:1], p_s[k % 2][:, :], AX, ALU.max, negate=True
                                      ).then_inc(max_done, 1)

                with dve.Fori(0, 2) as g:
                    maximum(g, 0)
                    for k in range(HALF):
                        i = g * HALF + k
                        dve.wait_ge(exp_done, i + 1)
                        dve.reciprocal(recip[k % 2][:, 0:1], total[k % 2][:, 0:1]).then_inc(recip_done, 1)
                        dve.wait_ge(recip_done, i + 1)
                        dve.tensor_scalar(e[k % 2][:, :], e[k % 2][:, :], recip[k % 2][:, 0:1], factor, ALU.mult, ALU.mult
                                          ).then_inc(e_ready, 1)
                        if k + 1 < HALF:
                            maximum(g, k + 1)
                        dve.wait_ge(t_ready[0], i + 1)
                        if k == 0:
                            dve.wait_ge(w_ready, g)
                        dve.tensor_copy(turned[:, 0:4, k * P:(k + 1) * P], p_t[0][:, :].rearrange("p (t a) -> p t a", a=P)
                                        ).then_inc(t_stored[0], 1)
                    dve.wait_ge(w_ready, g + 1)
                    dve.tensor_copy(dst[:, ds(g * 8, 8), :], p_w[:, :].rearrange("p (e s) -> p e s", s=SLOT)
                                    ).then_inc(w_stored, 1)


def slot_experts(nc, C, I, name, slotsT, eout):
    K = 4
    with Stage(nc, name) as S:
        wg = [S.sb(f"wg{k}", [P, SFF]) for k in range(K)]
        wu = [S.sb(f"wu{k}", [P, SFF]) for k in range(K)]
        wd = [S.sb(f"wd{k}", [P, MSF, D]) for k in range(K)]
        b_rows = S.sb("b_rows", [2 * SE * MSF, P])
        b_cols = S.sb("b_cols", [P, 2, SE * MSF])
        bias = [S.sb(f"bias{k}", [P, 2, MSF]) for k in range(2)]
        bd = S.sb("bd", [P, ST, D])
        gate = [S.sb(f"gate{k}", [P, MSF, P]) for k in range(2)]
        hidden = [S.sb(f"hidden{k}", [P, MSF, P]) for k in range(2)]
        p_up = [S.ps(f"p_up{k}", [P, 2, MSF, P]) for k in range(2)]
        p_out = [S.ps(f"p_out{k}", [P, BATCH, CH // 2]) for k in range(2)]
        p_b = S.ps("p_b", [P, CH])
        loaded = [S.sem(f"loaded{k}") for k in range(K)]
        b_loaded, b_turned, b_stored = S.sem("b_loaded"), S.sem("b_turned"), S.sem("b_stored")
        b_set, up_ready, gate_done, hidden_done = S.sem("b_set"), S.sem("up_ready"), S.sem("gate_done"), S.sem("hidden_done")
        down_done, stored = S.sem("down_done"), S.sem("stored")
        with nc.Block() as block:

            @block.sync
            def _(sp):
                def fetch(e, k):
                    sp.dma_start(wg[k][:, :], I["L3_ffn_Wg"][ds(e, 1)].rearrange("e d f -> d (e f)")).then_inc(loaded[k], 16)
                    sp.dma_start(wu[k][:, :], I["L3_ffn_Wu"][ds(e, 1)].rearrange("e d f -> d (e f)")).then_inc(loaded[k], 16)
                    sp.dma_start(wd[k][:, :, :], I["L3_ffn_Wd"][ds(e, 1)].rearrange("e (m p) d -> p (e m) d", p=P)
                                 ).then_inc(loaded[k], 16)

                sp.dma_start(b_rows[0:SE * MSF, :], I["L3_ffn_bg"].rearrange("e (m p) -> (e m) p", p=P)).then_inc(b_loaded, 16)
                sp.dma_start(b_rows[SE * MSF:, :], I["L3_ffn_bu"].rearrange("e (m p) -> (e m) p", p=P)).then_inc(b_loaded, 16)
                for h in range(2):
                    sp.dma_start(bd[h * SLOT:(h + 1) * SLOT, :, :],
                                 I["L3_ffn_bd"].rearrange("(t h) d -> h t d", h=2)[h].partition_broadcast(SLOT)
                                 ).then_inc(b_loaded, 16)
                for k in range(K):
                    fetch(k, k)
                with sp.Fori(0, SE // K - 1) as i:
                    for k in range(K):
                        sp.wait_ge(down_done, i * K + k + 1)
                        fetch(i * K + K + k, k)

            @block.tensor
            def _(pe):
                def up(i, k):
                    e = i * K + k
                    pe.wait_ge(loaded[k], i * 48 + 48)
                    pe.wait_ge(hidden_done, e - 1 if k > 1 else i * K)
                    for j, w in enumerate((wg, wu)):
                        for m in range(MSF):
                            mm = pe.matmul(p_up[k % 2][:, j, m, :], w[k][:, m * P:(m + 1) * P], slotsT[:, ds(e, 1), :, :],
                                           start=True, stop=True)
                    mm.then_inc(up_ready, 1)

                def down(i, k):
                    pe.wait_ge(hidden_done, i * K + k + 1)
                    if k % 2 == 0:
                        pe.wait_ge(stored, i * 2 + k // 2 - 1 if k // 2 > 1 else i * 2)
                    h = slice(k % 2 * SLOT, (k % 2 + 1) * SLOT)
                    for b in range(BATCH):
                        for m in range(MSF):
                            mm = pe.matmul(p_out[k // 2][h, b, 0:D], hidden[k % 2][:, m, b * SLOT:(b + 1) * SLOT],
                                           wd[k][:, m, :], start=(m == 0), stop=(m == MSF - 1),
                                           tile_position=(0, k % 2 * SLOT))
                    mm.then_inc(down_done, 1)

                pe.wait_ge(b_loaded, 64)
                pe.transpose(p_b[:, 0:2 * SE * MSF], b_rows[:, :], C.ident[0:2 * SE * MSF, 0:2 * SE * MSF]
                             ).then_inc(b_turned, 1)
                with pe.Fori(0, SE // K) as i:
                    up(i, 0)
                    for k in range(K):
                        if k + 1 < K:
                            up(i, k + 1)
                        down(i, k)

            @block.scalar
            def _(act):
                with act.Fori(0, SE // K) as i:
                    for k in range(K):
                        e = i * K + k
                        act.wait_ge(b_set, e + 1)
                        act.wait_ge(up_ready, e + 1)
                        for m in range(MSF):
                            ins = act.activation(gate[k % 2][:, m, :], p_up[k % 2][:, 0, m, :], ACT.Gelu,
                                                 bias=bias[k % 2][:, 0, m:m + 1])
                        ins.then_inc(gate_done, 1)

            @block.vector
            def _(dve):
                dve.wait_ge(b_turned, 1)
                dve.tensor_copy(b_cols[:, :, :], p_b[:, 0:2 * SE * MSF].rearrange("p (j c) -> p j c", j=2)
                                ).then_inc(b_stored, 1)
                dve.wait_ge(b_stored, 1)
                with dve.Fori(0, SE // K) as i:
                    def set_bias(k):
                        e = i * K + k
                        dve.wait_ge(hidden_done, e - 1 if k > 1 else i * K)
                        dve.tensor_copy(bias[k % 2][:, :, :], b_cols[:, :, ds(e * MSF, MSF)]).then_inc(b_set, 1)

                    set_bias(0)
                    for k in range(K):
                        e = i * K + k
                        if k + 1 < K:
                            set_bias(k + 1)
                        dve.wait_ge(gate_done, e + 1)
                        dve.wait_ge(b_set, e + 1)
                        dve.wait_ge(down_done, e - 1 if k > 1 else i * K)
                        for m in range(MSF):
                            ins = dve.scalar_tensor_tensor(out=hidden[k % 2][:, m, :], in0=p_up[k % 2][:, 1, m, :],
                                                           scalar=bias[k % 2][:, 1, m:m + 1], in1=gate[k % 2][:, m, :],
                                                           op0=ALU.add, op1=ALU.mult)
                        ins.then_inc(hidden_done, 1)
                        if k % 2:
                            dve.wait_ge(down_done, e + 1)
                            t = i * 2 + k // 2
                            for b in range(BATCH):
                                ins = dve.tensor_tensor(eout[:, b, ds(t, 1), :], p_out[k // 2][:, b, 0:D].unsqueeze(1), bd[:, ds(t, 1), :],
                                                        ALU.add)
                            ins.then_inc(stored, 1)


def build_program(nc, I, out):
    with ExitStack() as stack:
        class C:
            pass

        def sb(name, shape, dt=F32):
            return stack.enter_context(nc.sbuf_tensor(name, shape, dt))

        C.ident = sb("ident", [P, P])
        C.ones = sb("ones", [P, P])
        C.zeros = sb("zeros", [P, P])
        C.half = sb("half", [P, NT])
        C.neg_half = sb("neg_half", [P, NT])
        C.rms_eps = sb("rms_eps", [P, NT])
        C.neg_one = sb("neg_one", [P, NT])
        X = sb("X", [P, NT, D])
        xn = sb("xn", [P, NT, D])
        xnT = sb("xnT", [P, TOK])
        constants(nc, C)
        load_inputs(nc, I, X)

        def layer_norm(name):
            normalise(nc, C, name, X, xn, xnT)

        with Stage(nc, "ffn0") as S:
            up, down = S.sb("up", [P, DFF]), S.sb("down", [P, MFF, D])
            b1, b2 = S.sb("b1", [P, MFF]), S.sb("b2", [1, D])
            ternary_weights(nc, C, "ffn0_w", I["L0_ffn_W1"], I["L0_ffn_W2"], 1e-8, up, down)
            load(nc, "ffn0_b", [(b1[:, :], I["L0_ffn_b1"].rearrange("(m p) -> p m", p=P)),
                                (b2[:, :], I["L0_ffn_b2"].unsqueeze(0))])
            layer_norm("ln0a")
            ffn(nc, C, "ffn0a", X, xnT, up, down, b1, b2[0:1, :])
            layer_norm("ln0b")
            gated_scan_mixer(nc, C, I, X, xn, xnT)
            layer_norm("ln0c")
            ffn(nc, C, "ffn0b", X, xnT, up, down, b1, b2[0:1, :])
        layer_norm("ln1a")
        moe_ffn(nc, C, I, "moe_a", X, xnT)
        layer_norm("ln1b")
        stacked_attention_mixer(nc, C, I, X, xn, xnT)
        layer_norm("ln1c")
        moe_ffn(nc, C, I, "moe_b", X, xnT)
        with Stage(nc, "ffn2") as S:
            up, down = S.sb("up", [P, DFF]), S.sb("down", [P, MFF, D])
            ternary_weights(nc, C, "ffn2_w", I["L2_ffn_w_up"], I["L2_ffn_w_down"], 0.0, up, down)
            layer_norm("ln2a")
            normalise(nc, C, "ln2a_rms", xn, xn, xnT, kind="rms")
            ffn(nc, C, "ffn2a", X, xnT, up, down, rms=True)
            layer_norm("ln2b")
            alibi_attention_mixer(nc, C, I, X, xn, xnT)
            layer_norm("ln2c")
            normalise(nc, C, "ln2c_rms", xn, xn, xnT, kind="rms")
            ffn(nc, C, "ffn2b", X, xnT, up, down, rms=True)
        with Stage(nc, "ffn3") as S:
            seT = S.sb("seT", [P, NSLOT])
            slot_directions(nc, C, I, seT)
            layer_norm("ln3a")
            soft_moe_ffn(nc, C, I, "ffn3a", X, xn, xnT, seT)
            layer_norm("ln3b")
            resonant_mixer(nc, C, I, X, xn)
            layer_norm("ln3c")
            soft_moe_ffn(nc, C, I, "ffn3b", X, xn, xnT, seT)
        store_outputs(nc, X, out)


def load(nc, name, pairs):
    with Stage(nc, name) as S:
        loaded = S.sem("loaded")
        with nc.Block() as block:

            @block.sync
            def _(sp):
                for dst, src in pairs:
                    sp.dma_start(dst, src, allow_slow_non_contiguous=True).then_inc(loaded, 16)
                sp.wait_ge(loaded, 16 * len(pairs))


def load_inputs(nc, I, X):
    load(nc, "load_x", [(X[:, b * TPB:(b + 1) * TPB, :], I["L0_attn_x"][b].rearrange("(t p) d -> p t d", p=P))
                        for b in range(BATCH)])


def store_outputs(nc, X, out):
    with Stage(nc, "store_x") as S:
        stored = S.sem("stored")
        with nc.Block() as block:

            @block.sync
            def _(sp):
                for b in range(BATCH):
                    sp.dma_start(out[b].rearrange("(t p) d -> p t d", p=P),
                                 X[:, b * TPB:(b + 1) * TPB, :]).then_inc(stored, 16)
                sp.wait_ge(stored, 16 * BATCH)


_INS = ['L0_attn_x', 'L0_attn_Wq', 'L0_attn_Wk', 'L0_attn_Wv', 'L0_attn_Wf', 'L0_attn_bf', 'L0_attn_Wg',
        'L0_attn_Wout', 'L0_attn_gamma', 'L0_attn_beta', 'L0_ffn_W1', 'L0_ffn_b1', 'L0_ffn_W2', 'L0_ffn_b2',
        'L1_attn_W_attn', 'L1_attn_b_attn', 'L1_attn_W_k2', 'L1_attn_b_k2', 'L1_attn_W_proj', 'L1_attn_b_proj',
        'L1_ffn_Wr', 'L1_ffn_br', 'L1_ffn_W1', 'L1_ffn_b1', 'L1_ffn_W2', 'L1_ffn_b2', 'L2_attn_ln_gamma',
        'L2_attn_ln_beta', 'L2_attn_Wq', 'L2_attn_Wk', 'L2_attn_Wv', 'L2_attn_Wo', 'L2_ffn_w_up', 'L2_ffn_w_down',
        'L3_attn_lmlg', 'L3_attn_theta', 'L3_attn_last_conv_init', 'L3_ffn_norm_g', 'L3_ffn_norm_b',
        'L3_ffn_slot_g', 'L3_ffn_slot_b', 'L3_ffn_scale', 'L3_ffn_slot_embeds', 'L3_ffn_Wg', 'L3_ffn_bg',
        'L3_ffn_Wu', 'L3_ffn_bu', 'L3_ffn_Wd', 'L3_ffn_bd']


def kernel(**inputs):
    import numpy as _np
    import concourse.bacc as _bacc
    from concourse import mybir as _mybir
    from concourse.bass_utils import run_bass_kernel_spmd as _run

    nc = _bacc.Bacc("TRN2", target_bir_lowering=False, num_devices=1)
    arrays, ins = {}, {}
    for name in _INS:
        a = _np.ascontiguousarray(inputs[name])
        arrays[f"in_{name}_dram"] = a
        ins[name] = nc.dram_tensor(f"in_{name}_dram", a.shape, _mybir.dt.from_np(a.dtype), kind="ExternalInput").ap()
    out = nc.dram_tensor("out_0_dram", (BATCH, SEQ, D), _mybir.dt.float32, kind="ExternalOutput").ap()
    build_program(nc, ins, out)
    r = _run(nc, [arrays], core_ids=[0])
    return r.results[0]["out_0_dram"]
```

```python
from contextlib import ExitStack

import numpy as np

import concourse.bass as bass
from concourse import mybir

F32 = mybir.dt.float32
F32R = mybir.dt.float32r
BF16 = mybir.dt.bfloat16
ALU = mybir.AluOpType
ACT = mybir.ActivationFunctionType
AX = mybir.AxisListType.X

P = 128
D = 128
BATCH, SEQ = 2, 1024
TOK = BATCH * SEQ
NT = TOK // P
TPB = SEQ // P
CH = 512
NCH = TOK // CH
TPC = CH // P
DFF = 4 * D
MFF = DFF // P
LN_EPS = 1e-5
RMS_EPS = 1e-8
BIG = 1.0e30
ds = bass.ds


class Stage:

    def __init__(self, nc, name):
        self.nc, self.name, self.stack, self.sems = nc, name, ExitStack(), []

    def __enter__(self):
        return self

    def __exit__(self, *err):
        self.stack.close()
        if self.sems:
            self.nc.clear_and_free_semaphores(self.sems)
            self.nc.all_engine_barrier()

    def sb(self, name, shape, dt=F32):
        return self.stack.enter_context(self.nc.sbuf_tensor(f"{self.name}_{name}", shape, dt))

    def ps(self, name, shape, dt=F32):
        return self.stack.enter_context(self.nc.psum_tensor(f"{self.name}_{name}", shape, dt))

    def sem(self, name):
        self.sems.append(self.nc.alloc_semaphore(name=f"{self.name}_{name}"))
        return self.sems[-1]


class Chain:

    def __init__(self, eng, sem, first=0):
        self.eng, self.sem, self.first, self.n = eng, sem, first, 0

    def step(self, ins):
        ins.then_inc(self.sem, 1)
        self.n += 1
        self.eng.wait_ge(self.sem, self.first + self.n)


class Count:

    def __init__(self, i, times, plus):
        self.i, self.times, self.plus = i, times, plus

    def __mul__(self, n):
        return Count(self.i, self.times * n, self.plus * n)

    def __add__(self, n):
        return Count(self.i, self.times, self.plus + n)

    def __sub__(self, n):
        return self + -n

    def value(self):
        return self.i * self.times + self.plus


def at_turn(value):
    return value.value() if isinstance(value, Count) else value


def wait(eng, sem, value):
    if not (isinstance(value, int) and value <= 0):
        eng.wait_ge(sem, at_turn(value))


def per_token(col, width):
    n = col.shape[1]
    return col.unsqueeze(2).to_broadcast([P, n, width])


def per_feature(row, tiles):
    return row.unsqueeze(1).to_broadcast([P, tiles, row.shape[1]])


def constants(nc, C):
    with Stage(nc, "const") as S:
        made = S.sem("made")
        with nc.Block() as block:

            @block.gpsimd
            def _(pool):
                chain = Chain(pool, made)
                chain.step(pool.memset(C.ident[:, :], 0.0))
                chain.step(pool.affine_select(out=C.ident[:, :], in_=C.ident[:, :], compare_op=ALU.not_equal,
                                              fill=1.0, base=0, pattern=[[-1, P]], channel_multiplier=1))
                pool.memset(C.ones[:, :], 1.0)
                pool.memset(C.zeros[:, :], 0.0)
                pool.memset(C.rms_eps[:, :], RMS_EPS)
                pool.memset(C.neg_half[:, :], -0.5)
                pool.memset(C.half[:, :], 0.5)
                chain.step(pool.memset(C.neg_one[:, :], -1.0))


def normalise(nc, C, name, src, dst, dstT=None, kind="layer", gamma=None, beta=None, tiles=NT):
    G = 4
    TG = tiles // G
    with Stage(nc, name) as S:
        sums = S.sb("sums", [P, tiles])
        neg_mean = S.sb("neg_mean", [P, tiles])
        square = S.sb("square", [P, tiles, D])
        sumsq = S.sb("sumsq", [P, tiles])
        var = S.sb("var", [P, tiles])
        root = S.sb("root", [P, tiles])
        rstd = S.sb("rstd", [P, tiles])
        turned = S.ps("turned", [P, G, CH])
        own = S.sem("own")
        centred = S.sem("centred")
        squared = S.sem("squared")
        summed = S.sem("summed")
        own_pool = S.sem("own_pool")
        scaled = S.sem("scaled")
        normed = S.sem("normed")
        turned_ok = S.sem("turned_ok")
        stored = S.sem("stored")
        with nc.Block() as block:

            @block.vector
            def _(dve):
                chain = Chain(dve, own)
                for g in range(G):
                    t = slice(g * TG, (g + 1) * TG)
                    if kind == "layer":
                        chain.step(dve.tensor_reduce(sums[:, t], src[:, t, :], AX, ALU.add))
                        dve.tensor_scalar(neg_mean[:, t], sums[:, t], -1.0 / D, None, ALU.mult).then_inc(centred, 1)
                if kind == "rms":
                    for g in range(G):
                        t = slice(g * TG, (g + 1) * TG)
                        dve.wait_ge(squared, g + 1)
                        dve.tensor_reduce(sumsq[:, t], square[:, t, :], AX, ALU.add).then_inc(summed, 1)
                for g in range(G):
                    t = slice(g * TG, (g + 1) * TG)
                    dve.wait_ge(scaled, g + 1)
                    if kind == "layer":
                        dve.wait_ge(centred, g + 1)
                    if kind == "layer":
                        for n in range(g * TG, (g + 1) * TG):
                            last = dve.tensor_scalar(dst[:, n, :], src[:, n, :], neg_mean[:, n:n + 1], rstd[:, n:n + 1],
                                                     ALU.add, ALU.mult)
                    else:
                        last = dve.tensor_tensor(dst[:, t, :], src[:, t, :], per_token(rstd[:, t], D), ALU.mult)
                    if gamma is not None:
                        chain.step(last)
                        chain.step(dve.tensor_tensor(dst[:, t, :], dst[:, t, :], per_feature(gamma, TG), ALU.mult))
                        last = dve.tensor_tensor(dst[:, t, :], dst[:, t, :], per_feature(beta, TG), ALU.add)
                    last.then_inc(normed, 1)

            @block.scalar
            def _(act):
                for g in range(G):
                    if kind == "layer":
                        act.wait_ge(centred, g + 1)
                        for n in range(g * TG, (g + 1) * TG):
                            ins = act.activation(square[:, n, :], src[:, n, :], ACT.Square, bias=neg_mean[:, n:n + 1],
                                                 accum_out=sumsq[:, n:n + 1])
                        ins.then_inc(summed, 1)
                    else:
                        t = slice(g * TG, (g + 1) * TG)
                        act.activation(square[:, t, :], src[:, t, :], ACT.Square).then_inc(squared, 1)
                if dstT is not None:
                    for g in range(G):
                        act.wait_ge(turned_ok, g + 1)
                        act.copy(dstT[:, g * TG * P:(g + 1) * TG * P], turned[:, g, 0:TG * P]).then_inc(stored, 1)

            @block.gpsimd
            def _(pool):
                chain = Chain(pool, own_pool)
                for g in range(G):
                    t = slice(g * TG, (g + 1) * TG)
                    pool.wait_ge(summed, g + 1)
                    if kind == "layer":
                        chain.step(pool.tensor_scalar(var[:, t], sumsq[:, t], 1.0 / D, LN_EPS, ALU.mult, ALU.add))
                        pool.tensor_tensor(rstd[:, t], var[:, t], C.neg_half[:, 0:TG], ALU.pow).then_inc(scaled, 1)
                    else:
                        chain.step(pool.tensor_scalar(var[:, t], sumsq[:, t], 1.0 / D, None, ALU.mult))
                        chain.step(pool.tensor_tensor(root[:, t], var[:, t], C.half[:, 0:TG], ALU.pow))
                        chain.step(pool.tensor_scalar(var[:, t], root[:, t], RMS_EPS, None, ALU.add))
                        pool.tensor_tensor(rstd[:, t], var[:, t], C.neg_one[:, 0:TG], ALU.pow).then_inc(scaled, 1)

            if dstT is not None:
                @block.tensor
                def _(pe):
                    for g in range(G):
                        pe.wait_ge(normed, g + 1)
                        for k in range(TG):
                            mm = pe.transpose(turned[:, g, k * P:(k + 1) * P], dst[:, g * TG + k, :], C.ident[:, :])
                        mm.then_inc(turned_ok, 1)


def ternary_weights(nc, C, name, W1, W2, floor, up, down):
    with Stage(nc, name) as S:
        raw = S.sb("raw", [P, 2, DFF])
        sign = S.sb("sign", [P, 2, DFF])
        below = S.sb("below", [P, 2, DFF])
        rows = S.sb("rows", [P, 2])
        cut = S.sb("cut", [P, 2])
        neg_cut = S.sb("neg_cut", [P, 2])
        total = S.ps("total", [P, CH])
        turned = S.ps("turned", [P, 2, DFF])
        loaded = S.sem("loaded")
        own = S.sem("own")
        summed = S.sem("summed")
        totalled = S.sem("totalled")
        turned_ok = S.sem("turned_ok")
        with nc.Block() as block:

            @block.sync
            def _(sp):
                sp.dma_start(raw[:, 0, :].rearrange("p (m d) -> p m d", m=MFF),
                             W1.rearrange("(m p) d -> p m d", p=P)).then_inc(loaded, 16)
                sp.dma_start(raw[:, 1, :], W2).then_inc(loaded, 16)

            @block.vector
            def _(dve):
                chain = Chain(dve, own)
                dve.wait_ge(loaded, 32)
                for w in range(2):
                    dve.tensor_reduce(rows[:, w:w + 1], raw[:, w, :], AX, ALU.add,
                                      apply_absolute_value=True).then_inc(summed, 1)
                dve.wait_ge(totalled, 1)
                chain.step(dve.tensor_scalar(cut[:, :], total[:, 0:2], 1.0 / (D * DFF), floor, ALU.mult, ALU.max))
                chain.step(dve.tensor_scalar(cut[:, :], cut[:, :], 0.5, None, ALU.mult))
                chain.step(dve.tensor_scalar(neg_cut[:, :], cut[:, :], -1.0, None, ALU.mult))
                for w in range(2):
                    dve.tensor_scalar(below[:, w, :], raw[:, w, :], neg_cut[:, w:w + 1], None, ALU.is_lt)
                    chain.step(dve.tensor_scalar(sign[:, w, :], raw[:, w, :], cut[:, w:w + 1], None, ALU.is_gt))
                    chain.step(dve.tensor_tensor(sign[:, w, :], sign[:, w, :], below[:, w, :], ALU.subtract))
                dve.wait_ge(turned_ok, 1)
                dve.tensor_copy(up[:, :], turned[:, 0, :])
                dve.tensor_copy(down[:, :, :], turned[:, 1, :].rearrange("p (m d) -> p m d", m=MFF))

            @block.tensor
            def _(pe):
                pe.wait_ge(summed, 2)
                pe.matmul(total[:, 0:2], C.ones[:, :], rows[:, :], start=True, stop=True).then_inc(totalled, 1)
                pe.wait_ge(own, 7)
                for w in range(2):
                    for m in range(MFF):
                        mm = pe.transpose(turned[:, w, m * P:(m + 1) * P], sign[:, w, m * P:(m + 1) * P], C.ident[:, :])
                mm.then_inc(turned_ok, 1)


def ffn(nc, C, name, X, xnT, up, down, b1=None, b2=None, rms=False):
    with Stage(nc, name) as S:
        hidden = [S.sb(f"hidden{k}", [P, MFF, CH]) for k in range(2)]
        square = [S.sb(f"square{k}", [P, MFF, CH]) for k in range(2)] if rms else None
        hidden_out = S.sb("hidden_out", [P, 2, TPC, D]) if rms else None
        mean_sq = S.sb("mean_sq", [P, 2, TPC])
        root = S.sb("root", [P, 2, TPC])
        scale = S.sb("scale", [P, 2, TPC])
        p_up = S.ps("p_up", [P, MFF, CH])
        p_down = S.ps("p_down", [P, 2, CH])
        p_sq = S.ps("p_sq", [P, 2, CH]) if rms else None
        up_ready = S.sem("up_ready")
        gelu_done = S.sem("gelu_done")
        square_done = S.sem("square_done")
        down_ready = S.sem("down_ready")
        sums_ready = S.sem("sums_ready")
        scale_ready = S.sem("scale_ready")
        own_pool = S.sem("own_pool")
        copied = S.sem("copied")
        added = S.sem("added")
        with nc.Block() as block:

            @block.tensor
            def _(pe):
                with pe.Fori(0, NCH // 2) as i:
                    for k in range(2):
                        for m in range(MFF):
                            if k:
                                pe.wait_ge(gelu_done, i * 2 * MFF + m + 1)
                            else:
                                pe.wait_ge(gelu_done, i * 2 * MFF)
                            pe.matmul(p_up[:, m, :], up[:, m * P:(m + 1) * P], xnT[:, ds((i * 2 + k) * CH, CH)],
                                      start=True, stop=True).then_inc(up_ready, 1)
                    for k in range(2):
                        pe.wait_ge(gelu_done, i * 2 * MFF + (k + 1) * MFF)
                        pe.wait_ge(added, i * 2)
                        for t in range(TPC):
                            if b2 is not None:
                                pe.matmul(p_down[:, k, t * D:(t + 1) * D], C.ones[0:1, :], b2, start=True, stop=False)
                            for m in range(MFF):
                                mm = pe.matmul(p_down[:, k, t * D:(t + 1) * D], hidden[k][:, m, t * P:(t + 1) * P],
                                               down[:, m, :], start=(m == 0 and b2 is None), stop=(m == MFF - 1))
                        mm.then_inc(down_ready, 1)
                        if rms:
                            pe.wait_ge(square_done, i * 2 + k + 1)
                            for t in range(TPC):
                                for m in range(MFF):
                                    mm = pe.matmul(p_sq[:, k, t:t + 1], square[k][:, m, t * P:(t + 1) * P],
                                                   C.ones[:, 0:1], start=(m == 0), stop=(m == MFF - 1))
                            mm.then_inc(sums_ready, 1)

            @block.scalar
            def _(act):
                with act.Fori(0, NCH // 2) as i:
                    for k in range(2):
                        act.wait_ge(down_ready, i * 2)
                        for m in range(MFF):
                            act.wait_ge(up_ready, i * 2 * MFF + k * MFF + m + 1)
                            bias = b1[:, m:m + 1] if b1 is not None else 0.0
                            act.activation(hidden[k][:, m, :], p_up[:, m, :], ACT.Gelu, bias=bias).then_inc(gelu_done, 1)

                        if rms:
                            act.wait_ge(gelu_done, i * 2 * MFF + (k + 1) * MFF)
                            act.wait_ge(sums_ready, i * 2)
                            act.activation(square[k][:, :, :], hidden[k][:, :, :], ACT.Square).then_inc(square_done, 1)

            if rms:
                @block.gpsimd
                def _(pool):
                    with pool.Fori(0, NCH // 2) as i:
                        for k in range(2):
                            chain = Chain(pool, own_pool, i * 4 + k * 2)
                            pool.wait_ge(copied, i * 2 + k + 1)
                            chain.step(pool.tensor_tensor(root[:, k, :], mean_sq[:, k, :], C.half[:, 0:TPC], ALU.pow))
                            chain.step(pool.tensor_tensor(root[:, k, :], root[:, k, :], C.rms_eps[:, 0:TPC], ALU.add))
                            pool.wait_ge(added, i * 2)
                            pool.tensor_tensor(scale[:, k, :], root[:, k, :], C.neg_one[:, 0:TPC],
                                               ALU.pow).then_inc(scale_ready, 1)

            @block.vector
            def _(dve):
                with dve.Fori(0, NCH // 2) as i:
                    for k in range(2):
                        tiles = ds((i * 2 + k) * TPC, TPC)
                        if rms:
                            dve.wait_ge(sums_ready, i * 2 + k + 1)
                            dve.tensor_scalar(mean_sq[:, k, :], p_sq[:, k, 0:TPC], 1.0 / DFF, None,
                                              ALU.mult).then_inc(copied, 1)
                    for k in range(2):
                        dve.wait_ge(down_ready, i * 2 + k + 1)
                        if not rms:
                            tiles = ds((i * 2 + k) * TPC, TPC)
                            dve.scalar_tensor_tensor(
                                out=X[:, tiles, :], in0=p_down[:, k, :].rearrange("p (t d) -> p t d", d=D), scalar=0.5,
                                in1=X[:, tiles, :], op0=ALU.mult, op1=ALU.add).then_inc(added, 1)
                        else:
                            dve.wait_ge(scale_ready, i * 2 + k + 1)
                            for t in range(TPC):
                                row = ds((i * 2 + k) * TPC + t, 1)
                                last = dve.tensor_scalar(hidden_out[:, k, t, :], p_down[:, k, t * D:(t + 1) * D],
                                                         scale[:, k, t:t + 1], 0.5, ALU.mult, ALU.mult)
                            last.then_inc(added, 1)
                            dve.wait_ge(added, i * 2 + k + 1)
                            tiles = ds((i * 2 + k) * TPC, TPC)
                            dve.tensor_tensor(X[:, tiles, :], X[:, tiles, :], hidden_out[:, k, :, :], ALU.add)



H, HD = 16, 8


def gated_scan_mixer(nc, C, I, X, xn, xnT):
    with Stage(nc, "mix0") as M:
        mixed = M.sb("mixed", [P, NT, D])
        gamma = M.sb("gamma", [P, D])
        beta = M.sb("beta", [P, D])
        Wg = M.sb("Wg", [P, D])
        Wout = M.sb("Wout", [P, D])
        with Stage(nc, "scan") as S:
            W = {n: S.sb(n, [P, D]) for n in ("Wq", "Wk", "Wv", "Wf")}
            bf = S.sb("bf", [P, 1])
            load(nc, "mix0_load", [(W[n][:, :], I[f"L0_attn_{n}"]) for n in W] + [
                (Wg[:, :], I["L0_attn_Wg"]), (Wout[:, :], I["L0_attn_Wout"]), (bf[:, :], I["L0_attn_bf"].unsqueeze(1)),
                (gamma[:, :], I["L0_attn_gamma"].partition_broadcast(P)),
                (beta[:, :], I["L0_attn_beta"].partition_broadcast(P))])
            krep_w = S.sb("krep_w", [P, HD, D])
            qrep_w = S.sb("qrep_w", [P, HD, D])
            with nc.Block() as block:

                @block.vector
                def _(dve):
                    for j in range(HD):
                        for rep, w in ((krep_w, W["Wk"]), (qrep_w, W["Wq"])):
                            dve.tensor_copy(rep[:, j, :].rearrange("p (h i) -> p h i", i=HD),
                                            w[:, j:D:HD].unsqueeze(2).to_broadcast([P, H, HD]))

            scan_over_tokens(nc, C, S, W, bf, krep_w, qrep_w, xnT, mixed)
        normalise(nc, C, "mix0_norm", mixed, mixed, gamma=gamma[:, :], beta=beta[:, :])
        gate_and_project(nc, C, X, xnT, mixed, Wg, Wout)


def scan_over_tokens(nc, C, S, W, bf, krep_w, qrep_w, xnT, mixed):
    vT = S.sb("vT", [P, SEQ])
    gT = S.sb("gT", [P, SEQ])
    vk = S.sb("vk", [P, SEQ])
    state = S.sb("state", [P, SEQ])
    sq = [S.sb(f"sq{k}", [P, SEQ]) for k in range(2)]
    p_k = [S.ps(f"p_k{k}", [P, SEQ]) for k in range(2)]
    p_q = S.ps("p_q", [P, SEQ])
    p_out = S.ps("p_out", [P, SEQ])
    v_ready, f_ready = S.sem("v_ready"), S.sem("f_ready")
    v_stored, g_stored = S.sem("v_stored"), S.sem("g_stored")
    k_ready, q_ready = S.sem("k_ready"), S.sem("q_ready")
    vk_done = S.sem("vk_done")
    sq_done = S.sem("sq_done")
    summed = S.sem("summed")
    out_stored = S.sem("out_stored")
    own = S.sem("own")
    with nc.Block() as block:

        @block.tensor
        def _(pe):
            with pe.Fori(0, BATCH) as b:
                def product(dst, w):
                    for c in range(SEQ // CH):
                        mm = pe.matmul(dst[:, c * CH:(c + 1) * CH], w, xnT[:, ds(b * SEQ + c * CH, CH)],
                                       start=True, stop=True)
                    return mm

                def k_of(j):
                    if j == 0:
                        pe.wait_ge(v_stored, b + 1)
                    else:
                        pe.wait_ge(vk_done, b * HD + j - 1)
                    product(p_k[j % 2], krep_w[:, j, :]).then_inc(k_ready, 1)

                def q_of(j):
                    if j == 0:
                        pe.wait_ge(g_stored, b + 1)
                    else:
                        pe.wait_ge(sq_done, b * HD + j)
                    product(p_q, qrep_w[:, j, :]).then_inc(q_ready, 1)

                pe.wait_ge(sq_done, b * HD)
                product(p_k[0], W["Wv"][:, :]).then_inc(v_ready, 1)
                product(p_q, W["Wf"][:, :]).then_inc(f_ready, 1)
                k_of(0)
                q_of(0)
                for j in range(HD):
                    if j + 1 < HD:
                        k_of(j + 1)
                        q_of(j + 1)
                    if j == 0:
                        pe.wait_ge(out_stored, b)
                    pe.wait_ge(sq_done, b * HD + j + 1)
                    for t in range(TPB):
                        mm = pe.matmul(p_out[:, t * D:(t + 1) * D], sq[j % 2][:, t * P:(t + 1) * P], C.ident[:, :],
                                       start=(j == 0 and t % TPC == 0), stop=(j == HD - 1), skip_group_check=True)
                    mm.then_inc(summed, 1)

        @block.scalar
        def _(act):
            with act.Fori(0, BATCH) as b:
                act.wait_ge(vk_done, b * HD)
                act.wait_ge(v_ready, b + 1)
                act.copy(vT[:, :], p_k[0][:, :]).then_inc(v_stored, 1)
                act.wait_ge(f_ready, b + 1)
                act.activation(gT[:, :], p_q[:, :], ACT.Sigmoid, bias=bf[:, 0:1]).then_inc(g_stored, 1)
                act.wait_ge(summed, (b + 1) * HD)
                act.copy(mixed[:, ds(b * TPB, TPB), :], p_out[:, :].rearrange("p (t d) -> p t d", d=D)
                         ).then_inc(out_stored, 1)

        @block.vector
        def _(dve):
            with dve.Fori(0, BATCH) as b:
                chain = Chain(dve, own, b * HD * 2)
                dve.wait_ge(v_stored, b + 1)
                dve.wait_ge(g_stored, b + 1)
                for j in range(HD):
                    dve.wait_ge(k_ready, b * HD + j + 1)
                    dve.tensor_tensor(vk[:, :], vT[:, :], p_k[j % 2][:, :], ALU.mult).then_inc(vk_done, 1)
                    dve.wait_ge(vk_done, b * HD + j + 1)
                    dve.tensor_tensor_scan(state[:, :], gT[:, :], vk[:, :], 0.0, ALU.mult, ALU.add).then_inc(own, 1)
                    dve.wait_ge(own, b * HD + j + 1)
                    dve.wait_ge(q_ready, b * HD + j + 1)
                    if j >= 2:
                        dve.wait_ge(summed, b * HD + j - 1)
                    else:
                        dve.wait_ge(summed, b * HD)
                    dve.tensor_tensor(sq[j % 2][:, :], state[:, :], p_q[:, :], ALU.mult).then_inc(sq_done, 1)


def gate_and_project(nc, C, X, xnT, mixed, Wg, Wout):
    G = NT // TPC
    with Stage(nc, "gate") as S:
        gate = S.sb("gate", [P, NT, D])
        gated = S.sb("gated", [P, NT, D])
        gatedT = S.sb("gatedT", [P, TOK])
        p_gate = S.ps("p_gate", [P, 2, CH])
        p_turn = S.ps("p_turn", [P, 2, CH])
        p_proj = S.ps("p_proj", [P, 2, CH])
        gate_ready, gate_done = S.sem("gate_ready"), S.sem("gate_done")
        gated_done, turned, turned_stored = S.sem("gated_done"), S.sem("turned"), S.sem("turned_stored")
        projected, added = S.sem("projected"), S.sem("added")
        with nc.Block() as block:

            @block.tensor
            def _(pe):
                def gates(g):
                    if g >= 2:
                        pe.wait_ge(gate_done, g - 1)
                    for k in range(TPC):
                        t = g * TPC + k
                        mm = pe.matmul(p_gate[:, g % 2, k * D:(k + 1) * D], xnT[:, t * P:(t + 1) * P], Wg[:, :],
                                       start=True, stop=True)
                    mm.then_inc(gate_ready, 1)

                gates(0)
                for g in range(G):
                    if g + 1 < G:
                        gates(g + 1)
                    pe.wait_ge(gated_done, g + 1)
                    if g >= 2:
                        pe.wait_ge(turned_stored, g - 1)
                    for k in range(TPC):
                        mm = pe.transpose(p_turn[:, g % 2, k * P:(k + 1) * P], gated[:, g * TPC + k, :], C.ident[:, :])
                    mm.then_inc(turned, 1)
                    pe.wait_ge(turned_stored, g + 1)
                    if g >= 2:
                        pe.wait_ge(added, g - 1)
                    for k in range(TPC):
                        t = g * TPC + k
                        mm = pe.matmul(p_proj[:, g % 2, k * D:(k + 1) * D], gatedT[:, t * P:(t + 1) * P], Wout[:, :],
                                       start=True, stop=True)
                    mm.then_inc(projected, 1)

            @block.scalar
            def _(act):
                for g in range(G):
                    act.wait_ge(gate_ready, g + 1)
                    act.activation(gate[:, g * TPC:(g + 1) * TPC, :],
                                   p_gate[:, g % 2, :].rearrange("p (t d) -> p t d", d=D), ACT.Silu).then_inc(gate_done, 1)
                    act.wait_ge(turned, g + 1)
                    act.copy(gatedT[:, g * CH:(g + 1) * CH], p_turn[:, g % 2, :]).then_inc(turned_stored, 1)

            @block.vector
            def _(dve):
                for g in range(G):
                    t = slice(g * TPC, (g + 1) * TPC)
                    dve.wait_ge(gate_done, g + 1)
                    dve.tensor_tensor(gated[:, t, :], gate[:, t, :], mixed[:, t, :], ALU.mult).then_inc(gated_done, 1)
                    dve.wait_ge(projected, g + 1)
                    dve.tensor_tensor(X[:, t, :], X[:, t, :], p_proj[:, g % 2, :].rearrange("p (t d) -> p t d", d=D),
                                      ALU.add).then_inc(added, 1)


NEXP = 8


def moe_ffn(nc, C, I, name, X, xnT):
    with Stage(nc, name) as M:
        pick = M.sb("pick", [P, NT, NEXP])
        b1T = M.sb("b1T", [P, NEXP * MFF])
        route(nc, C, I, name, X, xnT, pick, b1T)
        experts(nc, C, I, name, X, xnT, pick, b1T)


def route(nc, C, I, name, X, xnT, pick, b1T):
    with Stage(nc, name + "_route") as S:
        WrT = S.sb("WrT", [P, NEXP])
        br = S.sb("br", [P, NEXP])
        b1 = S.sb("b1", [NEXP * MFF, P])
        b2 = S.sb("b2", [NEXP, D])
        rank = S.sb("rank", [P, NEXP])
        logits = S.sb("logits", [P, NT, NEXP])
        best = S.sb("best", [P, NT])
        tied = S.sb("tied", [P, NT, NEXP])
        first = S.sb("first", [P, NT])
        pickT = S.sb("pickT", [NEXP, TOK])
        p_logits = S.ps("p_logits", [P, CH])
        p_b1T = S.ps("p_b1T", [P, CH])
        p_pickT = S.ps("p_pickT", [P, TOK])
        loaded, ranked = S.sem("loaded"), S.sem("ranked")
        logits_ready, own, picked = S.sem("logits_ready"), S.sem("own"), S.sem("picked")
        turned, stored = S.sem("turned"), S.sem("stored")
        bias_ready, b1_ready, bias_added = S.sem("bias_ready"), S.sem("b1_ready"), S.sem("bias_added")
        with nc.Block() as block:

            @block.sync
            def _(sp):
                sp.dma_start(WrT[:, :], I["L1_ffn_Wr"].rearrange("e d -> d e"),
                             allow_slow_non_contiguous=True).then_inc(loaded, 16)
                sp.dma_start(br[:, :], I["L1_ffn_br"].partition_broadcast(P)).then_inc(loaded, 16)
                sp.dma_start(b1[:, :], I["L1_ffn_b1"].rearrange("e (m p) -> (e m) p", p=P)).then_inc(loaded, 16)
                sp.dma_start(b2[:, :], I["L1_ffn_b2"]).then_inc(loaded, 16)

            @block.gpsimd
            def _(pool):
                for e in range(NEXP):
                    pool.memset(rank[:, e:e + 1], float(NEXP - e)).then_inc(ranked, 1)

            @block.tensor
            def _(pe):
                pe.wait_ge(loaded, 64)
                for t in range(NT):
                    mm = pe.matmul(p_logits[:, t * NEXP:(t + 1) * NEXP], xnT[:, t * P:(t + 1) * P], WrT[:, :],
                                   start=True, stop=True)
                mm.then_inc(logits_ready, 1)
                pe.transpose(p_b1T[:, 0:NEXP * MFF], b1[:, :], C.ident[0:NEXP * MFF, 0:NEXP * MFF]).then_inc(b1_ready, 1)
                pe.wait_ge(picked, 1)
                for t in range(NT):
                    mm = pe.transpose(p_pickT[0:NEXP, t * P:(t + 1) * P], pick[:, t, :], C.ident[:, :])
                mm.then_inc(turned, 1)
                pe.wait_ge(stored, 1)
                for t in range(NT):
                    mm = pe.matmul(p_pickT[:, t * D:(t + 1) * D], pickT[:, t * P:(t + 1) * P], b2[:, :],
                                   start=True, stop=True)
                mm.then_inc(bias_ready, 1)

            @block.scalar
            def _(act):
                act.wait_ge(b1_ready, 1)
                act.copy(b1T[:, :], p_b1T[:, 0:NEXP * MFF])
                act.wait_ge(turned, 1)
                act.copy(pickT[:, :], p_pickT[0:NEXP, :]).then_inc(stored, 1)

            @block.vector
            def _(dve):
                chain = Chain(dve, own)
                dve.wait_ge(loaded, 64)
                dve.wait_ge(ranked, NEXP)
                dve.wait_ge(logits_ready, 1)
                chain.step(dve.tensor_tensor(logits[:, :, :], p_logits[:, 0:NT * NEXP].rearrange("p (t e) -> p t e", e=NEXP),
                                             per_feature(br[:, :], NT), ALU.add))
                chain.step(dve.tensor_reduce(best[:, :], logits[:, :, :], AX, ALU.max))
                chain.step(dve.tensor_tensor(tied[:, :, :], logits[:, :, :], per_token(best[:, :], NEXP), ALU.is_equal))
                chain.step(dve.tensor_tensor(tied[:, :, :], tied[:, :, :], per_feature(rank[:, :], NT), ALU.mult))
                chain.step(dve.tensor_reduce(first[:, :], tied[:, :, :], AX, ALU.max))
                chain.step(dve.tensor_tensor(tied[:, :, :], tied[:, :, :], per_token(first[:, :], NEXP), ALU.is_equal))
                dve.tensor_scalar(pick[:, :, :], tied[:, :, :], 0.5, None, ALU.mult).then_inc(picked, 1)
                dve.wait_ge(bias_ready, 1)
                dve.tensor_tensor(X[:, :, :], X[:, :, :], p_pickT[:, :].rearrange("p (t d) -> p t d", d=D), ALU.add)


def experts(nc, C, I, name, X, xnT, pick, b1T):
    W1 = I["L1_ffn_W1"]
    W2 = I["L1_ffn_W2"]
    with Stage(nc, name + "_experts") as S:
        raw1 = [S.sb(f"raw1_{k}", [P, MFF, D]) for k in range(2)]
        raw2 = [S.sb(f"raw2_{k}", [P, DFF]) for k in range(2)]
        up = [S.sb(f"up{k}", [P, DFF]) for k in range(2)]
        down = [S.sb(f"down{k}", [P, MFF, D]) for k in range(2)]
        b1 = [S.sb(f"b1_{k}", [P, MFF]) for k in range(2)]
        hidden = [S.sb(f"hidden{k}", [P, MFF, CH]) for k in range(2)]
        p_up = S.ps("p_up", [P, MFF, CH])
        p_down = S.ps("p_down", [P, 2, CH])
        p_turn = S.ps("p_turn", [P, 2, DFF])
        loaded = [S.sem(f"loaded{k}") for k in range(2)]
        turned = S.sem("turned")
        up_stored, down_stored = S.sem("up_stored"), S.sem("down_stored")
        up_ready, relu_done = S.sem("up_ready"), S.sem("relu_done")
        down_ready, added = S.sem("down_ready"), S.sem("added")
        PAIRS = NEXP // 2

        with nc.Block() as block:

            @block.sync
            def _(sp):
                def fetch(e, k):
                    sp.dma_start(raw1[k][:, :, :], W1[ds(e, 1)].rearrange("e (m p) d -> p (e m) d", p=P)
                                 ).then_inc(loaded[k], 16)
                    sp.dma_start(raw2[k][:, :], W2[ds(e, 1)].rearrange("e d f -> d (e f)")).then_inc(loaded[k], 16)

                fetch(0, 0)
                fetch(1, 1)
                with sp.Fori(0, PAIRS - 1) as i:
                    for k in range(2):
                        sp.wait_ge(turned, i * 2 + k + 1)
                        fetch(i * 2 + k + 2, k)

            @block.tensor
            def _(pe):
                def turn(k, pair):
                    pe.wait_ge(loaded[k], pair * 32 + 32)
                    for m in range(MFF):
                        pe.transpose(p_turn[:, 0, m * P:(m + 1) * P], raw1[k][:, m, :], C.ident[:, :])
                    for m in range(MFF):
                        mm = pe.transpose(p_turn[:, 1, m * P:(m + 1) * P], raw2[k][:, m * P:(m + 1) * P], C.ident[:, :])
                    mm.then_inc(turned, 1)

                def up_products(i, k, c):
                    before = i * 8 * MFF + (k * NCH + c) * MFF
                    for m in range(MFF):
                        if k or c:
                            pe.wait_ge(relu_done, before - MFF + m + 1)
                        else:
                            pe.wait_ge(relu_done, before)
                        pe.matmul(p_up[:, m, :], up[k][:, m * P:(m + 1) * P], xnT[:, c * CH:(c + 1) * CH],
                                  start=True, stop=True).then_inc(up_ready, 1)

                def down_products(i, k, c):
                    n = i * 8 + k * NCH + c
                    pe.wait_ge(relu_done, (n + 1) * MFF)
                    pe.wait_ge(added, n - 1 if k or c else n)
                    for t in range(TPC):
                        for m in range(MFF):
                            mm = pe.matmul(p_down[:, c % 2, t * D:(t + 1) * D], hidden[c % 2][:, m, t * P:(t + 1) * P],
                                           down[k][:, m, :], start=(m == 0), stop=(m == MFF - 1))
                    mm.then_inc(down_ready, 1)

                def pair(i, last):
                    for k in range(2):
                        pe.wait_ge(up_stored, i * 2 + k + 1)
                        pe.wait_ge(down_stored, i * 2 + k + 1)
                        up_products(i, k, 0)
                        for c in range(NCH):
                            if c + 1 < NCH:
                                up_products(i, k, c + 1)
                            down_products(i, k, c)
                            if c == 1 and not (last and k):
                                turn(1 - k, i + k)

                turn(0, 0)
                with pe.Fori(0, PAIRS - 1) as i:
                    pair(i, False)
                pair(PAIRS - 1, True)

            @block.scalar
            def _(act):
                def pair(i, last):
                    for k in range(2):
                        for c in range(NCH):
                            n = i * 8 + k * NCH + c
                            act.wait_ge(down_ready, n - 1 if k or c else n)
                            for m in range(MFF):
                                act.wait_ge(up_ready, n * MFF + m + 1)
                                act.activation(hidden[c % 2][:, m, :], p_up[:, m, :], ACT.Relu,
                                               bias=b1[k][:, m:m + 1]).then_inc(relu_done, 1)
                        if not (last and k):
                            act.wait_ge(turned, i * 2 + k + 2)
                            act.copy(up[1 - k][:, :], p_turn[:, 0, :]).then_inc(up_stored, 1)

                act.wait_ge(turned, 1)
                act.copy(up[0][:, :], p_turn[:, 0, :]).then_inc(up_stored, 1)
                with act.Fori(0, PAIRS - 1) as i:
                    pair(i, False)
                pair(PAIRS - 1, True)

            @block.vector
            def _(dve):
                def pair(i, last):
                    for k in range(2):
                        for c in range(NCH):
                            n = i * 8 + k * NCH + c
                            dve.wait_ge(down_ready, n + 1)
                            dve.wait_ge(added, n)
                            for t in range(TPC):
                                tile = c * TPC + t
                                last_add = dve.scalar_tensor_tensor(
                                    out=X[:, tile, :], in0=p_down[:, c % 2, t * D:(t + 1) * D],
                                    scalar=pick[:, tile, ds(i * 2 + k, 1)], in1=X[:, tile, :], op0=ALU.mult, op1=ALU.add)
                            last_add.then_inc(added, 1)
                        if not (last and k):
                            dve.wait_ge(turned, i * 2 + k + 2)
                            dve.tensor_copy(down[1 - k][:, :, :], p_turn[:, 1, :].rearrange("p (m d) -> p m d", d=D))
                            dve.tensor_copy(b1[1 - k][:, :], b1T[:, ds((i * 2 + k + 1) * MFF, MFF)]).then_inc(down_stored, 1)

                dve.wait_ge(turned, 1)
                dve.tensor_copy(down[0][:, :, :], p_turn[:, 1, :].rearrange("p (m d) -> p m d", d=D))
                dve.tensor_copy(b1[0][:, :], b1T[:, 0:MFF]).then_inc(down_stored, 1)
                with dve.Fori(0, PAIRS - 1) as i:
                    pair(i, False)
                pair(PAIRS - 1, True)


UNITS = BATCH * H
NP = 3
KR = NP * NP * HD
KM = KR + NP
VW = HD + 1


def stacked_attention_mixer(nc, C, I, X, xn, xnT):
    with Stage(nc, "mix1") as M:
        parts = {n: nc.dram_tensor(f"mix1_{n}", [NP, HD, UNITS, SEQ], BF16, kind="Internal") for n in ("q", "k", "k2")}
        V = M.sb("V", [P, UNITS, TPB, VW])
        shifted = M.sb("shifted", [P, NT, D])
        Y = [M.sb(f"Y{n}", [P, UNITS, TPB, HD]) for n in range(2)]
        mask_q = M.sb("mask_q", [P, 2, 2, P], BF16)
        mask_k = M.sb("mask_k", [P, 2, 2, P], BF16)
        ident16 = M.sb("ident16", [P, P], BF16)
        project_and_split(nc, C, I, xn, xnT, parts, V, shifted, mask_q, mask_k, ident16)
        causal_attention(nc, C, "mix1_a", parts["q"], parts["k"], V, Y[0], mask_q[:, 0], mask_k[:, 0], ident16)
        errors(nc, V, shifted, Y[0])
        causal_attention(nc, C, "mix1_b", parts["q"], parts["k2"], V, Y[1], mask_q[:, 1], mask_k[:, 1], ident16)
        project_out(nc, C, I, X, Y)


def tokens_of(V, b):
    return V[:, b * H:(b + 1) * H, :, 0:HD].rearrange("p h t d -> p t h d")


def project_and_split(nc, C, I, xn, xnT, parts, V, shifted, mask_q, mask_k, ident16):
    SCALE = float(HD) ** -0.5
    with Stage(nc, "mix1_proj") as S:
        W = S.sb("W", [P, 3, D])
        bias = S.sb("bias", [P, 3])
        bias_s = S.sb("bias_s", [P, 3])
        full = [S.sb(f"full{k}", [P, CH]) for k in range(2)]
        rest = [S.sb(f"rest{k}", [P, CH]) for k in range(2)]
        split_parts = S.sb("split_parts", [P, NP, 3, TOK], BF16)
        p = S.ps("p", [P, 2, CH])
        loaded, biased, shifted_ok, cleared = S.sem("loaded"), S.sem("biased"), S.sem("shifted_ok"), S.sem("cleared")
        ready, stored, split = S.sem("ready"), S.sem("stored"), S.sem("split")
        own, rest_ready = S.sem("own"), S.sem("rest_ready")
        sent, masks = S.sem("sent"), S.sem("masks")
        N = 3 * NCH
        with nc.Block() as block:

            @block.sync
            def _(sp):
                sp.dma_start(W[:, 0:2, :].rearrange("p a d -> p (a d)"), I["L1_attn_W_attn"]).then_inc(loaded, 16)
                sp.dma_start(W[:, 2, :], I["L1_attn_W_k2"]).then_inc(loaded, 16)
                sp.dma_start(bias[:, 0:2], I["L1_attn_b_attn"].rearrange("(a p) -> p a", p=P),
                             allow_slow_non_contiguous=True).then_inc(loaded, 16)
                sp.dma_start(bias[:, 2:3], I["L1_attn_b_k2"].unsqueeze(1)).then_inc(loaded, 16)
                sp.dma_start(shifted[0:112, :, :], xn[1:113, :, :]).then_inc(shifted_ok, 16)
                sp.dma_start(shifted[112:127, :, :], xn[113:128, :, :]).then_inc(shifted_ok, 16)
                sp.dma_start(shifted[127:128, 0:NT - 1, :], xn[0:1, 1:NT, :]).then_inc(shifted_ok, 16)
                sp.dma_start(shifted[127:128, NT - 1, :], xn[0:1, 0, :]).then_inc(shifted_ok, 16)
                for n, name in enumerate(("q", "k", "k2")):
                    sp.wait_ge(split, NCH * (n + 1))
                    for a in range(NP):
                        for b in range(BATCH):
                            sp.dma_start(parts[name][a, :, b * H:(b + 1) * H, :].rearrange("d h s -> h d s"),
                                         split_parts[:, a, n, b * SEQ:(b + 1) * SEQ]).then_inc(sent, 16)
                sp.wait_ge(sent, 16 * 3 * NP * BATCH)
                sp.wait_ge(shifted_ok, 64)

            @block.tensor
            def _(pe):
                pe.wait_ge(loaded, 64)
                for n in range(3):
                    for c in range(NCH):
                        i = n * NCH + c
                        if i >= 2:
                            pe.wait_ge(stored, i - 1)
                        pe.matmul(p[:, i % 2, :], W[:, n, :], xnT[:, c * CH:(c + 1) * CH],
                                  start=True, stop=True).then_inc(ready, 1)

            @block.scalar
            def _(act):
                act.wait_ge(biased, 1)
                for i in range(N):
                    n = i // NCH
                    act.wait_ge(ready, i + 1)
                    if i >= 2:
                        act.wait_ge(rest_ready, i - 1)
                    act.activation(full[i % 2][:, :], p[:, i % 2, :], ACT.Identity, bias=bias_s[:, n:n + 1],
                                   scale=SCALE if n == 0 else 1.0).then_inc(stored, 1)

            @block.vector
            def _(dve):
                dve.wait_ge(loaded, 64)
                chain = Chain(dve, own)
                dve.tensor_scalar(bias_s[:, 0:1], bias[:, 0:1], SCALE, None, ALU.mult)
                dve.tensor_copy(bias_s[:, 1:3], bias[:, 1:3]).then_inc(biased, 1)
                for i in range(N):
                    n, c = i // NCH, i % NCH
                    col = slice(c * CH, (c + 1) * CH)
                    dve.wait_ge(stored, i + 1)
                    if i >= 2:
                        dve.wait_ge(split, i - 1)
                    chain.step(dve.tensor_copy(split_parts[:, 0, n, col], full[i % 2][:, :]))
                    dve.tensor_tensor(rest[i % 2][:, :], full[i % 2][:, :], split_parts[:, 0, n, col], ALU.subtract
                                      ).then_inc(rest_ready, 1)
                    dve.wait_ge(rest_ready, i + 1)
                    chain.step(dve.tensor_copy(split_parts[:, 1, n, col], rest[i % 2][:, :]))
                    dve.tensor_tensor(split_parts[:, 2, n, col], rest[i % 2][:, :], split_parts[:, 1, n, col],
                                      ALU.subtract).then_inc(split, 1)
                for b in range(BATCH):
                    for h in range(H):
                        dve.tensor_copy(V[:, b * H + h, :, 0:HD], xn[:, b * TPB:(b + 1) * TPB, h * HD:(h + 1) * HD])
                dve.memset(V[:, :, :, HD:VW], 1.0)
                dve.tensor_copy(ident16[:, :], C.ident[:, :])

            @block.gpsimd
            def _(pool):
                pool.memset(mask_q[:, :, :, :], 0.0)
                pool.memset(mask_k[:, :, :, :], 0.0).then_inc(cleared, 1)
                pool.wait_ge(cleared, 1)
                for strict in range(2):
                    for tile in range(2):
                        pool.affine_select(out=mask_q[:, strict, tile, :], in_=mask_q[:, strict, tile, :],
                                           compare_op=ALU.is_ge, fill=-BIG, base=-strict, pattern=[[-1, P]],
                                           channel_multiplier=1)
                        pool.affine_select(out=mask_k[:, strict, tile, :], in_=mask_k[:, strict, tile, :],
                                           compare_op=ALU.is_ge, fill=-BIG, base=-strict, pattern=[[1, P]],
                                           channel_multiplier=-1).then_inc(masks, 1)
                pool.wait_ge(masks, 4)
                pool.memset(mask_q[0:1, 1, 0, 0:1], 0.0)
                pool.memset(mask_k[0:1, 1, 0, 0:1], 0.0)


QH = 4
QUADS = UNITS // QH
SETS = 3


def causal_attention(nc, C, name, q_parts, k_parts, V, Y, mask_q, mask_k, ident16):
    GROUPS = [(qc, kt) for qc in range(SEQ // CH) for kt in range((qc + 1) * TPC)]
    NG = len(GROUPS)
    CHUNKS = [(g, 0) for g in range(TPB)] + [(g, 1) for g in range(TPC, TPB)]
    LEAD = 12
    NE, NS = QH * NG, QH * len(CHUNKS)
    SCHEDULE = []
    taken = 0
    for i in range(NE):
        if i == 0:
            SCHEDULE.append(("Y", 0))
        SCHEDULE.append(("E", i))
        if i % QH == QH - 1 and i >= QH:
            SCHEDULE.append(("V", i // QH - 1))
        while taken < min(NS, -(-NS * (i + 1) // (NE - LEAD))):
            SCHEDULE.append(("S", taken))
            taken += 1
        SCHEDULE += {8: [("N", 0)], 13: [("N", 1)], NE - LEAD + 1: [("M", 0)], NE - LEAD + 3: [("T", 0)]}.get(i, [])
    SCHEDULE.append(("V", NG - 1))

    with Stage(nc, name) as S:
        q = S.sb("q", [KM, SETS, QH, SEQ], BF16)
        k_ = S.sb("k", [KM, SETS, QH, SEQ], BF16)
        vals = S.sb("vals", [P, SETS, QH, TPB, VW])
        part_max = S.sb("part_max", [P, QH, NS // QH])
        rest_max = S.sb("rest_max", [P, QH, TPB])
        max_all = S.sb("max_all", [P, P], BF16)
        max_parts = max_all[:, 0:NP * QH * TPB].rearrange("p (a j t) -> p a j t", a=NP, j=QH)
        max_rows = S.sb("max_rows", [NP * QH * TPB, P], BF16)
        e = S.sb("e", [P, 2, QH, CH])
        y = S.sb("y", [P, SEQ])
        recip = S.sb("recip", [P, 2, TPC, QH])
        p_s = [S.ps(f"p_s{n}", [P, CH]) for n in range(2)]
        p_e = [S.ps(f"p_e{n}", [P, CH]) for n in range(3)]
        p_y = S.ps("p_y", [P, SEQ])
        p_t = S.ps("p_t", [P, CH])
        ones_set, cleared, vals_ready = S.sem("ones_set"), S.sem("cleared"), S.sem("vals_ready")
        loaded = [S.sem(f"loaded{n}") for n in range(SETS)]
        s_ready = [S.sem(f"s_ready{n}") for n in range(2)]
        s_read = [S.sem(f"s_read{n}") for n in range(2)]
        m_own, m_split, m_turned, m_copied, m_sent = (S.sem("m_own"), S.sem("m_split"), S.sem("m_turned"),
                                                      S.sem("m_copied"), S.sem("m_sent"))
        e_scores, e_done, pv_done = S.sem("e_scores"), S.sem("e_done"), S.sem("pv_done")
        y_copied, y_turned, y_own, y_normed = S.sem("y_copied"), S.sem("y_turned"), S.sem("y_own"), S.sem("y_normed")

        def steps(eng, step):
            step(0, 0, 0)
            with eng.Fori(0, (QUADS - 2) // SETS) as i:
                for k in range(1, SETS + 1):
                    step(Count(i, SETS, k), k, i)
            step(QUADS - 1, QUADS - 1, 0)

        def last(m, ahead):
            return isinstance(m, int) and m + ahead >= QUADS

        with nc.Block() as block:

            @block.sync
            def _(sp):
                def fetch(m, n):
                    heads = ds(at_turn(m * QH), QH)
                    for a in range(NP):
                        rows = slice(a * NP * HD, (a + 1) * NP * HD)
                        sp.dma_start(q[rows, n, :, :], q_parts[a, :, heads, :].rearrange("d j s -> d (j s)").unsqueeze(0)
                                     .to_broadcast([NP, HD, QH * SEQ])).then_inc(loaded[n], 16)
                        sp.dma_start(k_[rows, n, :, :], k_parts[:, :, heads, :].rearrange("b d j s -> b d (j s)")
                                     ).then_inc(loaded[n], 16)

                def send(m, n):
                    wait(sp, m_copied, m + 1)
                    for a in range(NP):
                        sp.dma_start(q[KR + a:KR + a + 1, n, :, :], max_rows[a * QH * TPB:(a + 1) * QH * TPB, :]
                                     ).then_inc(m_sent, 16)

                wait(sp, ones_set, 1)
                fetch(0, 0)
                fetch(1, 1)
                send(0, 0)
                with sp.Fori(0, (QUADS - 2) // SETS) as i:
                    for k in range(SETS):
                        m = Count(i, SETS, k)
                        wait(sp, pv_done, m * NG)
                        fetch(m + 2, (k + 2) % SETS)
                        send(m + 1, (k + 1) % SETS)
                send(QUADS - 1, (QUADS - 1) % SETS)

            @block.gpsimd
            def _(pool):
                def copy_values(m, n):
                    pool.tensor_copy(vals[:, n, :, :, :], V[:, ds(at_turn(m * QH), QH), :, :]).then_inc(vals_ready, 1)

                copy_values(0, 0)
                copy_values(1, 1)
                with pool.Fori(0, (QUADS - 2) // SETS) as i:
                    for k in range(SETS):
                        m = Count(i, SETS, k)
                        wait(pool, pv_done, m * NG)
                        copy_values(m + 2, (k + 2) % SETS)

            @block.tensor
            def _(pe):
                def scores(m, k, i, s):
                    j, (g, c) = s // len(CHUNKS), CHUNKS[s % len(CHUNKS)]
                    if s == 0:
                        wait(pe, loaded[k % SETS], (i + k // SETS + 1) * (NP * 32))
                    wait(pe, s_read[s % 2], m * (NS // 2) + s // 2)
                    n = (g + 1) * P
                    w = min(n - c * CH, CH)
                    diag = (c == 1) == (g >= TPC)
                    mm = pe.matmul(p_s[s % 2][:, 0:w], q[0:KR, k % SETS, j, g * P:(g + 1) * P],
                                   k_[0:KR, k % SETS, j, c * CH:c * CH + w], start=True, stop=not diag,
                                   skip_group_check=True)
                    if diag:
                        mm = pe.matmul(p_s[s % 2][:, w - P:w], ident16[:, :], mask_q[:, min(g, 1), :], start=False,
                                       stop=True, skip_group_check=True)
                    mm.then_inc(s_ready[s % 2], 1)

                def turn_max(m):
                    wait(pe, m_split, m + 1)
                    wait(pe, y_normed, (m - 1) * 2)
                    pe.transpose(p_t[:, 0:P // 2].bitcast(BF16), max_all[:, :], ident16[:, :]).then_inc(m_turned, 1)

                def exp_scores(m, k, e_at):
                    (qc, kt), j = GROUPS[e_at // QH], e_at % QH
                    q0 = max(kt * P, qc * CH)
                    w = (qc + 1) * CH - q0
                    if e_at == 0:
                        wait(pe, m_sent, m * (NP * 16) + NP * 16)
                    wait(pe, e_done, m * NE + e_at - 2)
                    diag = kt * P >= qc * CH
                    bank = p_e[e_at % 3]
                    mm = pe.matmul(bank[:, 0:w], k_[:, k % SETS, j, kt * P:(kt + 1) * P],
                                   q[:, k % SETS, j, q0:q0 + w], start=True, stop=not diag, skip_group_check=True)
                    if diag:
                        mm = pe.matmul(bank[:, 0:P], ident16[:, :], mask_k[:, min(kt, 1), :], start=False, stop=True,
                                       skip_group_check=True)
                    mm.then_inc(e_scores, 1)

                def times_values(m, k, n):
                    qc, kt = GROUPS[n]
                    q0 = max(kt * P, qc * CH)
                    w = (qc + 1) * CH - q0
                    if n == 0:
                        wait(pe, y_copied, m + 1)
                        wait(pe, vals_ready, m + 1)
                    wait(pe, e_done, m * NE + (n + 1) * QH)
                    for j in range(QH):
                        mm = pe.matmul(p_y[32 * j:32 * j + VW, q0:q0 + w], vals[:, k % SETS, j, kt, :], e[:, n % 2, j, 0:w],
                                       start=(kt == 0), stop=(kt == qc * TPC + TPC - 1), skip_group_check=True,
                                       tile_position=(0, 32 * j))
                    mm.then_inc(pv_done, 1)

                def turn_result(m, h):
                    if h == 0:
                        wait(pe, y_copied, m + 2)
                        wait(pe, m_copied, m + 2 if not last(m, 1) else QUADS)
                    else:
                        wait(pe, y_normed, m * 2 + 1)
                    for t in range(TPC):
                        at = (h * TPC + t) * P
                        mm = pe.transpose(p_t[:, t * P:(t + 1) * P], y[:, at:at + P], C.ident[:, :])
                    mm.then_inc(y_turned, 1)

                def step(m, k, i):
                    for what, n in SCHEDULE:
                        if what == "E":
                            exp_scores(m, k, n)
                        elif what == "V":
                            times_values(m, k, n)
                        elif what == "S" and not last(m, 1):
                            scores(m + 1, k + 1, i, n)
                        elif what == "T" and not last(m, 1):
                            turn_max(m + 1)
                        elif what == "N" and k > 0:
                            turn_result(m - 1, n)

                wait(pe, ones_set, 1)
                for s in range(NS):
                    scores(0, 0, 0, s)
                turn_max(0)
                steps(pe, step)
                for h in range(2):
                    turn_result(QUADS - 1, h)

            @block.scalar
            def _(act):
                def step(m, k, i):
                    for n in range(NE):
                        (qc, kt), j = GROUPS[n // QH], n % QH
                        w = (qc + 1) * CH - max(kt * P, qc * CH)
                        wait(act, e_scores, m * NE + n + 1)
                        if j == 0:
                            wait(act, pv_done, m * NG + n // QH - 1)
                        act.activation(e[:, n // QH % 2, j, 0:w], p_e[n % 3][:, 0:w], ACT.Exp).then_inc(e_done, 1)

                steps(act, step)

            @block.vector
            def _(dve):
                def max_of(m, s):
                    j, (g, c) = s // len(CHUNKS), CHUNKS[s % len(CHUNKS)]
                    w = min((g + 1) * P - c * CH, CH)
                    if s == 0:
                        wait(dve, m_split, m)
                    wait(dve, s_ready[s % 2], m * (NS // 2) + s // 2 + 1)
                    at = s % len(CHUNKS)
                    dve.tensor_reduce(part_max[:, j, at:at + 1], p_s[s % 2][:, 0:w], AX, ALU.max, negate=True
                                      ).then_inc(s_read[s % 2], 1)

                def split_max(m):
                    for n in range(2):
                        wait(dve, s_read[n], (m + 1) * (NS // 2))
                    whole = part_max[:, :, 0:TPB]
                    a, b = part_max[:, :, TPC:TPB], part_max[:, :, TPB:TPB + TPC]
                    dve.tensor_tensor(a, a, b, ALU.min).then_inc(m_own, 1)
                    wait(dve, m_own, m * 4 + 1)
                    wait(dve, m_turned, m)
                    dve.tensor_copy(max_parts[:, 0, :, :], whole).then_inc(m_own, 1)
                    wait(dve, m_own, m * 4 + 2)
                    dve.tensor_tensor(rest_max[:, :, :], whole, max_parts[:, 0, :, :], ALU.subtract).then_inc(m_own, 1)
                    wait(dve, m_own, m * 4 + 3)
                    dve.tensor_copy(max_parts[:, 1, :, :], rest_max[:, :, :]).then_inc(m_own, 1)
                    wait(dve, m_own, m * 4 + 4)
                    dve.tensor_tensor(max_parts[:, 2, :, :], rest_max[:, :, :], max_parts[:, 1, :, :], ALU.subtract
                                      ).then_inc(m_split, 1)

                def copy_max(m):
                    wait(dve, m_turned, m + 1)
                    wait(dve, m_sent, m * (NP * 16))
                    dve.tensor_copy(max_rows[:, :], p_t[0:NP * QH * TPB, 0:P // 2].bitcast(BF16)).then_inc(m_copied, 1)

                def copy_result(m):
                    wait(dve, pv_done, (m + 1) * NG)
                    wait(dve, y_turned, m * 2)
                    dve.tensor_copy(y[:, :], p_y[:, :]).then_inc(y_copied, 1)

                def divide(m, h):
                    wait(dve, y_turned, m * 2 + h + 1)
                    p = p_t[:, :].rearrange("p (t j w) -> p t j w", t=TPC, j=QH)
                    dve.reciprocal(recip[:, h, :, :], p[:, :, :, HD]).then_inc(y_own, 1)
                    wait(dve, y_own, m * 2 + h + 1)
                    for t in range(TPC):
                        last_one = dve.tensor_tensor(Y[:, ds(at_turn(m * QH), QH), h * TPC + t, :], p[:, t, :, 0:HD],
                                                     recip[:, h, t, :].unsqueeze(2).to_broadcast([P, QH, HD]), ALU.mult)
                    last_one.then_inc(y_normed, 1)

                def step(m, k, i):
                    for what, n in SCHEDULE:
                        if what == "Y" and k > 0:
                            copy_result(m - 1)
                        elif what == "S" and not last(m, 1):
                            max_of(m + 1, n)
                        elif what == "M" and not last(m, 1):
                            split_max(m + 1)
                        elif what == "T" and not last(m, 1):
                            copy_max(m + 1)
                        elif what == "N" and k > 0:
                            divide(m - 1, n)

                dve.memset(p_y[:, :], 0.0).then_inc(y_copied, 1)
                dve.memset(max_all[:, :], 0.0).then_inc(cleared, 1)
                wait(dve, cleared, 1)
                dve.memset(k_[64:KM, :, :, :], 1.0).then_inc(ones_set, 1)
                for s in range(NS):
                    max_of(0, s)
                split_max(0)
                copy_max(0)
                steps(dve, step)
                copy_result(QUADS - 1)
                for h in range(2):
                    divide(QUADS - 1, h)


def errors(nc, V, shifted, Y):
    with nc.Block() as block:

        @block.vector
        def _(dve):
            for b in range(BATCH):
                for h in range(H):
                    dve.tensor_tensor(V[:, b * H + h, :, 0:HD], shifted[:, b * TPB:(b + 1) * TPB, h * HD:(h + 1) * HD],
                                      Y[:, b * H + h, :, :], ALU.subtract)


def project_out(nc, C, I, X, Y):
    G = NT // TPC
    with Stage(nc, "mix1_out") as S:
        W = S.sb("W", [P, D])
        bias = S.sb("bias", [1, D])
        bias2 = S.sb("bias2", [1, D])
        total = S.sb("total", [P, NT, D])
        totalT = S.sb("totalT", [P, TOK])
        p_turn = S.ps("p_turn", [P, 2, CH])
        p_out = S.ps("p_out", [P, 2, CH])
        loaded, own, summed = S.sem("loaded"), S.sem("own"), S.sem("summed")
        turned, stored, ready, added, bias_ok = (S.sem("turned"), S.sem("stored"), S.sem("ready"), S.sem("added"),
                                                 S.sem("bias_ok"))
        with nc.Block() as block:

            @block.sync
            def _(sp):
                sp.dma_start(W[:, :], I["L1_attn_W_proj"]).then_inc(loaded, 16)
                sp.dma_start(bias[:, :], I["L1_attn_b_proj"].unsqueeze(0)).then_inc(loaded, 16)

            @block.vector
            def _(dve):
                chain = Chain(dve, own)
                for b in range(BATCH):
                    chain.step(dve.memset(Y[1][0:1, b * H:(b + 1) * H, 0, :], 0.0))
                for b in range(BATCH):
                    for h in range(H):
                        last = dve.tensor_tensor(total[:, b * TPB:(b + 1) * TPB, h * HD:(h + 1) * HD], Y[0][:, b * H + h, :, :],
                                                 Y[1][:, b * H + h, :, :], ALU.add)
                    last.then_inc(summed, 1)
                dve.wait_ge(loaded, 32)
                dve.tensor_scalar(bias2[:, :], bias[:, :], 2.0, None, ALU.mult).then_inc(bias_ok, 1)
                for g in range(G):
                    t = slice(g * TPC, (g + 1) * TPC)
                    dve.wait_ge(ready, g + 1)
                    dve.tensor_tensor(X[:, t, :], X[:, t, :], p_out[:, g % 2, :].rearrange("p (t d) -> p t d", d=D),
                                      ALU.add).then_inc(added, 1)

            @block.tensor
            def _(pe):
                def turn(g):
                    pe.wait_ge(summed, g * TPC // TPB + 1)
                    if g >= 2:
                        pe.wait_ge(stored, g - 1)
                    for k in range(TPC):
                        mm = pe.transpose(p_turn[:, g % 2, k * P:(k + 1) * P], total[:, g * TPC + k, :], C.ident[:, :])
                    mm.then_inc(turned, 1)

                turn(0)
                pe.wait_ge(bias_ok, 1)
                for g in range(G):
                    if g + 1 < G:
                        turn(g + 1)
                    pe.wait_ge(stored, g + 1)
                    if g >= 2:
                        pe.wait_ge(added, g - 1)
                    for k in range(TPC):
                        t = g * TPC + k
                        pe.matmul(p_out[:, g % 2, k * D:(k + 1) * D], C.ones[0:1, :], bias2[:, :], start=True, stop=False)
                        mm = pe.matmul(p_out[:, g % 2, k * D:(k + 1) * D], totalT[:, t * P:(t + 1) * P], W[:, :],
                                       start=False, stop=True)
                    mm.then_inc(ready, 1)

            @block.scalar
            def _(act):
                for g in range(G):
                    act.wait_ge(turned, g + 1)
                    act.copy(totalT[:, g * CH:(g + 1) * CH], p_turn[:, g % 2, :]).then_inc(stored, 1)


AH, AD = 16, 64
DIST0 = SEQ - P


def alibi_attention_mixer(nc, C, I, X, xn, xnT):
    with Stage(nc, "mix2") as M:
        gamma = M.sb("gamma", [P, D])
        beta = M.sb("beta", [P, D])
        dist = M.sb("dist", [P, DIST0 + SEQ])
        slopes = M.sb("slopes", [P, AH])
        load(nc, "mix2_load", [(gamma[:, :], I["L2_attn_ln_gamma"].partition_broadcast(P)),
                               (beta[:, :], I["L2_attn_ln_beta"].partition_broadcast(P))])
        normalise(nc, C, "mix2_norm", xn, xn, xnT, gamma=gamma[:, :], beta=beta[:, :])
        with Stage(nc, "mix2_tables") as S:
            steps = S.sb("steps", [P, DIST0 + SEQ], mybir.dt.int32)
            signed = S.sb("signed", [P, DIST0 + SEQ])
            made, own = S.sem("made"), S.sem("own")
            with nc.Block() as block:

                @block.gpsimd
                def _(pool):
                    pool.iota(steps[:, :], pattern=[[-1, DIST0 + SEQ]], base=DIST0, channel_multiplier=1).then_inc(made, 1)
                    for h in range(AH):
                        pool.memset(slopes[:, h:h + 1], -float(np.float32(2.0 ** (-8.0 / (AH - h)))))

                @block.vector
                def _(dve):
                    chain = Chain(dve, own)
                    dve.wait_ge(made, 1)
                    chain.step(dve.tensor_copy(signed[:, :], steps[:, :]))
                    chain.step(dve.tensor_scalar(dist[:, :], signed[:, :], -1.0, None, ALU.mult))
                    chain.step(dve.tensor_tensor(dist[:, :], dist[:, :], signed[:, :], ALU.max))

        for b in range(BATCH):
            with Stage(nc, f"mix2_{b}") as S:
                V = S.sb("V", [P, AH, TPB, AD])
                head_values(nc, C, I, f"mix2_v{b}", b, xnT, V)
                alibi_heads(nc, C, I, f"mix2_h{b}", b, xnT, V, dist, slopes, X)


def head_values(nc, C, I, name, b, xnT, V):
    with Stage(nc, name) as S:
        Wv = S.sb("Wv", [P, AH * AD])
        p = S.ps("p", [P, 4, CH])
        loaded, ready, stored = S.sem("loaded"), S.sem("ready"), S.sem("stored")
        HC = CH // AD
        with nc.Block() as block:

            @block.sync
            def _(sp):
                sp.dma_start(Wv[:, :], I["L2_attn_Wv"]).then_inc(loaded, 16)

            @block.tensor
            def _(pe):
                pe.wait_ge(loaded, 16)
                for t in range(TPB):
                    for c in range(2):
                        i = t * 2 + c
                        if i >= 4:
                            pe.wait_ge(stored, i - 3)
                        pe.matmul(p[:, i % 4, :], xnT[:, b * SEQ + t * P:b * SEQ + (t + 1) * P], Wv[:, c * CH:(c + 1) * CH],
                                  start=True, stop=True).then_inc(ready, 1)

            @block.scalar
            def _(act):
                for t in range(TPB):
                    for c in range(2):
                        i = t * 2 + c
                        act.wait_ge(ready, i + 1)
                        act.copy(V[:, c * HC:(c + 1) * HC, t, 0:AD], p[:, i % 4, :].rearrange("p (h d) -> p h d", d=AD)
                                 ).then_inc(stored, 1)


def alibi_heads(nc, C, I, name, b, xnT, V, dist, slopes, X):
    NS = 2 * TPB
    SLOTS = 4
    SCHEDULE = []
    for t in range(TPB):
        SCHEDULE += [("S", 2 * t, 0), ("S", 2 * t + 1, 0), ("X", t, 0), ("T", (t - 1) % TPB, int(t == 0))]
        SCHEDULE += {0: [("V", 3, 1), ("Y", 0, 1), ("R", 0, 1)],
                     1: [("o", 0, 1), ("V", 4, 1), ("P", 0, 0)],
                     2: [("V", 5, 1), ("L", 0, 0), ("P", 1, 0)],
                     3: [("V", 6, 1), ("L", 1, 0), ("P", 2, 0)],
                     4: [("V", 7, 1), ("Y", 1, 1), ("L", 2, 0)],
                     5: [("V", 0, 0), ("P", 3, 0)],
                     6: [("V", 1, 0), ("o", 1, 1), ("L", 3, 0)],
                     7: [("V", 2, 0)]}[t]

    with Stage(nc, name) as S:
        wq = [S.sb(f"wq{k}", [P, 2 * AD]) for k in range(SLOTS)]
        wk = [S.sb(f"wk{k}", [P, 2 * AD]) for k in range(SLOTS)]
        wo = [S.sb(f"wo{k}", [P, D]) for k in range(SLOTS)]
        sums = [S.sb(f"sums{k}", [P, TPB]) for k in range(SLOTS)]
        recip = [S.sb(f"recip{k}", [P, TPB]) for k in range(SLOTS)]
        q1 = [S.sb(f"q1_{k}", [P, SEQ], F32R) for k in range(2)]
        k1 = [S.sb(f"k1_{k}", [P, SEQ], F32R) for k in range(2)]
        q2 = [S.sb(f"q2_{k}", [AD, SEQ], F32R) for k in range(2)]
        k2 = [S.sb(f"k2_{k}", [AD, SEQ], F32R) for k in range(2)]
        bias = [S.sb(f"bias{k}", [P, DIST0 + SEQ]) for k in range(2)]
        vals = [S.sb(f"vals{k}", [P, TPB, AD]) for k in range(2)]
        slope = S.sb("slope", [P, 1])
        start, zero = S.sb("start", [1, NS]), C.zeros[0:1, 0:1]
        half_max = S.sb("half_max", [P, TPB, 2])
        neg_max = S.sb("neg_max", [P, TPB])
        weights = [S.sb(f"weights{k}", [P, SEQ]) for k in range(2)]
        turned = [S.sb(f"turned{c}", [P, TPB, CH]) for c in range(2)]
        y = [S.sb(f"y{c}", [P, CH]) for c in range(2)]
        p_p = S.ps("p_p", [P, CH])
        p_s = [S.ps(f"p_s{k}", [P, CH]) for k in range(2)]
        p_t = [S.ps(f"p_t{k}", [P, CH]) for k in range(2)]
        p_y = [S.ps(f"p_y{c}", [P, CH]) for c in range(2)]
        p_x = S.ps("p_x", [P, CH])
        loaded = [S.sem(f"loaded{k}") for k in range(SLOTS)]
        sloped, bias_ready, vals_ready = S.sem("sloped"), S.sem("bias_ready"), S.sem("vals_ready")
        p_ready, high_done, low_done, q2_done = S.sem("p_ready"), S.sem("high_done"), S.sem("low_done"), S.sem("q2_done")
        s_ready, s_read, max_done, x_done = S.sem("s_ready"), S.sem("s_read"), S.sem("max_done"), S.sem("x_done")
        t_ready = [S.sem(f"t_ready{h}") for h in range(2)]
        t_stored = [S.sem(f"t_stored{h}") for h in range(2)]
        v_done, y_copied, r_done = S.sem("v_done"), S.sem("y_copied"), S.sem("r_done")
        o_ready, o_added = S.sem("o_ready"), S.sem("o_added")

        def steps(eng, step):
            step(0, 0)
            with eng.Fori(0, AH // SLOTS - 1) as i:
                for k in range(1, SLOTS + 1):
                    step(Count(i, SLOTS, k), k % SLOTS)
            for u in range(AH - SLOTS + 1, AH):
                step(u, u % SLOTS)

        def exists(u, ahead):
            return not isinstance(u, int) or 0 <= u + ahead < AH

        def entries(u, k):
            for what, n, before in SCHEDULE:
                if what in "PL":
                    if exists(u, 1):
                        yield what, n, u + 1, (k + 1) % SLOTS
                elif exists(u, -before):
                    yield what, n, u - before, (k - before) % SLOTS

        LEFT = [(what, n) for what, n, before in SCHEDULE if before]

        with nc.Block() as block:

            @block.sync
            def _(sp):
                def fetch(u, k):
                    for half in range(2):
                        cols = slice(half * AD, (half + 1) * AD)
                        head = ds(at_turn(u * AD), AD)
                        sp.dma_start(wq[k][:, cols], I["L2_attn_Wq"][:, head]).then_inc(loaded[k], 16)
                        sp.dma_start(wk[k][:, cols], I["L2_attn_Wk"][:, head]).then_inc(loaded[k], 16)
                        sp.dma_start(wo[k][cols, :], I["L2_attn_Wo"][head, :]).then_inc(loaded[k], 16)

                def step(u, k):
                    if exists(u, 3):
                        wait(sp, o_added, u * 2)
                        fetch(u + 3, (k + 3) % SLOTS)

                for u in range(3):
                    fetch(u, u)
                steps(sp, step)

            @block.gpsimd
            def _(pool):
                def prepare(u, k):
                    pool.tensor_copy(slope[:, :], slopes[:, ds(at_turn(u), 1)]).then_inc(sloped, 1)
                    wait(pool, sloped, u + 1)
                    wait(pool, s_read, (u - 1) * NS)
                    pool.tensor_tensor(bias[k % 2][:, :], dist[:, :], slope[:, 0:1].to_broadcast([P, DIST0 + SEQ]), ALU.mult
                                       ).then_inc(bias_ready, 1)
                    wait(pool, bias_ready, u + 1)
                    wait(pool, v_done, (u - 1) * TPB)
                    pool.tensor_copy(vals[k % 2][:, :, :], V[:, ds(at_turn(u), 1), :, :].rearrange("p u t d -> p (u t) d")
                                     ).then_inc(vals_ready, 1)

                def step(u, k):
                    if exists(u, 1):
                        prepare(u + 1, k + 1)

                prepare(0, 0)
                steps(pool, step)

            @block.tensor
            def _(pe):
                def project(u, k, j):
                    if j == 0:
                        wait(pe, loaded[k], (u - k) * (96 // SLOTS) + 96)
                    wait(pe, low_done, u * 4 + j)
                    at = b * SEQ + j % 2 * CH
                    pe.matmul(p_p[:, :], (wq if j < 2 else wk)[k][:, :], xnT[:, at:at + CH], start=True, stop=True
                              ).then_inc(p_ready, 1)

                def scores(u, k, g):
                    t, c = g // 2, g % 2
                    if g == 0:
                        wait(pe, low_done, u * 4 + 4)
                        wait(pe, q2_done, u * 2 + 2)
                    wait(pe, s_read, u * NS + g - 1)
                    keys = slice(c * CH, (c + 1) * CH)
                    queries = slice(t * P, (t + 1) * P)
                    pe.matmul(p_s[c][:, :], q1[k % 2][:, queries], k1[k % 2][:, keys], start=True, stop=False)
                    pe.matmul(p_s[c][:, :], q2[k % 2][:, queries], k2[k % 2][:, keys], start=False, stop=True
                              ).then_inc(s_ready, 1)

                def turn(u, t):
                    wait(pe, x_done, u * TPB + t + 1)
                    for h in range(2):
                        wait(pe, t_stored[h], u * TPB + t)
                        for j in range(TPC):
                            at = (h * TPC + j) * P
                            mm = pe.transpose(p_t[h][:, j * P:(j + 1) * P], weights[t % 2][:, at:at + P], C.ident[:, :])
                        mm.then_inc(t_ready[h], 1)

                def times_values(u, k, n):
                    c, pair = n // 4, n % 4
                    if pair == 0:
                        for h in range(2):
                            wait(pe, t_stored[h], u * TPB + (c + 1) * TPC)
                        wait(pe, vals_ready, u + 1)
                        wait(pe, y_copied, u * 2 + c - 1)
                    for half in range(2):
                        j = pair * 2 + half
                        mm = pe.matmul(p_y[c][half * AD:(half + 1) * AD, :], vals[k % 2][:, j, :], turned[c][:, j, :],
                                       start=(pair == 0), stop=(pair == 3), skip_group_check=True,
                                       tile_position=(0, half * AD))
                    mm.then_inc(v_done, 1)

                def output(u, k, c):
                    wait(pe, y_copied, u * 2 + c + 1)
                    wait(pe, o_added, u * 2 + c)
                    for t in range(TPC):
                        mm = pe.matmul(p_x[:, t * P:(t + 1) * P], y[c][:, t * P:(t + 1) * P], wo[k][:, :],
                                       start=True, stop=True)
                    mm.then_inc(o_ready, 1)

                def do(what, n, u, k):
                    if what == "S":
                        scores(u, k, n)
                    elif what == "T":
                        turn(u, n)
                    elif what == "V":
                        times_values(u, k, n)
                    elif what == "P":
                        project(u, k, n)
                    elif what == "o":
                        output(u, k, n)

                def step(u, k):
                    for entry in entries(u, k):
                        do(*entry)

                for j in range(4):
                    project(0, 0, j)
                steps(pe, step)
                for what, n in LEFT:
                    do(what, n, AH - 1, (AH - 1) % SLOTS)

            @block.scalar
            def _(act):
                def high_parts(u, k, j):
                    c = slice(j % 2 * CH, (j % 2 + 1) * CH)
                    wait(act, p_ready, u * 4 + j + 1)
                    if j == 0:
                        wait(act, s_ready, (u - 1) * NS)
                    if j < 2:
                        act.activation(q1[k % 2][:, c], p_p[:, :], ACT.Copy, scale=AD ** -0.5).then_inc(high_done, 1)
                        wait(act, high_done, u * 4 + j + 1)
                        act.copy(q2[k % 2][:, c], q1[k % 2][0:AD, c].bitcast(F32)).then_inc(q2_done, 1)
                    else:
                        act.copy(k1[k % 2][:, c], p_p[:, :]).then_inc(high_done, 1)

                def exp_tile(u, k, t):
                    wait(act, max_done, u * TPB + t + 1)
                    act.activation(weights[t % 2][:, :], weights[t % 2][:, :], ACT.Exp, bias=neg_max[:, t:t + 1],
                                   accum_out=sums[k][:, t:t + 1]).then_inc(x_done, 1)

                def store_turned(u, t):
                    c, at = t // TPC, t % TPC * P
                    if at == 0:
                        wait(act, v_done, (u - 1) * TPB + (c + 1) * 4)
                    wait(act, t_ready[0], u * TPB + t + 1)
                    act.copy(turned[c][:, 0:TPC, at:at + P], p_t[0][:, :].rearrange("p (t a) -> p t a", a=P)
                             ).then_inc(t_stored[0], 1)

                def copy_result(u, c):
                    wait(act, v_done, u * TPB + c * 4 + 4)
                    wait(act, o_ready, u * 2)
                    act.copy(y[c][:, :], p_y[c][:, :]).then_inc(y_copied, 1)

                def do(what, n, u, k):
                    if what == "P":
                        high_parts(u, k, n)
                    elif what == "X":
                        exp_tile(u, k, n)
                    elif what == "T":
                        store_turned(u, n)
                    elif what == "Y":
                        copy_result(u, n)

                def step(u, k):
                    for entry in entries(u, k):
                        do(*entry)

                for j in range(4):
                    high_parts(0, 0, j)
                steps(act, step)
                for what, n in LEFT:
                    do(what, n, AH - 1, (AH - 1) % SLOTS)

            @block.vector
            def _(dve):
                def low_parts(u, k, j):
                    c = slice(j % 2 * CH, (j % 2 + 1) * CH)
                    wait(dve, high_done, u * 4 + j + 1)
                    if j == 0:
                        wait(dve, s_ready, (u - 1) * NS)
                    if j < 2:
                        dve.scalar_tensor_tensor(out=q1[k % 2][AD:P, c], in0=p_p[AD:P, :], scalar=AD ** -0.5,
                                                 in1=q1[k % 2][AD:P, c].bitcast(F32), op0=ALU.mult, op1=ALU.subtract
                                                 ).then_inc(low_done, 1)
                    else:
                        dve.tensor_tensor(k2[k % 2][:, c], p_p[0:AD, :], k1[k % 2][0:AD, c].bitcast(F32), ALU.subtract
                                          ).then_inc(low_done, 1)

                def max_of(u, k, g):
                    t, c = g // 2, g % 2
                    if g == 0:
                        wait(dve, bias_ready, u + 1)
                    if c == 0:
                        wait(dve, t_ready[1], u * TPB + t - 1)
                    wait(dve, s_ready, u * NS + g + 1)
                    dve.tensor_copy(start[:, g:g + 1], zero[:, :])
                    at = DIST0 - t * P + c * CH
                    dve.tensor_tensor_reduce(weights[t % 2][:, c * CH:(c + 1) * CH], p_s[c][:, :],
                                             bias[k % 2][:, at:at + CH], 1.0, -3.0e38, ALU.add, ALU.max,
                                             half_max[:, t, c:c + 1]).then_inc(s_read, 1)
                    if c == 1:
                        wait(dve, s_read, u * NS + g + 1)
                        dve.tensor_reduce(neg_max[:, t:t + 1], half_max[:, t, :], AX, ALU.max, negate=True
                                          ).then_inc(max_done, 1)

                def store_turned(u, t):
                    c, at = t // TPC, t % TPC * P
                    if at == 0:
                        wait(dve, v_done, (u - 1) * TPB + (c + 1) * 4)
                    wait(dve, t_ready[1], u * TPB + t + 1)
                    dve.tensor_copy(turned[c][:, TPC:TPB, at:at + P], p_t[1][:, :].rearrange("p (t a) -> p t a", a=P)
                                    ).then_inc(t_stored[1], 1)

                def reciprocals(u, k):
                    wait(dve, x_done, (u + 1) * TPB)
                    dve.reciprocal(recip[k][:, :], sums[k][:, :]).then_inc(r_done, 1)

                def add_output(u, k, c):
                    wait(dve, r_done, u + 1)
                    wait(dve, o_ready, u * 2 + c + 1)
                    wait(dve, o_added, u * 2 + c)
                    for t in range(TPC):
                        tile = b * TPB + c * TPC + t
                        added = dve.scalar_tensor_tensor(out=X[:, tile, :], in0=p_x[:, t * P:(t + 1) * P],
                                                         scalar=recip[k][:, c * TPC + t:c * TPC + t + 1],
                                                         in1=X[:, tile, :], op0=ALU.mult, op1=ALU.add)
                    added.then_inc(o_added, 1)

                def do(what, n, u, k):
                    if what == "S":
                        max_of(u, k, n)
                    elif what == "T":
                        store_turned(u, n)
                    elif what == "L":
                        low_parts(u, k, n)
                    elif what == "R":
                        reciprocals(u, k)
                    elif what == "o":
                        add_output(u, k, n)

                def step(u, k):
                    for entry in entries(u, k):
                        do(*entry)

                for j in range(4):
                    low_parts(0, 0, j)
                steps(dve, step)
                for what, n in LEFT:
                    do(what, n, AH - 1, (AH - 1) % SLOTS)


def add_turned(nc, C, name, X, outT):
    with Stage(nc, name) as S:
        p = S.ps("p", [P, NCH, CH])
        ready = S.sem("ready")
        with nc.Block() as block:

            @block.tensor
            def _(pe):
                for g in range(NCH):
                    for k in range(TPC):
                        t = g * TPC + k
                        mm = pe.transpose(p[:, g, k * P:(k + 1) * P], outT[:, t * P:(t + 1) * P], C.ident[:, :])
                    mm.then_inc(ready, 1)

            @block.vector
            def _(dve):
                for g in range(NCH):
                    t = slice(g * TPC, (g + 1) * TPC)
                    dve.wait_ge(ready, g + 1)
                    dve.tensor_tensor(X[:, t, :], X[:, t, :], p[:, g, :].rearrange("p (t d) -> p t d", d=D), ALU.add)


TWO_PI = (6.28125, 0.0019350051879882812, 3.0199159819567e-07)
ROUND = 1.5 * 2.0 ** 23


def resonant_mixer(nc, C, I, X, xn):
    with Stage(nc, "mix3") as S:
        rows = S.sb("rows", [P, 3, D])
        gamma = S.sb("gamma", [P, D])
        turns = S.sb("turns", [P, D])
        angle = S.sb("angle", [P, D])
        re_c = S.sb("re_c", [P, D])
        past0 = S.sb("past0", [P, D])
        past1 = S.sb("past1", [P, D])
        y0 = S.sb("y0", [P, TPB, D])
        y1 = S.sb("y1", [P, TPB, D])
        loaded, own, own_act, own_pool = S.sem("loaded"), S.sem("own"), S.sem("own_act"), S.sem("own_pool")
        decayed, reduced, cos_done, past_done = S.sem("decayed"), S.sem("reduced"), S.sem("cos_done"), S.sem("past_done")
        x0, x1 = xn[:, 0:TPB, :], xn[:, TPB:NT, :]
        with nc.Block() as block:

            @block.sync
            def _(sp):
                for j, row in enumerate(("lmlg", "theta", "last_conv_init")):
                    sp.dma_start(rows[:, j, :], I["L3_attn_" + row].partition_broadcast(P)).then_inc(loaded, 16)

            @block.scalar
            def _(act):
                chain = Chain(act, own_act)
                act.wait_ge(loaded, 48)
                chain.step(act.activation(gamma[:, :], rows[:, 0, :], ACT.Exp))
                act.activation(gamma[:, :], gamma[:, :], ACT.Exp, scale=-1.0).then_inc(decayed, 1)
                act.wait_ge(reduced, 1)
                act.activation(re_c[:, :], angle[:, :], ACT.Sin).then_inc(cos_done, 1)

            @block.vector
            def _(dve):
                chain = Chain(dve, own)
                dve.wait_ge(loaded, 48)
                chain.step(dve.tensor_scalar(turns[:, :], rows[:, 1, :], float(1.0 / (2 * np.pi)), None, ALU.mult))
                chain.step(dve.tensor_scalar(turns[:, :], turns[:, :], ROUND, None, ALU.add))
                chain.step(dve.tensor_scalar(turns[:, :], turns[:, :], -ROUND, None, ALU.add))
                chain.step(dve.tensor_copy(angle[:, :], rows[:, 1, :]))
                for part in TWO_PI:
                    chain.step(dve.scalar_tensor_tensor(out=angle[:, :], in0=turns[:, :], scalar=-part, in1=angle[:, :],
                                                        op0=ALU.mult, op1=ALU.add))
                chain.step(dve.tensor_scalar(turns[:, :], angle[:, :], -1.0, None, ALU.mult))
                chain.step(dve.tensor_tensor(angle[:, :], angle[:, :], turns[:, :], ALU.max))
                dve.tensor_scalar(angle[:, :], angle[:, :], -1.0, float(np.pi / 2), ALU.mult, ALU.add).then_inc(reduced, 1)
                dve.wait_ge(decayed, 1)
                dve.wait_ge(cos_done, 1)
                chain.step(dve.tensor_tensor(re_c[:, :], re_c[:, :], gamma[:, :], ALU.mult))
                chain.step(dve.tensor_tensor(past0[:, :], re_c[:, :], rows[:, 2, :], ALU.mult))
                chain.step(dve.tensor_tensor(past1[:, :], re_c[:, :], re_c[:, :], ALU.mult))
                chain.step(dve.tensor_tensor(gamma[:, :], gamma[:, :], gamma[:, :], ALU.mult))
                chain.step(dve.scalar_tensor_tensor(out=past1[:, :], in0=past1[:, :], scalar=2.0, in1=gamma[:, :],
                                                    op0=ALU.mult, op1=ALU.subtract))
                dve.tensor_tensor(past1[:, :], past1[:, :], rows[:, 2, :], ALU.mult).then_inc(past_done, 1)
                dve.wait_ge(past_done, 1)
                chain.step(dve.tensor_tensor(y1[:, :, :], x0, per_feature(re_c[:, :], TPB), ALU.mult))
                chain.step(dve.tensor_tensor(y1[:, :, :], y1[:, :, :], per_feature(past1[:, :], TPB), ALU.add))
                chain.step(dve.tensor_tensor(y1[:, :, :], y1[:, :, :], x1, ALU.add))
                chain.step(dve.tensor_tensor(y1[:, :, :], y1[:, :, :], x1, ALU.mult))
                dve.tensor_tensor(X[:, TPB:NT, :], X[:, TPB:NT, :], y1[:, :, :], ALU.add)

            @block.gpsimd
            def _(pool):
                chain = Chain(pool, own_pool)
                pool.wait_ge(past_done, 1)
                chain.step(pool.tensor_tensor(y0[:, :, :], x0, per_feature(past0[:, :], TPB), ALU.add))
                chain.step(pool.tensor_tensor(y0[:, :, :], y0[:, :, :], x0, ALU.mult))
                pool.tensor_tensor(X[:, 0:TPB, :], X[:, 0:TPB, :], y0[:, :, :], ALU.add)


SE = 16
SLOT = 64
NSLOT = SE * SLOT
ST = NSLOT // P
SFF = 256
MSF = SFF // P


def slot_directions(nc, C, I, seT):
    with Stage(nc, "slots") as S:
        raw = S.sb("raw", [P, ST, D])
        gamma, beta, scale = S.sb("gamma", [P, D]), S.sb("beta", [P, D]), S.sb("scale", [P, 1])
        load(nc, "slots_load", [(raw[:, :, :], I["L3_ffn_slot_embeds"].rearrange("e s d -> (e s) d").rearrange(
                                    "(t p) d -> p t d", p=P)),
                                (gamma[:, :], I["L3_ffn_slot_g"].partition_broadcast(P)),
                                (beta[:, :], I["L3_ffn_slot_b"].partition_broadcast(P)),
                                (scale[:, :], I["L3_ffn_scale"].partition_broadcast(P))])
        with nc.Block() as block:

            @block.vector
            def _(dve):
                dve.tensor_scalar(gamma[:, :], gamma[:, :], scale[:, 0:1], None, ALU.mult)
                dve.tensor_scalar(beta[:, :], beta[:, :], scale[:, 0:1], None, ALU.mult)

        normalise(nc, C, "slots_norm", raw, raw, seT, gamma=gamma[:, :], beta=beta[:, :], tiles=ST)


def soft_moe_ffn(nc, C, I, name, X, xn, xnT, seT):
    with Stage(nc, name) as M:
        gamma, beta = M.sb("gamma", [P, D]), M.sb("beta", [P, D])
        slotsT = M.sb("slotsT", [P, SE, BATCH, SLOT])
        eout = M.sb("eout", [P, BATCH, ST, D])
        outT = M.sb("outT", [P, TOK])
        load(nc, name + "_load", [(gamma[:, :], I["L3_ffn_norm_g"].partition_broadcast(P)),
                                  (beta[:, :], I["L3_ffn_norm_b"].partition_broadcast(P))])
        normalise(nc, C, name + "_norm", xn, xn, xnT, gamma=gamma[:, :], beta=beta[:, :])
        def half(x, b):
            return x[:, b * SEQ:(b + 1) * SEQ]

        softmax_apply(nc, C, name + "_in", lambda b: seT, lambda b: half(xnT, b),
                      lambda b: xn[:, b * TPB:(b + 1) * TPB, :], lambda b: slotsT[:, :, b, :], 1.0)
        slot_experts(nc, C, I, name + "_exp", slotsT, eout)
        softmax_apply(nc, C, name + "_out", lambda b: half(xnT, b), lambda b: seT, lambda b: eout[:, b, :, :],
                      lambda b: half(outT, b).rearrange("p (e s) -> p e s", s=SLOT), 0.5)
        add_turned(nc, C, name + "_add", X, outT)


def softmax_apply(nc, C, name, A, B, W, dst, factor):
    GT = TPC
    TILES = BATCH * TPB
    GROUPS = TILES // GT
    with Stage(nc, name) as S:
        neg_max = [S.sb(f"neg_max{k}", [P, 1]) for k in range(2)]
        total = [S.sb(f"total{k}", [P, 1]) for k in range(2)]
        recip = [S.sb(f"recip{k}", [P, 1]) for k in range(2)]
        e = [S.sb(f"e{k}", [P, SEQ]) for k in range(2)]
        turned = [S.sb(f"turned{k}", [P, TPB, CH]) for k in range(2)]
        p_s = [S.ps(f"p_s{k}", [P, SEQ]) for k in range(2)]
        p_t = [S.ps(f"p_t{k}", [P, CH]) for k in range(2)]
        p_w = S.ps("p_w", [P, CH])
        s_ready, max_done, exp_done = S.sem("s_ready"), S.sem("max_done"), S.sem("exp_done")
        recip_done, e_ready = S.sem("recip_done"), S.sem("e_ready")
        t_ready = [S.sem(f"t_ready{h}") for h in range(2)]
        t_stored = [S.sem(f"t_stored{h}") for h in range(2)]
        w_ready, w_stored = S.sem("w_ready"), S.sem("w_stored")

        def place(i, h):
            return turned[i // GT % 2][:, h * 4:h * 4 + 4, i % GT * P:(i % GT + 1) * P]

        with nc.Block() as block:

            @block.tensor
            def _(pe):
                def scores(i):
                    if i >= TILES:
                        return
                    b, t = i // TPB, i % TPB
                    wait(pe, exp_done, i - 1)
                    for c in range(2):
                        mm = pe.matmul(p_s[i % 2][:, c * CH:(c + 1) * CH], A(b)[:, t * P:(t + 1) * P],
                                       B(b)[:, c * CH:(c + 1) * CH], start=True, stop=True)
                    mm.then_inc(s_ready, 1)

                def turn(i):
                    wait(pe, e_ready, i + 1)
                    for h in range(2):
                        wait(pe, t_stored[h], i)
                        for j in range(4):
                            at = (h * 4 + j) * P
                            mm = pe.transpose(p_t[h][:, j * P:(j + 1) * P], e[i % 2][:, at:at + P], C.ident[:, :])
                        mm.then_inc(t_ready[h], 1)

                def weigh(g, piece):
                    if piece == 0:
                        wait(pe, w_stored, g)
                        for h in range(2):
                            wait(pe, t_stored[h], (g + 1) * GT)
                    for k in (2 * piece, 2 * piece + 1):
                        mm = pe.matmul(p_w[:, :], W(g * GT // TPB)[:, k, :], turned[g % 2][:, k, :], start=(k == 0),
                                       stop=(k == TPB - 1))
                    if piece == GT - 1:
                        mm.then_inc(w_ready, 1)

                scores(0)
                scores(1)
                for i in range(TILES):
                    turn(i)
                    scores(i + 2)
                    if i >= GT:
                        weigh(i // GT - 1, i % GT)
                for piece in range(GT):
                    weigh(GROUPS - 1, piece)

            @block.scalar
            def _(act):
                def exp(i):
                    if i < TILES:
                        wait(act, max_done, i + 1)
                        wait(act, t_ready[1], i - 1)
                        act.activation(e[i % 2][:, :], p_s[i % 2][:, :], ACT.Exp, bias=neg_max[i % 2][:, 0:1],
                                       accum_out=total[i % 2][:, 0:1]).then_inc(exp_done, 1)

                exp(0)
                exp(1)
                for i in range(TILES):
                    wait(act, t_ready[1], i + 1)
                    wait(act, w_ready, i // GT - 1)
                    act.copy(place(i, 1), p_t[1][:, :].rearrange("p (t a) -> p t a", a=P)).then_inc(t_stored[1], 1)
                    exp(i + 2)

            @block.vector
            def _(dve):
                def maximum(i):
                    if i < TILES:
                        wait(dve, s_ready, i + 1)
                        dve.tensor_reduce(neg_max[i % 2][:, 0:1], p_s[i % 2][:, :], AX, ALU.max, negate=True
                                          ).then_inc(max_done, 1)

                def store(g):
                    wait(dve, w_ready, g + 1)
                    b, half = g * GT // TPB, g % (TPB // GT)
                    dve.tensor_copy(dst(b)[:, half * 8:(half + 1) * 8, :], p_w[:, :].rearrange("p (e s) -> p e s", s=SLOT)
                                    ).then_inc(w_stored, 1)

                def divide(i):
                    if i < TILES:
                        wait(dve, exp_done, i + 1)
                        dve.reciprocal(recip[i % 2][:, 0:1], total[i % 2][:, 0:1]).then_inc(recip_done, 1)
                        wait(dve, recip_done, i + 1)
                        dve.tensor_scalar(e[i % 2][:, :], e[i % 2][:, :], recip[i % 2][:, 0:1], factor, ALU.mult, ALU.mult
                                          ).then_inc(e_ready, 1)

                maximum(0)
                maximum(1)
                divide(0)
                for i in range(TILES):
                    divide(i + 1)
                    wait(dve, t_ready[0], i + 1)
                    wait(dve, w_ready, i // GT - 1)
                    dve.tensor_copy(place(i, 0), p_t[0][:, :].rearrange("p (t a) -> p t a", a=P)).then_inc(t_stored[0], 1)
                    if i >= GT and i % GT == GT - 1:
                        store(i // GT - 1)
                    maximum(i + 2)
                store(GROUPS - 1)


def slot_experts(nc, C, I, name, slotsT, eout):
    K = 4
    with Stage(nc, name) as S:
        wg = [S.sb(f"wg{k}", [P, SFF]) for k in range(K)]
        wu = [S.sb(f"wu{k}", [P, SFF]) for k in range(K)]
        wd = [S.sb(f"wd{k}", [P, MSF, D]) for k in range(K)]
        b_rows = S.sb("b_rows", [2 * SE * MSF, P])
        b_cols = S.sb("b_cols", [P, 2, SE * MSF])
        bias = [S.sb(f"bias{k}", [P, 2, MSF]) for k in range(2)]
        bd = S.sb("bd", [P, ST, D])
        gate = [S.sb(f"gate{k}", [P, MSF, P]) for k in range(2)]
        hidden = [S.sb(f"hidden{k}", [P, MSF, P]) for k in range(2)]
        p_up = [S.ps(f"p_up{k}", [P, 2, MSF, P]) for k in range(2)]
        p_out = [S.ps(f"p_out{k}", [P, BATCH, CH // 2]) for k in range(2)]
        p_b = S.ps("p_b", [P, CH])
        loaded = [S.sem(f"loaded{k}") for k in range(K)]
        b_loaded, b_turned, b_stored = S.sem("b_loaded"), S.sem("b_turned"), S.sem("b_stored")
        b_set, up_ready, gate_done, hidden_done = S.sem("b_set"), S.sem("up_ready"), S.sem("gate_done"), S.sem("hidden_done")
        down_done, stored = S.sem("down_done"), S.sem("stored")
        with nc.Block() as block:

            @block.sync
            def _(sp):
                def fetch(e, k):
                    sp.dma_start(wg[k][:, :], I["L3_ffn_Wg"][ds(e, 1)].rearrange("e d f -> d (e f)")).then_inc(loaded[k], 16)
                    sp.dma_start(wu[k][:, :], I["L3_ffn_Wu"][ds(e, 1)].rearrange("e d f -> d (e f)")).then_inc(loaded[k], 16)
                    sp.dma_start(wd[k][:, :, :], I["L3_ffn_Wd"][ds(e, 1)].rearrange("e (m p) d -> p (e m) d", p=P)
                                 ).then_inc(loaded[k], 16)

                sp.dma_start(b_rows[0:SE * MSF, :], I["L3_ffn_bg"].rearrange("e (m p) -> (e m) p", p=P)).then_inc(b_loaded, 16)
                sp.dma_start(b_rows[SE * MSF:, :], I["L3_ffn_bu"].rearrange("e (m p) -> (e m) p", p=P)).then_inc(b_loaded, 16)
                for h in range(2):
                    sp.dma_start(bd[h * SLOT:(h + 1) * SLOT, :, :],
                                 I["L3_ffn_bd"].rearrange("(t h) d -> h t d", h=2)[h].partition_broadcast(SLOT)
                                 ).then_inc(b_loaded, 16)
                for k in range(K):
                    fetch(k, k)
                with sp.Fori(0, SE // K - 1) as i:
                    for k in range(K):
                        sp.wait_ge(down_done, i * K + k + 1)
                        fetch(i * K + K + k, k)

            @block.tensor
            def _(pe):
                def up(i, k):
                    e = i * K + k
                    pe.wait_ge(loaded[k], i * 48 + 48)
                    pe.wait_ge(hidden_done, e - 1 if k > 1 else i * K)
                    for j, w in enumerate((wg, wu)):
                        for m in range(MSF):
                            mm = pe.matmul(p_up[k % 2][:, j, m, :], w[k][:, m * P:(m + 1) * P], slotsT[:, ds(e, 1), :, :],
                                           start=True, stop=True)
                    mm.then_inc(up_ready, 1)

                def down(i, k):
                    pe.wait_ge(hidden_done, i * K + k + 1)
                    if k % 2 == 0:
                        pe.wait_ge(stored, i * 2 + k // 2 - 1 if k // 2 > 1 else i * 2)
                    h = slice(k % 2 * SLOT, (k % 2 + 1) * SLOT)
                    for b in range(BATCH):
                        for m in range(MSF):
                            mm = pe.matmul(p_out[k // 2][h, b, 0:D], hidden[k % 2][:, m, b * SLOT:(b + 1) * SLOT],
                                           wd[k][:, m, :], start=(m == 0), stop=(m == MSF - 1),
                                           tile_position=(0, k % 2 * SLOT))
                    mm.then_inc(down_done, 1)

                pe.wait_ge(b_loaded, 64)
                pe.transpose(p_b[:, 0:2 * SE * MSF], b_rows[:, :], C.ident[0:2 * SE * MSF, 0:2 * SE * MSF]
                             ).then_inc(b_turned, 1)
                with pe.Fori(0, SE // K) as i:
                    up(i, 0)
                    for k in range(K):
                        if k + 1 < K:
                            up(i, k + 1)
                        down(i, k)

            @block.scalar
            def _(act):
                with act.Fori(0, SE // K) as i:
                    for k in range(K):
                        e = i * K + k
                        act.wait_ge(b_set, e + 1)
                        act.wait_ge(up_ready, e + 1)
                        for m in range(MSF):
                            ins = act.activation(gate[k % 2][:, m, :], p_up[k % 2][:, 0, m, :], ACT.Gelu,
                                                 bias=bias[k % 2][:, 0, m:m + 1])
                        ins.then_inc(gate_done, 1)

            @block.vector
            def _(dve):
                dve.wait_ge(b_turned, 1)
                dve.tensor_copy(b_cols[:, :, :], p_b[:, 0:2 * SE * MSF].rearrange("p (j c) -> p j c", j=2)
                                ).then_inc(b_stored, 1)
                dve.wait_ge(b_stored, 1)
                with dve.Fori(0, SE // K) as i:
                    def set_bias(k):
                        e = i * K + k
                        dve.wait_ge(hidden_done, e - 1 if k > 1 else i * K)
                        dve.tensor_copy(bias[k % 2][:, :, :], b_cols[:, :, ds(e * MSF, MSF)]).then_inc(b_set, 1)

                    set_bias(0)
                    for k in range(K):
                        e = i * K + k
                        if k + 1 < K:
                            set_bias(k + 1)
                        dve.wait_ge(gate_done, e + 1)
                        dve.wait_ge(b_set, e + 1)
                        dve.wait_ge(down_done, e - 1 if k > 1 else i * K)
                        for m in range(MSF):
                            ins = dve.scalar_tensor_tensor(out=hidden[k % 2][:, m, :], in0=p_up[k % 2][:, 1, m, :],
                                                           scalar=bias[k % 2][:, 1, m:m + 1], in1=gate[k % 2][:, m, :],
                                                           op0=ALU.add, op1=ALU.mult)
                        ins.then_inc(hidden_done, 1)
                        if k % 2:
                            dve.wait_ge(down_done, e + 1)
                            t = i * 2 + k // 2
                            for b in range(BATCH):
                                ins = dve.tensor_tensor(eout[:, b, ds(t, 1), :], p_out[k // 2][:, b, 0:D].unsqueeze(1), bd[:, ds(t, 1), :],
                                                        ALU.add)
                            ins.then_inc(stored, 1)


def build_program(nc, I, out):
    with ExitStack() as stack:
        class C:
            pass

        def sb(name, shape, dt=F32):
            return stack.enter_context(nc.sbuf_tensor(name, shape, dt))

        C.ident = sb("ident", [P, P])
        C.ones = sb("ones", [P, P])
        C.zeros = sb("zeros", [P, P])
        C.half = sb("half", [P, NT])
        C.neg_half = sb("neg_half", [P, NT])
        C.rms_eps = sb("rms_eps", [P, NT])
        C.neg_one = sb("neg_one", [P, NT])
        X = sb("X", [P, NT, D])
        xn = sb("xn", [P, NT, D])
        xnT = sb("xnT", [P, TOK])
        constants(nc, C)
        load_inputs(nc, I, X)

        def layer_norm(name):
            normalise(nc, C, name, X, xn, xnT)

        with Stage(nc, "ffn0") as S:
            up, down = S.sb("up", [P, DFF]), S.sb("down", [P, MFF, D])
            b1, b2 = S.sb("b1", [P, MFF]), S.sb("b2", [1, D])
            ternary_weights(nc, C, "ffn0_w", I["L0_ffn_W1"], I["L0_ffn_W2"], 1e-8, up, down)
            load(nc, "ffn0_b", [(b1[:, :], I["L0_ffn_b1"].rearrange("(m p) -> p m", p=P)),
                                (b2[:, :], I["L0_ffn_b2"].unsqueeze(0))])
            layer_norm("ln0a")
            ffn(nc, C, "ffn0a", X, xnT, up, down, b1, b2[0:1, :])
            layer_norm("ln0b")
            gated_scan_mixer(nc, C, I, X, xn, xnT)
            layer_norm("ln0c")
            ffn(nc, C, "ffn0b", X, xnT, up, down, b1, b2[0:1, :])
        layer_norm("ln1a")
        moe_ffn(nc, C, I, "moe_a", X, xnT)
        layer_norm("ln1b")
        stacked_attention_mixer(nc, C, I, X, xn, xnT)
        layer_norm("ln1c")
        moe_ffn(nc, C, I, "moe_b", X, xnT)
        with Stage(nc, "ffn2") as S:
            up, down = S.sb("up", [P, DFF]), S.sb("down", [P, MFF, D])
            ternary_weights(nc, C, "ffn2_w", I["L2_ffn_w_up"], I["L2_ffn_w_down"], 0.0, up, down)
            layer_norm("ln2a")
            normalise(nc, C, "ln2a_rms", xn, xn, xnT, kind="rms")
            ffn(nc, C, "ffn2a", X, xnT, up, down, rms=True)
            layer_norm("ln2b")
            alibi_attention_mixer(nc, C, I, X, xn, xnT)
            layer_norm("ln2c")
            normalise(nc, C, "ln2c_rms", xn, xn, xnT, kind="rms")
            ffn(nc, C, "ffn2b", X, xnT, up, down, rms=True)
        with Stage(nc, "ffn3") as S:
            seT = S.sb("seT", [P, NSLOT])
            slot_directions(nc, C, I, seT)
            layer_norm("ln3a")
            soft_moe_ffn(nc, C, I, "ffn3a", X, xn, xnT, seT)
            layer_norm("ln3b")
            resonant_mixer(nc, C, I, X, xn)
            layer_norm("ln3c")
            soft_moe_ffn(nc, C, I, "ffn3b", X, xn, xnT, seT)
        store_outputs(nc, X, out)


def load(nc, name, pairs):
    with Stage(nc, name) as S:
        loaded = S.sem("loaded")
        with nc.Block() as block:

            @block.sync
            def _(sp):
                for dst, src in pairs:
                    sp.dma_start(dst, src, allow_slow_non_contiguous=True).then_inc(loaded, 16)
                sp.wait_ge(loaded, 16 * len(pairs))


def load_inputs(nc, I, X):
    load(nc, "load_x", [(X[:, b * TPB:(b + 1) * TPB, :], I["L0_attn_x"][b].rearrange("(t p) d -> p t d", p=P))
                        for b in range(BATCH)])


def store_outputs(nc, X, out):
    with Stage(nc, "store_x") as S:
        stored = S.sem("stored")
        with nc.Block() as block:

            @block.sync
            def _(sp):
                for b in range(BATCH):
                    sp.dma_start(out[b].rearrange("(t p) d -> p t d", p=P),
                                 X[:, b * TPB:(b + 1) * TPB, :]).then_inc(stored, 16)
                sp.wait_ge(stored, 16 * BATCH)


_INS = ['L0_attn_x', 'L0_attn_Wq', 'L0_attn_Wk', 'L0_attn_Wv', 'L0_attn_Wf', 'L0_attn_bf', 'L0_attn_Wg',
        'L0_attn_Wout', 'L0_attn_gamma', 'L0_attn_beta', 'L0_ffn_W1', 'L0_ffn_b1', 'L0_ffn_W2', 'L0_ffn_b2',
        'L1_attn_W_attn', 'L1_attn_b_attn', 'L1_attn_W_k2', 'L1_attn_b_k2', 'L1_attn_W_proj', 'L1_attn_b_proj',
        'L1_ffn_Wr', 'L1_ffn_br', 'L1_ffn_W1', 'L1_ffn_b1', 'L1_ffn_W2', 'L1_ffn_b2', 'L2_attn_ln_gamma',
        'L2_attn_ln_beta', 'L2_attn_Wq', 'L2_attn_Wk', 'L2_attn_Wv', 'L2_attn_Wo', 'L2_ffn_w_up', 'L2_ffn_w_down',
        'L3_attn_lmlg', 'L3_attn_theta', 'L3_attn_last_conv_init', 'L3_ffn_norm_g', 'L3_ffn_norm_b',
        'L3_ffn_slot_g', 'L3_ffn_slot_b', 'L3_ffn_scale', 'L3_ffn_slot_embeds', 'L3_ffn_Wg', 'L3_ffn_bg',
        'L3_ffn_Wu', 'L3_ffn_bu', 'L3_ffn_Wd', 'L3_ffn_bd']


def kernel(**inputs):
    import numpy as _np
    import concourse.bacc as _bacc
    from concourse import mybir as _mybir
    from concourse.bass_utils import run_bass_kernel_spmd as _run

    nc = _bacc.Bacc("TRN2", target_bir_lowering=False, num_devices=1)
    arrays, ins = {}, {}
    for name in _INS:
        a = _np.ascontiguousarray(inputs[name])
        arrays[f"in_{name}_dram"] = a
        ins[name] = nc.dram_tensor(f"in_{name}_dram", a.shape, _mybir.dt.from_np(a.dtype), kind="ExternalInput").ap()
    out = nc.dram_tensor("out_0_dram", (BATCH, SEQ, D), _mybir.dt.float32, kind="ExternalOutput").ap()
    build_program(nc, ins, out)
    r = _run(nc, [arrays], core_ids=[0])
    return r.results[0]["out_0_dram"]
```

```python
from contextlib import ExitStack

import numpy as np

import concourse.bass as bass
from concourse import mybir

F32 = mybir.dt.float32
F32R = mybir.dt.float32r
BF16 = mybir.dt.bfloat16
ALU = mybir.AluOpType
ACT = mybir.ActivationFunctionType
AX = mybir.AxisListType.X

P = 128
D = 128
BATCH, SEQ = 2, 1024
TOK = BATCH * SEQ
NT = TOK // P
TPB = SEQ // P
CH = 512
NCH = TOK // CH
TPC = CH // P
DFF = 4 * D
MFF = DFF // P
LN_EPS = 1e-5
RMS_EPS = 1e-8
BIG = 1.0e30
ds = bass.ds


class Stage:

    def __init__(self, nc, name):
        self.nc, self.name, self.stack, self.sems = nc, name, ExitStack(), []

    def __enter__(self):
        return self

    def __exit__(self, *err):
        self.stack.close()
        if self.sems:
            self.nc.clear_and_free_semaphores(self.sems)
            self.nc.all_engine_barrier()

    def sb(self, name, shape, dt=F32):
        return self.stack.enter_context(self.nc.sbuf_tensor(f"{self.name}_{name}", shape, dt))

    def ps(self, name, shape, dt=F32):
        return self.stack.enter_context(self.nc.psum_tensor(f"{self.name}_{name}", shape, dt))

    def sem(self, name):
        self.sems.append(self.nc.alloc_semaphore(name=f"{self.name}_{name}"))
        return self.sems[-1]


class Chain:

    def __init__(self, eng, sem, first=0):
        self.eng, self.sem, self.first, self.n = eng, sem, first, 0

    def step(self, ins):
        ins.then_inc(self.sem, 1)
        self.n += 1
        self.eng.wait_ge(self.sem, self.first + self.n)


class Count:

    def __init__(self, i, times, plus):
        self.i, self.times, self.plus = i, times, plus

    def __mul__(self, n):
        return Count(self.i, self.times * n, self.plus * n)

    def __add__(self, n):
        return Count(self.i, self.times, self.plus + n)

    def __sub__(self, n):
        return self + -n

    def value(self):
        return self.i * self.times + self.plus


def at_turn(value):
    return value.value() if isinstance(value, Count) else value


def wait(eng, sem, value):
    if not (isinstance(value, int) and value <= 0):
        eng.wait_ge(sem, at_turn(value))


def per_token(col, width):
    n = col.shape[1]
    return col.unsqueeze(2).to_broadcast([P, n, width])


def per_feature(row, tiles):
    return row.unsqueeze(1).to_broadcast([P, tiles, row.shape[1]])


def constants(nc, C):
    with Stage(nc, "const") as S:
        made = S.sem("made")
        with nc.Block() as block:

            @block.gpsimd
            def _(pool):
                chain = Chain(pool, made)
                chain.step(pool.memset(C.ident[:, :], 0.0))
                chain.step(pool.affine_select(out=C.ident[:, :], in_=C.ident[:, :], compare_op=ALU.not_equal,
                                              fill=1.0, base=0, pattern=[[-1, P]], channel_multiplier=1))
                pool.memset(C.ones[:, :], 1.0)
                pool.memset(C.zeros[:, :], 0.0)
                pool.memset(C.rms_eps[:, :], RMS_EPS)
                pool.memset(C.neg_half[:, :], -0.5)
                pool.memset(C.half[:, :], 0.5)
                chain.step(pool.memset(C.neg_one[:, :], -1.0))


def normalise(nc, C, name, src, dst, dstT=None, kind="layer", gamma=None, beta=None, tiles=NT):
    G = 4
    TG = tiles // G
    with Stage(nc, name) as S:
        sums = S.sb("sums", [P, tiles])
        neg_mean = S.sb("neg_mean", [P, tiles])
        square = S.sb("square", [P, tiles, D])
        sumsq = S.sb("sumsq", [P, tiles])
        var = S.sb("var", [P, tiles])
        root = S.sb("root", [P, tiles])
        rstd = S.sb("rstd", [P, tiles])
        turned = S.ps("turned", [P, G, CH])
        own = S.sem("own")
        centred = S.sem("centred")
        squared = S.sem("squared")
        summed = S.sem("summed")
        own_pool = S.sem("own_pool")
        scaled = S.sem("scaled")
        normed = S.sem("normed")
        turned_ok = S.sem("turned_ok")
        stored = S.sem("stored")
        with nc.Block() as block:

            @block.vector
            def _(dve):
                chain = Chain(dve, own)
                for g in range(G):
                    t = slice(g * TG, (g + 1) * TG)
                    if kind == "layer":
                        chain.step(dve.tensor_reduce(sums[:, t], src[:, t, :], AX, ALU.add))
                        dve.tensor_scalar(neg_mean[:, t], sums[:, t], -1.0 / D, None, ALU.mult).then_inc(centred, 1)
                if kind == "rms":
                    for g in range(G):
                        t = slice(g * TG, (g + 1) * TG)
                        dve.wait_ge(squared, g + 1)
                        dve.tensor_reduce(sumsq[:, t], square[:, t, :], AX, ALU.add).then_inc(summed, 1)
                for g in range(G):
                    t = slice(g * TG, (g + 1) * TG)
                    dve.wait_ge(scaled, g + 1)
                    if kind == "layer":
                        dve.wait_ge(centred, g + 1)
                    if kind == "layer":
                        for n in range(g * TG, (g + 1) * TG):
                            last = dve.tensor_scalar(dst[:, n, :], src[:, n, :], neg_mean[:, n:n + 1], rstd[:, n:n + 1],
                                                     ALU.add, ALU.mult)
                    else:
                        last = dve.tensor_tensor(dst[:, t, :], src[:, t, :], per_token(rstd[:, t], D), ALU.mult)
                    if gamma is not None:
                        chain.step(last)
                        chain.step(dve.tensor_tensor(dst[:, t, :], dst[:, t, :], per_feature(gamma, TG), ALU.mult))
                        last = dve.tensor_tensor(dst[:, t, :], dst[:, t, :], per_feature(beta, TG), ALU.add)
                    last.then_inc(normed, 1)

            @block.scalar
            def _(act):
                for g in range(G):
                    if kind == "layer":
                        act.wait_ge(centred, g + 1)
                        for n in range(g * TG, (g + 1) * TG):
                            ins = act.activation(square[:, n, :], src[:, n, :], ACT.Square, bias=neg_mean[:, n:n + 1],
                                                 accum_out=sumsq[:, n:n + 1])
                        ins.then_inc(summed, 1)
                    else:
                        t = slice(g * TG, (g + 1) * TG)
                        act.activation(square[:, t, :], src[:, t, :], ACT.Square).then_inc(squared, 1)
                if dstT is not None:
                    for g in range(G):
                        act.wait_ge(turned_ok, g + 1)
                        act.copy(dstT[:, g * TG * P:(g + 1) * TG * P], turned[:, g, 0:TG * P]).then_inc(stored, 1)

            @block.gpsimd
            def _(pool):
                chain = Chain(pool, own_pool)
                for g in range(G):
                    t = slice(g * TG, (g + 1) * TG)
                    pool.wait_ge(summed, g + 1)
                    if kind == "layer":
                        chain.step(pool.tensor_scalar(var[:, t], sumsq[:, t], 1.0 / D, LN_EPS, ALU.mult, ALU.add))
                        pool.tensor_tensor(rstd[:, t], var[:, t], C.neg_half[:, 0:TG], ALU.pow).then_inc(scaled, 1)
                    else:
                        chain.step(pool.tensor_scalar(var[:, t], sumsq[:, t], 1.0 / D, None, ALU.mult))
                        chain.step(pool.tensor_tensor(root[:, t], var[:, t], C.half[:, 0:TG], ALU.pow))
                        chain.step(pool.tensor_scalar(var[:, t], root[:, t], RMS_EPS, None, ALU.add))
                        pool.tensor_tensor(rstd[:, t], var[:, t], C.neg_one[:, 0:TG], ALU.pow).then_inc(scaled, 1)

            if dstT is not None:
                @block.tensor
                def _(pe):
                    for g in range(G):
                        pe.wait_ge(normed, g + 1)
                        for k in range(TG):
                            mm = pe.transpose(turned[:, g, k * P:(k + 1) * P], dst[:, g * TG + k, :], C.ident[:, :])
                        mm.then_inc(turned_ok, 1)


def ternary_weights(nc, C, name, W1, W2, floor, up, down):
    with Stage(nc, name) as S:
        raw = S.sb("raw", [P, 2, DFF])
        sign = S.sb("sign", [P, 2, DFF])
        below = S.sb("below", [P, 2, DFF])
        rows = S.sb("rows", [P, 2])
        cut = S.sb("cut", [P, 2])
        neg_cut = S.sb("neg_cut", [P, 2])
        total = S.ps("total", [P, CH])
        turned = S.ps("turned", [P, 2, DFF])
        loaded = S.sem("loaded")
        own = S.sem("own")
        summed = S.sem("summed")
        totalled = S.sem("totalled")
        turned_ok = S.sem("turned_ok")
        with nc.Block() as block:

            @block.sync
            def _(sp):
                sp.dma_start(raw[:, 0, :].rearrange("p (m d) -> p m d", m=MFF),
                             W1.rearrange("(m p) d -> p m d", p=P)).then_inc(loaded, 16)
                sp.dma_start(raw[:, 1, :], W2).then_inc(loaded, 16)

            @block.vector
            def _(dve):
                chain = Chain(dve, own)
                dve.wait_ge(loaded, 32)
                for w in range(2):
                    dve.tensor_reduce(rows[:, w:w + 1], raw[:, w, :], AX, ALU.add,
                                      apply_absolute_value=True).then_inc(summed, 1)
                dve.wait_ge(totalled, 1)
                chain.step(dve.tensor_scalar(cut[:, :], total[:, 0:2], 1.0 / (D * DFF), floor, ALU.mult, ALU.max))
                chain.step(dve.tensor_scalar(cut[:, :], cut[:, :], 0.5, None, ALU.mult))
                chain.step(dve.tensor_scalar(neg_cut[:, :], cut[:, :], -1.0, None, ALU.mult))
                for w in range(2):
                    dve.tensor_scalar(below[:, w, :], raw[:, w, :], neg_cut[:, w:w + 1], None, ALU.is_lt)
                    chain.step(dve.tensor_scalar(sign[:, w, :], raw[:, w, :], cut[:, w:w + 1], None, ALU.is_gt))
                    chain.step(dve.tensor_tensor(sign[:, w, :], sign[:, w, :], below[:, w, :], ALU.subtract))
                dve.wait_ge(turned_ok, 1)
                dve.tensor_copy(up[:, :], turned[:, 0, :])
                dve.tensor_copy(down[:, :, :], turned[:, 1, :].rearrange("p (m d) -> p m d", m=MFF))

            @block.tensor
            def _(pe):
                pe.wait_ge(summed, 2)
                pe.matmul(total[:, 0:2], C.ones[:, :], rows[:, :], start=True, stop=True).then_inc(totalled, 1)
                pe.wait_ge(own, 7)
                for w in range(2):
                    for m in range(MFF):
                        mm = pe.transpose(turned[:, w, m * P:(m + 1) * P], sign[:, w, m * P:(m + 1) * P], C.ident[:, :])
                mm.then_inc(turned_ok, 1)


def ffn(nc, C, name, X, xnT, up, down, b1=None, b2=None, rms=False):
    with Stage(nc, name) as S:
        xT = [S.sb(f"xT_{part}", [P, TOK], F32R) for part in ("high", "low")]
        whole = S.sb("whole", [P, MFF, CH])
        hidden = [[S.sb(f"hidden{k}_{part}", [P, MFF, CH], F32R) for part in ("high", "low")] for k in range(2)]
        square = S.sb("square", [P, MFF, CH]) if rms else None
        folded = S.sb("folded", [P, CH]) if rms else None
        hidden_out = S.sb("hidden_out", [P, TPC, D]) if rms else None
        outT = [S.sb(f"outT{k}", [P, CH]) for k in range(2)]
        mean_sq, root, scale = S.sb("mean_sq", [P, TPC]), S.sb("root", [P, TPC]), S.sb("scale", [P, TPC])
        p_up = S.ps("p_up", [P, MFF, CH])
        p_down = S.ps("p_down", [P, CH])
        p_turn = S.ps("p_turn", [P, CH])
        p_sq = S.ps("p_sq", [P, CH])
        up_ready = S.sem("up_ready")
        gelu_done = S.sem("gelu_done")
        x_high, x_split, high_done, low_done = S.sem("x_high"), S.sem("x_split"), S.sem("high_done"), S.sem("low_done")
        square_done, folded_ok, sums_ready = S.sem("square_done"), S.sem("folded_ok"), S.sem("sums_ready")
        own_pool, copied, scale_ready = S.sem("own_pool"), S.sem("copied"), S.sem("scale_ready")
        down_ready, out_copied, turned_ok = S.sem("down_ready"), S.sem("out_copied"), S.sem("turned_ok")
        scaled, added = S.sem("scaled"), S.sem("added")
        with nc.Block() as block:

            @block.tensor
            def _(pe):
                def up_products(c):
                    wait(pe, x_split, c + 1)
                    for m in range(MFF):
                        wait(pe, gelu_done, (c - 1) * MFF + m + 1)
                        for x in range(2):
                            mm = pe.matmul(p_up[:, m, :], up[:, m * P:(m + 1) * P], xT[x][:, c * CH:(c + 1) * CH],
                                           start=(x == 0), stop=(x == 1))
                        mm.then_inc(up_ready, 1)

                def turn(c):
                    wait(pe, out_copied, c + 1)
                    wait(pe, scaled if rms else added, c)
                    for t in range(TPC):
                        mm = pe.transpose(p_turn[:, t * P:(t + 1) * P], outT[c % 2][:, t * P:(t + 1) * P], C.ident[:, :])
                    mm.then_inc(turned_ok, 1)

                up_products(0)
                for c in range(NCH):
                    if c + 1 < NCH:
                        up_products(c + 1)
                    wait(pe, out_copied, c)
                    for m in range(MFF):
                        wait(pe, low_done, c * MFF + m + 1)
                        for x in range(2):
                            mm = pe.matmul(p_down[:, :], down[:, m, :], hidden[c % 2][x][:, m, :], start=(m + x == 0),
                                           stop=(m == MFF - 1 and x == 1))
                    mm.then_inc(down_ready, 1)
                    if rms:
                        wait(pe, folded_ok, c + 1)
                        wait(pe, copied, c)
                        for t in range(TPC):
                            mm = pe.matmul(p_sq[:, t:t + 1], folded[:, t * P:(t + 1) * P], C.ones[:, 0:1], start=True,
                                           stop=True)
                        mm.then_inc(sums_ready, 1)
                    if c:
                        turn(c - 1)
                turn(NCH - 1)

            @block.scalar
            def _(act):
                def split(c):
                    at = slice(c * CH, (c + 1) * CH)
                    act.copy(xT[0][:, at], xnT[:, at]).then_inc(x_high, 1)

                split(0)
                split(1)
                for c in range(NCH):
                    if rms:
                        wait(act, square_done, c)
                    for m in range(MFF):
                        wait(act, up_ready, c * MFF + m + 1)
                        wait(act, low_done, (c - 1) * MFF + m + 1)
                        bias = b1[:, m:m + 1] if b1 is not None else 0.0
                        act.activation(whole[:, m, :], p_up[:, m, :], ACT.Gelu, bias=bias).then_inc(gelu_done, 1)
                    wait(act, down_ready, c - 1)
                    for m in range(MFF):
                        wait(act, gelu_done, c * MFF + m + 1)
                        act.copy(hidden[c % 2][0][:, m, :], whole[:, m, :]).then_inc(high_done, 1)
                    if c + 2 < NCH:
                        split(c + 2)

            if rms:
                @block.gpsimd
                def _(pool):
                    chain = Chain(pool, own_pool)

                    def squares(c):
                        wait(pool, gelu_done, (c + 1) * MFF)
                        wait(pool, folded_ok, c)
                        pool.tensor_tensor(square[:, :, :], whole[:, :, :], whole[:, :, :], ALU.mult).then_inc(square_done, 1)

                    squares(0)
                    for c in range(NCH):
                        if c + 1 < NCH:
                            squares(c + 1)
                        wait(pool, copied, c + 1)
                        chain.step(pool.tensor_tensor(root[:, :], mean_sq[:, :], C.half[:, 0:TPC], ALU.pow))
                        chain.step(pool.tensor_tensor(root[:, :], root[:, :], C.rms_eps[:, 0:TPC], ALU.add))
                        wait(pool, scaled, c)
                        pool.tensor_tensor(scale[:, :], root[:, :], C.neg_one[:, 0:TPC], ALU.pow).then_inc(scale_ready, 1)

            @block.vector
            def _(dve):
                def add(c):
                    tiles = slice(c * TPC, (c + 1) * TPC)
                    wait(dve, turned_ok, c + 1)
                    if not rms:
                        dve.scalar_tensor_tensor(
                            out=X[:, tiles, :], in0=p_turn[:, :].rearrange("p (t d) -> p t d", d=D), scalar=0.5,
                            in1=X[:, tiles, :], op0=ALU.mult, op1=ALU.add).then_inc(added, 1)
                    else:
                        wait(dve, scale_ready, c + 1)
                        wait(dve, added, c)
                        for t in range(TPC):
                            last = dve.tensor_scalar(hidden_out[:, t, :], p_turn[:, t * D:(t + 1) * D],
                                                     scale[:, t:t + 1], 0.5, ALU.mult, ALU.mult)
                        last.then_inc(scaled, 1)
                        wait(dve, scaled, c + 1)
                        dve.tensor_tensor(X[:, tiles, :], X[:, tiles, :], hidden_out[:, :, :], ALU.add
                                          ).then_inc(added, 1)

                def split(c):
                    at = slice(c * CH, (c + 1) * CH)
                    wait(dve, x_high, c + 1)
                    dve.tensor_tensor(xT[1][:, at], xnT[:, at], xT[0][:, at].bitcast(F32), ALU.subtract).then_inc(x_split, 1)

                split(0)
                split(1)
                for c in range(NCH):
                    for m in range(MFF):
                        wait(dve, high_done, c * MFF + m + 1)
                        dve.tensor_tensor(hidden[c % 2][1][:, m, :], whole[:, m, :], hidden[c % 2][0][:, m, :].bitcast(F32),
                                          ALU.subtract).then_inc(low_done, 1)
                    if c + 2 < NCH:
                        split(c + 2)
                    if rms:
                        wait(dve, square_done, c + 1)
                        wait(dve, sums_ready, c)
                        dve.tensor_reduce(folded[:, :], square[:, :, :].rearrange("p m t -> p t m"), AX, ALU.add
                                          ).then_inc(folded_ok, 1)
                    wait(dve, down_ready, c + 1)
                    wait(dve, turned_ok, c - 1)
                    if b2 is None:
                        dve.tensor_copy(outT[c % 2][:, :], p_down[:, :]).then_inc(out_copied, 1)
                    else:
                        dve.tensor_scalar(outT[c % 2][:, :], p_down[:, :], b2, None, ALU.add).then_inc(out_copied, 1)
                    if c:
                        add(c - 1)
                    if rms:
                        wait(dve, sums_ready, c + 1)
                        wait(dve, scale_ready, c)
                        dve.tensor_scalar(mean_sq[:, :], p_sq[:, 0:TPC], 1.0 / DFF, None, ALU.mult).then_inc(copied, 1)
                add(NCH - 1)



H, HD = 16, 8


def gated_scan_mixer(nc, C, I, X, xn, xnT):
    with Stage(nc, "mix0") as M:
        mixed = M.sb("mixed", [P, NT, D])
        gamma = M.sb("gamma", [P, D])
        beta = M.sb("beta", [P, D])
        Wg = M.sb("Wg", [P, D])
        Wout = M.sb("Wout", [P, D])
        with Stage(nc, "scan") as S:
            W = {n: S.sb(n, [P, D]) for n in ("Wq", "Wk", "Wv", "Wf")}
            bf = S.sb("bf", [P, 1])
            load(nc, "mix0_load", [(W[n][:, :], I[f"L0_attn_{n}"]) for n in W] + [
                (Wg[:, :], I["L0_attn_Wg"]), (Wout[:, :], I["L0_attn_Wout"]), (bf[:, :], I["L0_attn_bf"].unsqueeze(1)),
                (gamma[:, :], I["L0_attn_gamma"].partition_broadcast(P)),
                (beta[:, :], I["L0_attn_beta"].partition_broadcast(P))])
            krep_w = S.sb("krep_w", [P, HD, D])
            qrep_w = S.sb("qrep_w", [P, HD, D])
            with nc.Block() as block:

                @block.vector
                def _(dve):
                    for j in range(HD):
                        for rep, w in ((krep_w, W["Wk"]), (qrep_w, W["Wq"])):
                            dve.tensor_copy(rep[:, j, :].rearrange("p (h i) -> p h i", i=HD),
                                            w[:, j:D:HD].unsqueeze(2).to_broadcast([P, H, HD]))

            scan_over_tokens(nc, C, S, W, bf, krep_w, qrep_w, xnT, mixed)
        normalise(nc, C, "mix0_norm", mixed, mixed, gamma=gamma[:, :], beta=beta[:, :])
        gate_and_project(nc, C, X, xnT, mixed, Wg, Wout)


def scan_over_tokens(nc, C, S, W, bf, krep_w, qrep_w, xnT, mixed):
    vT = S.sb("vT", [P, SEQ])
    gT = S.sb("gT", [P, SEQ])
    vk = S.sb("vk", [P, SEQ])
    state = S.sb("state", [P, SEQ])
    sq = [S.sb(f"sq{k}", [P, SEQ]) for k in range(2)]
    p_k = [S.ps(f"p_k{k}", [P, SEQ]) for k in range(2)]
    p_q = S.ps("p_q", [P, SEQ])
    p_out = S.ps("p_out", [P, SEQ])
    v_ready, f_ready = S.sem("v_ready"), S.sem("f_ready")
    v_stored, g_stored = S.sem("v_stored"), S.sem("g_stored")
    k_ready, q_ready = S.sem("k_ready"), S.sem("q_ready")
    vk_done = S.sem("vk_done")
    sq_done = S.sem("sq_done")
    summed = S.sem("summed")
    out_stored = S.sem("out_stored")
    own = S.sem("own")
    with nc.Block() as block:

        @block.tensor
        def _(pe):
            with pe.Fori(0, BATCH) as b:
                def product(dst, w):
                    for c in range(SEQ // CH):
                        mm = pe.matmul(dst[:, c * CH:(c + 1) * CH], w, xnT[:, ds(b * SEQ + c * CH, CH)],
                                       start=True, stop=True)
                    return mm

                def k_of(j):
                    if j == 0:
                        pe.wait_ge(v_stored, b + 1)
                    else:
                        pe.wait_ge(vk_done, b * HD + j - 1)
                    product(p_k[j % 2], krep_w[:, j, :]).then_inc(k_ready, 1)

                def q_of(j):
                    if j == 0:
                        pe.wait_ge(g_stored, b + 1)
                    else:
                        pe.wait_ge(sq_done, b * HD + j)
                    product(p_q, qrep_w[:, j, :]).then_inc(q_ready, 1)

                pe.wait_ge(sq_done, b * HD)
                product(p_k[0], W["Wv"][:, :]).then_inc(v_ready, 1)
                product(p_q, W["Wf"][:, :]).then_inc(f_ready, 1)
                k_of(0)
                q_of(0)
                for j in range(HD):
                    if j + 1 < HD:
                        k_of(j + 1)
                        q_of(j + 1)
                    if j == 0:
                        pe.wait_ge(out_stored, b)
                    pe.wait_ge(sq_done, b * HD + j + 1)
                    for t in range(TPB):
                        mm = pe.matmul(p_out[:, t * D:(t + 1) * D], sq[j % 2][:, t * P:(t + 1) * P], C.ident[:, :],
                                       start=(j == 0 and t % TPC == 0), stop=(j == HD - 1), skip_group_check=True)
                    mm.then_inc(summed, 1)

        @block.scalar
        def _(act):
            with act.Fori(0, BATCH) as b:
                act.wait_ge(vk_done, b * HD)
                act.wait_ge(v_ready, b + 1)
                act.copy(vT[:, :], p_k[0][:, :]).then_inc(v_stored, 1)
                act.wait_ge(f_ready, b + 1)
                act.activation(gT[:, :], p_q[:, :], ACT.Sigmoid, bias=bf[:, 0:1]).then_inc(g_stored, 1)
                act.wait_ge(summed, (b + 1) * HD)
                act.copy(mixed[:, ds(b * TPB, TPB), :], p_out[:, :].rearrange("p (t d) -> p t d", d=D)
                         ).then_inc(out_stored, 1)

        @block.vector
        def _(dve):
            with dve.Fori(0, BATCH) as b:
                chain = Chain(dve, own, b * HD * 2)
                dve.wait_ge(v_stored, b + 1)
                dve.wait_ge(g_stored, b + 1)
                for j in range(HD):
                    dve.wait_ge(k_ready, b * HD + j + 1)
                    dve.tensor_tensor(vk[:, :], vT[:, :], p_k[j % 2][:, :], ALU.mult).then_inc(vk_done, 1)
                    dve.wait_ge(vk_done, b * HD + j + 1)
                    dve.tensor_tensor_scan(state[:, :], gT[:, :], vk[:, :], 0.0, ALU.mult, ALU.add).then_inc(own, 1)
                    dve.wait_ge(own, b * HD + j + 1)
                    dve.wait_ge(q_ready, b * HD + j + 1)
                    if j >= 2:
                        dve.wait_ge(summed, b * HD + j - 1)
                    else:
                        dve.wait_ge(summed, b * HD)
                    dve.tensor_tensor(sq[j % 2][:, :], state[:, :], p_q[:, :], ALU.mult).then_inc(sq_done, 1)


def gate_and_project(nc, C, X, xnT, mixed, Wg, Wout):
    G = NT // TPC
    with Stage(nc, "gate") as S:
        gate = S.sb("gate", [P, NT, D])
        gated = S.sb("gated", [P, NT, D])
        gatedT = S.sb("gatedT", [P, TOK])
        p_gate = S.ps("p_gate", [P, 2, CH])
        p_turn = S.ps("p_turn", [P, 2, CH])
        p_proj = S.ps("p_proj", [P, 2, CH])
        gate_ready, gate_done = S.sem("gate_ready"), S.sem("gate_done")
        gated_done, turned, turned_stored = S.sem("gated_done"), S.sem("turned"), S.sem("turned_stored")
        projected, added = S.sem("projected"), S.sem("added")
        with nc.Block() as block:

            @block.tensor
            def _(pe):
                def gates(g):
                    if g >= 2:
                        pe.wait_ge(gate_done, g - 1)
                    for k in range(TPC):
                        t = g * TPC + k
                        mm = pe.matmul(p_gate[:, g % 2, k * D:(k + 1) * D], xnT[:, t * P:(t + 1) * P], Wg[:, :],
                                       start=True, stop=True)
                    mm.then_inc(gate_ready, 1)

                gates(0)
                for g in range(G):
                    if g + 1 < G:
                        gates(g + 1)
                    pe.wait_ge(gated_done, g + 1)
                    if g >= 2:
                        pe.wait_ge(turned_stored, g - 1)
                    for k in range(TPC):
                        mm = pe.transpose(p_turn[:, g % 2, k * P:(k + 1) * P], gated[:, g * TPC + k, :], C.ident[:, :])
                    mm.then_inc(turned, 1)
                    pe.wait_ge(turned_stored, g + 1)
                    if g >= 2:
                        pe.wait_ge(added, g - 1)
                    for k in range(TPC):
                        t = g * TPC + k
                        mm = pe.matmul(p_proj[:, g % 2, k * D:(k + 1) * D], gatedT[:, t * P:(t + 1) * P], Wout[:, :],
                                       start=True, stop=True)
                    mm.then_inc(projected, 1)

            @block.scalar
            def _(act):
                for g in range(G):
                    act.wait_ge(gate_ready, g + 1)
                    act.activation(gate[:, g * TPC:(g + 1) * TPC, :],
                                   p_gate[:, g % 2, :].rearrange("p (t d) -> p t d", d=D), ACT.Silu).then_inc(gate_done, 1)
                    act.wait_ge(turned, g + 1)
                    act.copy(gatedT[:, g * CH:(g + 1) * CH], p_turn[:, g % 2, :]).then_inc(turned_stored, 1)

            @block.vector
            def _(dve):
                for g in range(G):
                    t = slice(g * TPC, (g + 1) * TPC)
                    dve.wait_ge(gate_done, g + 1)
                    dve.tensor_tensor(gated[:, t, :], gate[:, t, :], mixed[:, t, :], ALU.mult).then_inc(gated_done, 1)
                    dve.wait_ge(projected, g + 1)
                    dve.tensor_tensor(X[:, t, :], X[:, t, :], p_proj[:, g % 2, :].rearrange("p (t d) -> p t d", d=D),
                                      ALU.add).then_inc(added, 1)


NEXP = 8


def moe_ffn(nc, C, I, name, X, xnT):
    with Stage(nc, name) as M:
        pickT = M.sb("pickT", [NEXP, TOK])
        b1T = M.sb("b1T", [P, NEXP * MFF])
        b2 = M.sb("b2", [NEXP, D])
        outT = M.sb("outT", [P, TOK])
        pick_rows = nc.dram_tensor(f"{name}_pick_rows", [NEXP, TOK], F32, kind="Internal")
        route(nc, C, I, name, xnT, pickT, pick_rows, b1T, b2)
        experts(nc, C, I, name, xnT, pickT, pick_rows, b1T, b2, outT)
        add_turned(nc, C, name + "_add", X, outT)


def route(nc, C, I, name, xnT, pickT, pick_rows, b1T, b2):
    with Stage(nc, name + "_route") as S:
        WrT = S.sb("WrT", [P, NEXP])
        br = S.sb("br", [P, NEXP])
        b1 = S.sb("b1", [NEXP * MFF, P])
        rank = S.sb("rank", [P, NEXP])
        logits = S.sb("logits", [P, NT, NEXP])
        best = S.sb("best", [P, NT])
        tied = S.sb("tied", [P, NT, NEXP])
        first = S.sb("first", [P, NT])
        pick = S.sb("pick", [P, NT, NEXP])
        p_logits = S.ps("p_logits", [P, CH])
        p_b1T = S.ps("p_b1T", [P, CH])
        p_pickT = S.ps("p_pickT", [P, TOK])
        loaded, ranked = S.sem("loaded"), S.sem("ranked")
        logits_ready, own, picked = S.sem("logits_ready"), S.sem("own"), S.sem("picked")
        turned, stored = S.sem("turned"), S.sem("stored")
        b1_ready, sent = S.sem("b1_ready"), S.sem("sent")
        with nc.Block() as block:

            @block.sync
            def _(sp):
                sp.dma_start(WrT[:, :], I["L1_ffn_Wr"].rearrange("e d -> d e"),
                             allow_slow_non_contiguous=True).then_inc(loaded, 16)
                sp.dma_start(br[:, :], I["L1_ffn_br"].partition_broadcast(P)).then_inc(loaded, 16)
                sp.dma_start(b1[:, :], I["L1_ffn_b1"].rearrange("e (m p) -> (e m) p", p=P)).then_inc(loaded, 16)
                sp.dma_start(b2[:, :], I["L1_ffn_b2"]).then_inc(loaded, 16)
                sp.wait_ge(stored, 1)
                sp.dma_start(pick_rows[:, :], pickT[:, :]).then_inc(sent, 16)
                sp.wait_ge(sent, 16)

            @block.gpsimd
            def _(pool):
                for e in range(NEXP):
                    pool.memset(rank[:, e:e + 1], float(NEXP - e)).then_inc(ranked, 1)

            @block.tensor
            def _(pe):
                pe.wait_ge(loaded, 64)
                for t in range(NT):
                    mm = pe.matmul(p_logits[:, t * NEXP:(t + 1) * NEXP], xnT[:, t * P:(t + 1) * P], WrT[:, :],
                                   start=True, stop=True)
                mm.then_inc(logits_ready, 1)
                pe.transpose(p_b1T[:, 0:NEXP * MFF], b1[:, :], C.ident[0:NEXP * MFF, 0:NEXP * MFF]).then_inc(b1_ready, 1)
                pe.wait_ge(picked, 1)
                for t in range(NT):
                    mm = pe.transpose(p_pickT[0:NEXP, t * P:(t + 1) * P], pick[:, t, :], C.ident[:, :])
                mm.then_inc(turned, 1)

            @block.scalar
            def _(act):
                act.wait_ge(b1_ready, 1)
                act.copy(b1T[:, :], p_b1T[:, 0:NEXP * MFF])
                act.wait_ge(turned, 1)
                act.copy(pickT[:, :], p_pickT[0:NEXP, :]).then_inc(stored, 1)

            @block.vector
            def _(dve):
                chain = Chain(dve, own)
                dve.wait_ge(loaded, 64)
                dve.wait_ge(ranked, NEXP)
                dve.wait_ge(logits_ready, 1)
                chain.step(dve.tensor_tensor(logits[:, :, :], p_logits[:, 0:NT * NEXP].rearrange("p (t e) -> p t e", e=NEXP),
                                             per_feature(br[:, :], NT), ALU.add))
                chain.step(dve.tensor_reduce(best[:, :], logits[:, :, :], AX, ALU.max))
                chain.step(dve.tensor_tensor(tied[:, :, :], logits[:, :, :], per_token(best[:, :], NEXP), ALU.is_equal))
                chain.step(dve.tensor_tensor(tied[:, :, :], tied[:, :, :], per_feature(rank[:, :], NT), ALU.mult))
                chain.step(dve.tensor_reduce(first[:, :], tied[:, :, :], AX, ALU.max))
                chain.step(dve.tensor_tensor(tied[:, :, :], tied[:, :, :], per_token(first[:, :], NEXP), ALU.is_equal))
                dve.tensor_scalar(pick[:, :, :], tied[:, :, :], 0.5, None, ALU.mult).then_inc(picked, 1)


def experts(nc, C, I, name, xnT, pickT, pick_rows, b1T, b2, outT):
    W1 = I["L1_ffn_W1"]
    W2 = I["L1_ffn_W2"]
    with Stage(nc, name + "_experts") as S:
        raw1 = [S.sb(f"raw1_{k}", [P, MFF, D]) for k in range(2)]
        raw2 = [S.sb(f"raw2_{k}", [P, DFF]) for k in range(2)]
        xT = [S.sb(f"xT_{part}", [P, TOK], F32R) for part in ("high", "low")]
        up = [[S.sb(f"up{k}_{part}", [P, DFF], F32R) for part in ("high", "low")] for k in range(2)]
        down = [[S.sb(f"down{k}_{part}", [P, DFF], F32R) for part in ("high", "low")] for k in range(2)]
        b1 = [S.sb(f"b1_{k}", [P, MFF]) for k in range(2)]
        pick = [S.sb(f"pick{k}", [P, TOK]) for k in range(2)]
        whole = S.sb("whole", [P, MFF, CH])
        hidden = [[S.sb(f"hidden{k}_{part}", [P, MFF, CH], F32R) for part in ("high", "low")] for k in range(2)]
        p_up = [S.ps(f"p_up{k}", [P, CH]) for k in range(2)]
        p_out = S.ps("p_out", [P, NCH, CH])
        p_turn = [S.ps(f"p_turn{w}", [P, DFF]) for w in range(2)]
        loaded = [S.sem(f"loaded{k}") for k in range(2)]
        pick_loaded = [S.sem(f"pick_loaded{k}") for k in range(2)]
        turned = [S.sem(f"turned{w}") for w in range(2)]
        up_stored, down_stored, b1_set = S.sem("up_stored"), S.sem("down_stored"), S.sem("b1_set")
        x_high, x_split = S.sem("x_high"), S.sem("x_split")
        up_high, down_high = S.sem("up_high"), S.sem("down_high")
        up_ready, relu_done, masked = S.sem("up_ready"), S.sem("relu_done"), S.sem("masked")
        high_done, low_done = S.sem("high_done"), S.sem("low_done")
        down_ready = S.sem("down_ready")

        def turns(eng, expert):
            for e in (0, 1):
                expert(e, e)
            with eng.Fori(0, NEXP // 2 - 2) as i:
                for k in range(2):
                    expert(Count(i, 2, 2 + k), k)
            for e in (NEXP - 2, NEXP - 1):
                expert(e, e % 2)

        PASSES = ((0, 0), (0, 1), (1, 0))

        def last(e):
            return isinstance(e, int) and e == NEXP - 1

        with nc.Block() as block:

            @block.sync
            def _(sp):
                def fetch(e, k):
                    one = ds(at_turn(e), 1)
                    sp.dma_start(raw1[k][:, :, :], W1[one].rearrange("e (m p) d -> p (e m) d", p=P)).then_inc(loaded[k], 16)
                    sp.dma_start(raw2[k][:, :], W2[one].rearrange("e d f -> d (e f)")).then_inc(loaded[k], 16)

                def fetch_pick(e, k):
                    sp.dma_start(pick[k][:, :], pick_rows[ds(at_turn(e), 1), :].to_broadcast([P, TOK])
                                 ).then_inc(pick_loaded[k], 16)

                for e in range(2):
                    fetch(e, e)
                    fetch_pick(e, e)
                with sp.Fori(0, NEXP // 2 - 1) as i:
                    for k in range(2):
                        e = Count(i, 2, k)
                        for w in range(2):
                            wait(sp, turned[w], e + 1)
                        fetch(e + 2, k)
                        wait(sp, masked, (e + 1) * (NCH * MFF))
                        fetch_pick(e + 2, k)

            @block.tensor
            def _(pe):
                def turn(e, k, w):
                    raw = raw1[k][:, :, :].rearrange("p m d -> p (m d)") if w == 0 else raw2[k][:, :]
                    wait(pe, loaded[k], e * 16 + (32 - 16 * k))
                    wait(pe, (up_stored, down_stored)[w], e)
                    for m in range(MFF):
                        mm = pe.transpose(p_turn[w][:, m * P:(m + 1) * P], raw[:, m * P:(m + 1) * P], C.ident[:, :])
                    mm.then_inc(turned[w], 1)

                def up_product(e, k, c, m):
                    n = e * NCH + c
                    wait(pe, relu_done, n * MFF + (m - 1))
                    for w, x in PASSES:
                        mm = pe.matmul(p_up[m % 2][:, :], up[k][w][:, m * P:(m + 1) * P], xT[x][:, c * CH:(c + 1) * CH],
                                       start=(w + x == 0), stop=(w == 1))
                    mm.then_inc(up_ready, 1)

                def down_product(e, k, c, m):
                    n = e * NCH + c
                    wait(pe, low_done, n * MFF + (m + 1))
                    for w, x in PASSES:
                        mm = pe.matmul(p_out[:, c, :], down[k][w][:, m * P:(m + 1) * P], hidden[c % 2][x][:, m, :],
                                       start=False, stop=(last(e) and m == MFF - 1 and w == 1), skip_group_check=True)
                    if m == MFF - 1:
                        mm.then_inc(down_ready, 1)

                def expert(e, k):
                    wait(pe, up_stored, e + 1)
                    for c in range(NCH):
                        for m in range(MFF):
                            up_product(e, k, c, m)
                            if c:
                                down_product(e, k, c - 1, m)
                            elif not (isinstance(e, int) and e == 0):
                                down_product(e - 1, 1 - k, NCH - 1, m)
                        if c == 0:
                            wait(pe, down_stored, e + 1)
                        if c in (1, 2) and not last(e):
                            turn(e + 1, 1 - k, c - 1)

                for w in range(2):
                    turn(0, 0, w)
                for c in range(NCH):
                    pe.matmul(p_out[:, c, :], b2[:, :], pickT[:, c * CH:(c + 1) * CH], start=True, stop=False,
                              skip_group_check=True)
                wait(pe, x_split, NCH)
                turns(pe, expert)
                for m in range(MFF):
                    down_product(NEXP - 1, (NEXP - 1) % 2, NCH - 1, m)

            @block.scalar
            def _(act):
                def store_high(e, k):
                    wait(act, turned[0], e + 1)
                    act.copy(up[k][0][:, :], p_turn[0][:, :]).then_inc(up_high, 1)
                    wait(act, turned[1], e + 1)
                    act.copy(down[k][0][:, :], p_turn[1][:, :]).then_inc(down_high, 1)

                def high_part(e, c, m):
                    n = e * NCH + c
                    wait(act, masked, n * MFF + (m + 1))
                    if m == 0:
                        wait(act, down_ready, n - 1)
                    act.copy(hidden[c % 2][0][:, m, :], whole[:, m, :]).then_inc(high_done, 1)

                def expert(e, k):
                    for c in range(NCH):
                        n = e * NCH + c
                        if c == 0:
                            wait(act, b1_set, e + 1)
                        for m in range(MFF):
                            wait(act, up_ready, n * MFF + (m + 1))
                            wait(act, low_done, n * MFF + (m + 1 - MFF))
                            act.activation(whole[:, m, :], p_up[m % 2][:, :], ACT.Relu, bias=b1[k][:, m:m + 1]
                                           ).then_inc(relu_done, 1)
                            if m:
                                high_part(e, c, m - 1)
                        high_part(e, c, MFF - 1)
                        if c == 2 and not last(e):
                            store_high(e + 1, 1 - k)

                for c in range(NCH):
                    act.copy(xT[0][:, c * CH:(c + 1) * CH], xnT[:, c * CH:(c + 1) * CH]).then_inc(x_high, 1)
                store_high(0, 0)
                turns(act, expert)

            @block.vector
            def _(dve):
                def store_low(e, k):
                    wait(dve, up_high, e + 1)
                    dve.tensor_tensor(up[k][1][:, :], p_turn[0][:, :], up[k][0][:, :].bitcast(F32), ALU.subtract
                                      ).then_inc(up_stored, 1)
                    wait(dve, down_high, e + 1)
                    dve.tensor_tensor(down[k][1][:, :], p_turn[1][:, :], down[k][0][:, :].bitcast(F32), ALU.subtract
                                      ).then_inc(down_stored, 1)

                def low_part(e, c, m):
                    wait(dve, high_done, (e * NCH + c) * MFF + (m + 1))
                    dve.tensor_tensor(hidden[c % 2][1][:, m, :], whole[:, m, :], hidden[c % 2][0][:, m, :].bitcast(F32),
                                      ALU.subtract).then_inc(low_done, 1)

                def set_b1(e, k):
                    wait(dve, relu_done, (e - 1) * (NCH * MFF))
                    dve.tensor_copy(b1[k][:, :], b1T[:, ds(at_turn(e * MFF), MFF)]).then_inc(b1_set, 1)

                def expert(e, k):
                    wait(dve, pick_loaded[k], e * 8 + (16 - 8 * k))
                    for c in range(NCH):
                        for m in range(MFF):
                            n = e * NCH + c
                            wait(dve, relu_done, n * MFF + (m + 1))
                            dve.tensor_tensor(whole[:, m, :], whole[:, m, :], pick[k][:, c * CH:(c + 1) * CH], ALU.mult
                                              ).then_inc(masked, 1)
                            if m:
                                low_part(e, c, m - 1)
                        low_part(e, c, MFF - 1)
                        if c == 2 and not last(e):
                            store_low(e + 1, 1 - k)
                            set_b1(e + 1, 1 - k)

                for c in range(NCH):
                    at = slice(c * CH, (c + 1) * CH)
                    wait(dve, x_high, c + 1)
                    dve.tensor_tensor(xT[1][:, at], xnT[:, at], xT[0][:, at].bitcast(F32), ALU.subtract).then_inc(x_split, 1)
                set_b1(0, 0)
                store_low(0, 0)
                turns(dve, expert)
                for c in range(NCH):
                    wait(dve, down_ready, (NEXP - 1) * NCH + c + 1)
                    dve.tensor_copy(outT[:, c * CH:(c + 1) * CH], p_out[:, c, :])


UNITS = BATCH * H
NP = 3
KR = NP * NP * HD
KM = KR + NP
VW = HD + 1


def stacked_attention_mixer(nc, C, I, X, xn, xnT):
    with Stage(nc, "mix1") as M:
        parts = {n: nc.dram_tensor(f"mix1_{n}", [NP, HD, UNITS, SEQ], BF16, kind="Internal") for n in ("q", "k", "k2")}
        V = M.sb("V", [P, UNITS, TPB, VW])
        shifted = M.sb("shifted", [P, NT, D])
        Y = [M.sb(f"Y{n}", [P, UNITS, TPB, HD]) for n in range(2)]
        mask_q = M.sb("mask_q", [P, 2, 2, P], BF16)
        mask_k = M.sb("mask_k", [P, 2, 2, P], BF16)
        ident16 = M.sb("ident16", [P, P], BF16)
        project_and_split(nc, C, I, xn, xnT, parts, V, shifted, mask_q, mask_k, ident16)
        causal_attention(nc, C, "mix1_a", parts["q"], parts["k"], V, Y[0], mask_q[:, 0], mask_k[:, 0], ident16)
        errors(nc, V, shifted, Y[0])
        causal_attention(nc, C, "mix1_b", parts["q"], parts["k2"], V, Y[1], mask_q[:, 1], mask_k[:, 1], ident16)
        project_out(nc, C, I, X, Y)


def project_and_split(nc, C, I, xn, xnT, parts, V, shifted, mask_q, mask_k, ident16):
    SCALE = float(HD) ** -0.5
    with Stage(nc, "mix1_proj") as S:
        W = S.sb("W", [P, 3, D])
        bias = S.sb("bias", [P, 3])
        bias_s = S.sb("bias_s", [P, 3])
        full = [S.sb(f"full{k}", [P, CH]) for k in range(2)]
        rest = [S.sb(f"rest{k}", [P, CH]) for k in range(2)]
        split_parts = S.sb("split_parts", [P, NP, 3, TOK], BF16)
        p = S.ps("p", [P, 2, CH])
        loaded, biased, shifted_ok, cleared = S.sem("loaded"), S.sem("biased"), S.sem("shifted_ok"), S.sem("cleared")
        ready, stored, split = S.sem("ready"), S.sem("stored"), S.sem("split")
        own, rest_ready = S.sem("own"), S.sem("rest_ready")
        sent, masks = S.sem("sent"), S.sem("masks")
        N = 3 * NCH
        with nc.Block() as block:

            @block.sync
            def _(sp):
                sp.dma_start(W[:, 0:2, :].rearrange("p a d -> p (a d)"), I["L1_attn_W_attn"]).then_inc(loaded, 16)
                sp.dma_start(W[:, 2, :], I["L1_attn_W_k2"]).then_inc(loaded, 16)
                sp.dma_start(bias[:, 0:2], I["L1_attn_b_attn"].rearrange("(a p) -> p a", p=P),
                             allow_slow_non_contiguous=True).then_inc(loaded, 16)
                sp.dma_start(bias[:, 2:3], I["L1_attn_b_k2"].unsqueeze(1)).then_inc(loaded, 16)
                sp.dma_start(shifted[0:112, :, :], xn[1:113, :, :]).then_inc(shifted_ok, 16)
                sp.dma_start(shifted[112:127, :, :], xn[113:128, :, :]).then_inc(shifted_ok, 16)
                sp.dma_start(shifted[127:128, 0:NT - 1, :], xn[0:1, 1:NT, :]).then_inc(shifted_ok, 16)
                sp.dma_start(shifted[127:128, NT - 1, :], xn[0:1, 0, :]).then_inc(shifted_ok, 16)
                for n, name in enumerate(("q", "k", "k2")):
                    sp.wait_ge(split, NCH * (n + 1))
                    for a in range(NP):
                        for b in range(BATCH):
                            sp.dma_start(parts[name][a, :, b * H:(b + 1) * H, :].rearrange("d h s -> h d s"),
                                         split_parts[:, a, n, b * SEQ:(b + 1) * SEQ]).then_inc(sent, 16)
                sp.wait_ge(sent, 16 * 3 * NP * BATCH)
                sp.wait_ge(shifted_ok, 64)

            @block.tensor
            def _(pe):
                pe.wait_ge(loaded, 64)
                for n in range(3):
                    for c in range(NCH):
                        i = n * NCH + c
                        if i >= 2:
                            pe.wait_ge(stored, i - 1)
                        pe.matmul(p[:, i % 2, :], W[:, n, :], xnT[:, c * CH:(c + 1) * CH],
                                  start=True, stop=True).then_inc(ready, 1)

            @block.scalar
            def _(act):
                act.wait_ge(biased, 1)
                for i in range(N):
                    n = i // NCH
                    act.wait_ge(ready, i + 1)
                    if i >= 2:
                        act.wait_ge(rest_ready, i - 1)
                    act.activation(full[i % 2][:, :], p[:, i % 2, :], ACT.Identity, bias=bias_s[:, n:n + 1],
                                   scale=SCALE if n == 0 else 1.0).then_inc(stored, 1)

            @block.vector
            def _(dve):
                dve.wait_ge(loaded, 64)
                chain = Chain(dve, own)
                dve.tensor_scalar(bias_s[:, 0:1], bias[:, 0:1], SCALE, None, ALU.mult)
                dve.tensor_copy(bias_s[:, 1:3], bias[:, 1:3]).then_inc(biased, 1)
                for i in range(N):
                    n, c = i // NCH, i % NCH
                    col = slice(c * CH, (c + 1) * CH)
                    dve.wait_ge(stored, i + 1)
                    if i >= 2:
                        dve.wait_ge(split, i - 1)
                    chain.step(dve.tensor_copy(split_parts[:, 0, n, col], full[i % 2][:, :]))
                    dve.tensor_tensor(rest[i % 2][:, :], full[i % 2][:, :], split_parts[:, 0, n, col], ALU.subtract
                                      ).then_inc(rest_ready, 1)
                    dve.wait_ge(rest_ready, i + 1)
                    chain.step(dve.tensor_copy(split_parts[:, 1, n, col], rest[i % 2][:, :]))
                    dve.tensor_tensor(split_parts[:, 2, n, col], rest[i % 2][:, :], split_parts[:, 1, n, col],
                                      ALU.subtract).then_inc(split, 1)
                for b in range(BATCH):
                    for h in range(H):
                        dve.tensor_copy(V[:, b * H + h, :, 0:HD], xn[:, b * TPB:(b + 1) * TPB, h * HD:(h + 1) * HD])
                dve.memset(V[:, :, :, HD:VW], 1.0)
                dve.tensor_copy(ident16[:, :], C.ident[:, :])

            @block.gpsimd
            def _(pool):
                pool.memset(mask_q[:, :, :, :], 0.0)
                pool.memset(mask_k[:, :, :, :], 0.0).then_inc(cleared, 1)
                pool.wait_ge(cleared, 1)
                for strict in range(2):
                    for tile in range(2):
                        pool.affine_select(out=mask_q[:, strict, tile, :], in_=mask_q[:, strict, tile, :],
                                           compare_op=ALU.is_ge, fill=-BIG, base=-strict, pattern=[[-1, P]],
                                           channel_multiplier=1)
                        pool.affine_select(out=mask_k[:, strict, tile, :], in_=mask_k[:, strict, tile, :],
                                           compare_op=ALU.is_ge, fill=-BIG, base=-strict, pattern=[[1, P]],
                                           channel_multiplier=-1).then_inc(masks, 1)
                pool.wait_ge(masks, 4)
                pool.memset(mask_q[0:1, 1, 0, 0:1], 0.0)
                pool.memset(mask_k[0:1, 1, 0, 0:1], 0.0)


QH = 4
QUADS = UNITS // QH
SETS = 3


def causal_attention(nc, C, name, q_parts, k_parts, V, Y, mask_q, mask_k, ident16):
    GROUPS = [(qc, kt) for qc in range(SEQ // CH) for kt in range((qc + 1) * TPC)]
    NG = len(GROUPS)
    CHUNKS = [(g, 0) for g in range(TPB)] + [(g, 1) for g in range(TPC, TPB)]
    LEAD = 11
    NE, NS = QH * NG, QH * len(CHUNKS)
    SCHEDULE = []
    taken = 0
    for i in range(NE):
        if i == 0:
            SCHEDULE.append(("Y", 0))
        SCHEDULE.append(("E", i))
        if i % QH == 2 and i >= QH:
            SCHEDULE.append(("V", i // QH - 1))
        while taken < min(NS, -(-NS * (i + 1) // (NE - LEAD))):
            SCHEDULE.append(("S", taken))
            taken += 1
        SCHEDULE += {8: [("N", 0)], 13: [("N", 1)], NE - LEAD + 1: [("M", 0)], NE - LEAD + 3: [("T", 0)]}.get(i, [])
    SCHEDULE.append(("V", NG - 1))

    with Stage(nc, name) as S:
        q = S.sb("q", [KM, SETS, QH, SEQ], BF16)
        k_ = S.sb("k", [KM, SETS, QH, SEQ], BF16)
        vals = S.sb("vals", [P, SETS, QH, TPB, VW])
        part_max = S.sb("part_max", [P, QH, NS // QH])
        rest_max = S.sb("rest_max", [P, QH, TPB])
        max_all = S.sb("max_all", [P, P], BF16)
        max_parts = max_all[:, 0:NP * QH * TPB].rearrange("p (a j t) -> p a j t", a=NP, j=QH)
        max_rows = S.sb("max_rows", [NP * QH * TPB, P], BF16)
        e = S.sb("e", [P, 2, QH, CH])
        y = S.sb("y", [P, SEQ])
        recip = S.sb("recip", [P, 2, TPC, QH])
        p_s = [S.ps(f"p_s{n}", [P, CH]) for n in range(2)]
        p_e = [S.ps(f"p_e{n}", [P, CH]) for n in range(3)]
        p_y = S.ps("p_y", [P, SEQ])
        p_t = S.ps("p_t", [P, CH])
        ones_set, cleared, vals_ready = S.sem("ones_set"), S.sem("cleared"), S.sem("vals_ready")
        loaded = [S.sem(f"loaded{n}") for n in range(SETS)]
        s_ready = [S.sem(f"s_ready{n}") for n in range(2)]
        s_read = [S.sem(f"s_read{n}") for n in range(2)]
        m_own, m_split, m_turned, m_copied, m_sent = (S.sem("m_own"), S.sem("m_split"), S.sem("m_turned"),
                                                      S.sem("m_copied"), S.sem("m_sent"))
        e_scores, e_done, pv_done = S.sem("e_scores"), S.sem("e_done"), S.sem("pv_done")
        y_copied, y_turned, y_own, y_normed = S.sem("y_copied"), S.sem("y_turned"), S.sem("y_own"), S.sem("y_normed")

        def steps(eng, step):
            step(0, 0, 0)
            with eng.Fori(0, (QUADS - 2) // SETS) as i:
                for k in range(1, SETS + 1):
                    step(Count(i, SETS, k), k, i)
            step(QUADS - 1, QUADS - 1, 0)

        def last(m, ahead):
            return isinstance(m, int) and m + ahead >= QUADS

        with nc.Block() as block:

            @block.sync
            def _(sp):
                def fetch(m, n):
                    heads = ds(at_turn(m * QH), QH)
                    for a in range(NP):
                        rows = slice(a * NP * HD, (a + 1) * NP * HD)
                        sp.dma_start(q[rows, n, :, :], q_parts[a, :, heads, :].rearrange("d j s -> d (j s)").unsqueeze(0)
                                     .to_broadcast([NP, HD, QH * SEQ])).then_inc(loaded[n], 16)
                        sp.dma_start(k_[rows, n, :, :], k_parts[:, :, heads, :].rearrange("b d j s -> b d (j s)")
                                     ).then_inc(loaded[n], 16)

                def send(m, n):
                    wait(sp, m_copied, m + 1)
                    for a in range(NP):
                        sp.dma_start(q[KR + a:KR + a + 1, n, :, :], max_rows[a * QH * TPB:(a + 1) * QH * TPB, :]
                                     ).then_inc(m_sent, 16)

                wait(sp, ones_set, 1)
                fetch(0, 0)
                fetch(1, 1)
                send(0, 0)
                with sp.Fori(0, (QUADS - 2) // SETS) as i:
                    for k in range(SETS):
                        m = Count(i, SETS, k)
                        wait(sp, pv_done, m * NG)
                        fetch(m + 2, (k + 2) % SETS)
                        send(m + 1, (k + 1) % SETS)
                send(QUADS - 1, (QUADS - 1) % SETS)

            @block.gpsimd
            def _(pool):
                def copy_values(m, n):
                    pool.tensor_copy(vals[:, n, :, :, :], V[:, ds(at_turn(m * QH), QH), :, :]).then_inc(vals_ready, 1)

                copy_values(0, 0)
                copy_values(1, 1)
                with pool.Fori(0, (QUADS - 2) // SETS) as i:
                    for k in range(SETS):
                        m = Count(i, SETS, k)
                        wait(pool, pv_done, m * NG)
                        copy_values(m + 2, (k + 2) % SETS)

            @block.tensor
            def _(pe):
                def scores(m, k, i, s):
                    j, (g, c) = s // len(CHUNKS), CHUNKS[s % len(CHUNKS)]
                    if s == 0:
                        wait(pe, loaded[k % SETS], (i + k // SETS + 1) * (NP * 32))
                    wait(pe, s_read[s % 2], m * (NS // 2) + s // 2)
                    n = (g + 1) * P
                    w = min(n - c * CH, CH)
                    diag = (c == 1) == (g >= TPC)
                    mm = pe.matmul(p_s[s % 2][:, 0:w], q[0:KR, k % SETS, j, g * P:(g + 1) * P],
                                   k_[0:KR, k % SETS, j, c * CH:c * CH + w], start=True, stop=not diag,
                                   skip_group_check=True)
                    if diag:
                        mm = pe.matmul(p_s[s % 2][:, w - P:w], ident16[:, :], mask_q[:, min(g, 1), :], start=False,
                                       stop=True, skip_group_check=True)
                    mm.then_inc(s_ready[s % 2], 1)

                def turn_max(m):
                    wait(pe, m_split, m + 1)
                    wait(pe, y_normed, (m - 1) * 2)
                    pe.transpose(p_t[:, 0:P // 2].bitcast(BF16), max_all[:, :], ident16[:, :]).then_inc(m_turned, 1)

                def exp_scores(m, k, e_at):
                    (qc, kt), j = GROUPS[e_at // QH], e_at % QH
                    q0 = max(kt * P, qc * CH)
                    w = (qc + 1) * CH - q0
                    if e_at == 0:
                        wait(pe, m_sent, m * (NP * 16) + NP * 16)
                    wait(pe, e_done, m * NE + e_at - 2)
                    diag = kt * P >= qc * CH
                    bank = p_e[e_at % 3]
                    mm = pe.matmul(bank[:, 0:w], k_[:, k % SETS, j, kt * P:(kt + 1) * P],
                                   q[:, k % SETS, j, q0:q0 + w], start=True, stop=not diag, skip_group_check=True)
                    if diag:
                        mm = pe.matmul(bank[:, 0:P], ident16[:, :], mask_k[:, min(kt, 1), :], start=False, stop=True,
                                       skip_group_check=True)
                    mm.then_inc(e_scores, 1)

                def times_values(m, k, n):
                    qc, kt = GROUPS[n]
                    q0 = max(kt * P, qc * CH)
                    w = (qc + 1) * CH - q0
                    if n == 0:
                        wait(pe, y_copied, m + 1)
                        wait(pe, vals_ready, m + 1)
                    wait(pe, e_done, m * NE + (n + 1) * QH)
                    for j in range(QH):
                        mm = pe.matmul(p_y[32 * j:32 * j + VW, q0:q0 + w], vals[:, k % SETS, j, kt, :], e[:, n % 2, j, 0:w],
                                       start=(kt == 0), stop=(kt == qc * TPC + TPC - 1), skip_group_check=True,
                                       tile_position=(0, 32 * j))
                    mm.then_inc(pv_done, 1)

                def turn_result(m, h):
                    if h == 0:
                        wait(pe, y_copied, m + 2)
                        wait(pe, m_copied, m + 2 if not last(m, 1) else QUADS)
                    else:
                        wait(pe, y_normed, m * 2 + 1)
                    for t in range(TPC):
                        at = (h * TPC + t) * P
                        mm = pe.transpose(p_t[:, t * P:(t + 1) * P], y[:, at:at + P], C.ident[:, :])
                    mm.then_inc(y_turned, 1)

                def step(m, k, i):
                    for what, n in SCHEDULE:
                        if what == "E":
                            exp_scores(m, k, n)
                        elif what == "V":
                            times_values(m, k, n)
                        elif what == "S" and not last(m, 1):
                            scores(m + 1, k + 1, i, n)
                        elif what == "T" and not last(m, 1):
                            turn_max(m + 1)
                        elif what == "N" and k > 0:
                            turn_result(m - 1, n)

                wait(pe, ones_set, 1)
                for s in range(NS):
                    scores(0, 0, 0, s)
                turn_max(0)
                steps(pe, step)
                for h in range(2):
                    turn_result(QUADS - 1, h)

            @block.scalar
            def _(act):
                def step(m, k, i):
                    for n in range(NE):
                        (qc, kt), j = GROUPS[n // QH], n % QH
                        w = (qc + 1) * CH - max(kt * P, qc * CH)
                        wait(act, e_scores, m * NE + n + 1)
                        if j == 0:
                            wait(act, pv_done, m * NG + n // QH - 1)
                        act.activation(e[:, n // QH % 2, j, 0:w], p_e[n % 3][:, 0:w], ACT.Exp).then_inc(e_done, 1)

                steps(act, step)

            @block.vector
            def _(dve):
                def max_of(m, s):
                    j, (g, c) = s // len(CHUNKS), CHUNKS[s % len(CHUNKS)]
                    w = min((g + 1) * P - c * CH, CH)
                    if s == 0:
                        wait(dve, m_split, m)
                    wait(dve, s_ready[s % 2], m * (NS // 2) + s // 2 + 1)
                    at = s % len(CHUNKS)
                    dve.tensor_reduce(part_max[:, j, at:at + 1], p_s[s % 2][:, 0:w], AX, ALU.max, negate=True
                                      ).then_inc(s_read[s % 2], 1)

                def split_max(m):
                    for n in range(2):
                        wait(dve, s_read[n], (m + 1) * (NS // 2))
                    whole = part_max[:, :, 0:TPB]
                    a, b = part_max[:, :, TPC:TPB], part_max[:, :, TPB:TPB + TPC]
                    dve.tensor_tensor(a, a, b, ALU.min).then_inc(m_own, 1)
                    wait(dve, m_own, m * 4 + 1)
                    wait(dve, m_turned, m)
                    dve.tensor_copy(max_parts[:, 0, :, :], whole).then_inc(m_own, 1)
                    wait(dve, m_own, m * 4 + 2)
                    dve.tensor_tensor(rest_max[:, :, :], whole, max_parts[:, 0, :, :], ALU.subtract).then_inc(m_own, 1)
                    wait(dve, m_own, m * 4 + 3)
                    dve.tensor_copy(max_parts[:, 1, :, :], rest_max[:, :, :]).then_inc(m_own, 1)
                    wait(dve, m_own, m * 4 + 4)
                    dve.tensor_tensor(max_parts[:, 2, :, :], rest_max[:, :, :], max_parts[:, 1, :, :], ALU.subtract
                                      ).then_inc(m_split, 1)

                def copy_max(m):
                    wait(dve, m_turned, m + 1)
                    wait(dve, m_sent, m * (NP * 16))
                    dve.tensor_copy(max_rows[:, :], p_t[0:NP * QH * TPB, 0:P // 2].bitcast(BF16)).then_inc(m_copied, 1)

                def copy_result(m):
                    wait(dve, pv_done, (m + 1) * NG)
                    wait(dve, y_turned, m * 2)
                    dve.tensor_copy(y[:, :], p_y[:, :]).then_inc(y_copied, 1)

                def divide(m, h):
                    wait(dve, y_turned, m * 2 + h + 1)
                    p = p_t[:, :].rearrange("p (t j w) -> p t j w", t=TPC, j=QH)
                    dve.reciprocal(recip[:, h, :, :], p[:, :, :, HD]).then_inc(y_own, 1)
                    wait(dve, y_own, m * 2 + h + 1)
                    for t in range(TPC):
                        last_one = dve.tensor_tensor(Y[:, ds(at_turn(m * QH), QH), h * TPC + t, :], p[:, t, :, 0:HD],
                                                     recip[:, h, t, :].unsqueeze(2).to_broadcast([P, QH, HD]), ALU.mult)
                    last_one.then_inc(y_normed, 1)

                def step(m, k, i):
                    for what, n in SCHEDULE:
                        if what == "Y" and k > 0:
                            copy_result(m - 1)
                        elif what == "S" and not last(m, 1):
                            max_of(m + 1, n)
                        elif what == "M" and not last(m, 1):
                            split_max(m + 1)
                        elif what == "T" and not last(m, 1):
                            copy_max(m + 1)
                        elif what == "N" and k > 0:
                            divide(m - 1, n)

                dve.memset(p_y[:, :], 0.0).then_inc(y_copied, 1)
                dve.memset(max_all[:, :], 0.0).then_inc(cleared, 1)
                wait(dve, cleared, 1)
                dve.memset(k_[64:KM, :, :, :], 1.0).then_inc(ones_set, 1)
                for s in range(NS):
                    max_of(0, s)
                split_max(0)
                copy_max(0)
                steps(dve, step)
                copy_result(QUADS - 1)
                for h in range(2):
                    divide(QUADS - 1, h)


def errors(nc, V, shifted, Y):
    with nc.Block() as block:

        @block.vector
        def _(dve):
            for b in range(BATCH):
                for h in range(H):
                    dve.tensor_tensor(V[:, b * H + h, :, 0:HD], shifted[:, b * TPB:(b + 1) * TPB, h * HD:(h + 1) * HD],
                                      Y[:, b * H + h, :, :], ALU.subtract)


def project_out(nc, C, I, X, Y):
    G = NT // TPC
    with Stage(nc, "mix1_out") as S:
        W = S.sb("W", [P, D])
        bias = S.sb("bias", [1, D])
        bias2 = S.sb("bias2", [1, D])
        total = S.sb("total", [P, NT, D])
        totalT = S.sb("totalT", [P, TOK])
        p_turn = S.ps("p_turn", [P, 2, CH])
        p_out = S.ps("p_out", [P, 2, CH])
        loaded, own, summed = S.sem("loaded"), S.sem("own"), S.sem("summed")
        turned, stored, ready, added, bias_ok = (S.sem("turned"), S.sem("stored"), S.sem("ready"), S.sem("added"),
                                                 S.sem("bias_ok"))
        with nc.Block() as block:

            @block.sync
            def _(sp):
                sp.dma_start(W[:, :], I["L1_attn_W_proj"]).then_inc(loaded, 16)
                sp.dma_start(bias[:, :], I["L1_attn_b_proj"].unsqueeze(0)).then_inc(loaded, 16)

            @block.vector
            def _(dve):
                chain = Chain(dve, own)
                for b in range(BATCH):
                    chain.step(dve.memset(Y[1][0:1, b * H:(b + 1) * H, 0, :], 0.0))
                for b in range(BATCH):
                    for h in range(H):
                        last = dve.tensor_tensor(total[:, b * TPB:(b + 1) * TPB, h * HD:(h + 1) * HD], Y[0][:, b * H + h, :, :],
                                                 Y[1][:, b * H + h, :, :], ALU.add)
                    last.then_inc(summed, 1)
                dve.wait_ge(loaded, 32)
                dve.tensor_scalar(bias2[:, :], bias[:, :], 2.0, None, ALU.mult).then_inc(bias_ok, 1)
                for g in range(G):
                    t = slice(g * TPC, (g + 1) * TPC)
                    dve.wait_ge(ready, g + 1)
                    dve.tensor_tensor(X[:, t, :], X[:, t, :], p_out[:, g % 2, :].rearrange("p (t d) -> p t d", d=D),
                                      ALU.add).then_inc(added, 1)

            @block.tensor
            def _(pe):
                def turn(g):
                    pe.wait_ge(summed, g * TPC // TPB + 1)
                    if g >= 2:
                        pe.wait_ge(stored, g - 1)
                    for k in range(TPC):
                        mm = pe.transpose(p_turn[:, g % 2, k * P:(k + 1) * P], total[:, g * TPC + k, :], C.ident[:, :])
                    mm.then_inc(turned, 1)

                turn(0)
                pe.wait_ge(bias_ok, 1)
                for g in range(G):
                    if g + 1 < G:
                        turn(g + 1)
                    pe.wait_ge(stored, g + 1)
                    if g >= 2:
                        pe.wait_ge(added, g - 1)
                    for k in range(TPC):
                        t = g * TPC + k
                        pe.matmul(p_out[:, g % 2, k * D:(k + 1) * D], C.ones[0:1, :], bias2[:, :], start=True, stop=False)
                        mm = pe.matmul(p_out[:, g % 2, k * D:(k + 1) * D], totalT[:, t * P:(t + 1) * P], W[:, :],
                                       start=False, stop=True)
                    mm.then_inc(ready, 1)

            @block.scalar
            def _(act):
                for g in range(G):
                    act.wait_ge(turned, g + 1)
                    act.copy(totalT[:, g * CH:(g + 1) * CH], p_turn[:, g % 2, :]).then_inc(stored, 1)


AH, AD = 16, 64
DIST0 = SEQ - P


def alibi_attention_mixer(nc, C, I, X, xn, xnT):
    with Stage(nc, "mix2") as M:
        dist = M.sb("dist", [P, DIST0 + SEQ])
        slopes = M.sb("slopes", [P, AH])
        normalise(nc, C, "mix2_norm", xn, xn, xnT, gamma=C.row["L2_attn_ln_gamma"], beta=C.row["L2_attn_ln_beta"])
        with Stage(nc, "mix2_tables") as S:
            steps = S.sb("steps", [P, DIST0 + SEQ], mybir.dt.int32)
            signed = S.sb("signed", [P, DIST0 + SEQ])
            made, own = S.sem("made"), S.sem("own")
            with nc.Block() as block:

                @block.gpsimd
                def _(pool):
                    pool.iota(steps[:, :], pattern=[[-1, DIST0 + SEQ]], base=DIST0, channel_multiplier=1).then_inc(made, 1)
                    for h in range(AH):
                        pool.memset(slopes[:, h:h + 1], -float(np.float32(2.0 ** (-8.0 / (AH - h)))))

                @block.vector
                def _(dve):
                    chain = Chain(dve, own)
                    dve.wait_ge(made, 1)
                    chain.step(dve.tensor_copy(signed[:, :], steps[:, :]))
                    chain.step(dve.tensor_scalar(dist[:, :], signed[:, :], -1.0, None, ALU.mult))
                    chain.step(dve.tensor_tensor(dist[:, :], dist[:, :], signed[:, :], ALU.max))

        for b in range(BATCH):
            with Stage(nc, f"mix2_{b}") as S:
                V = S.sb("V", [P, AH, TPB, AD])
                head_values(nc, C, I, f"mix2_v{b}", b, xnT, V)
                alibi_heads(nc, C, I, f"mix2_h{b}", b, xnT, V, dist, slopes, X)


def head_values(nc, C, I, name, b, xnT, V):
    with Stage(nc, name) as S:
        Wv = S.sb("Wv", [P, AH * AD])
        p = S.ps("p", [P, 4, CH])
        loaded, ready, stored = S.sem("loaded"), S.sem("ready"), S.sem("stored")
        HC = CH // AD
        with nc.Block() as block:

            @block.sync
            def _(sp):
                sp.dma_start(Wv[:, :], I["L2_attn_Wv"]).then_inc(loaded, 16)

            @block.tensor
            def _(pe):
                pe.wait_ge(loaded, 16)
                for t in range(TPB):
                    for c in range(2):
                        i = t * 2 + c
                        if i >= 4:
                            pe.wait_ge(stored, i - 3)
                        pe.matmul(p[:, i % 4, :], xnT[:, b * SEQ + t * P:b * SEQ + (t + 1) * P], Wv[:, c * CH:(c + 1) * CH],
                                  start=True, stop=True).then_inc(ready, 1)

            @block.scalar
            def _(act):
                for t in range(TPB):
                    for c in range(2):
                        i = t * 2 + c
                        act.wait_ge(ready, i + 1)
                        act.copy(V[:, c * HC:(c + 1) * HC, t, 0:AD], p[:, i % 4, :].rearrange("p (h d) -> p h d", d=AD)
                                 ).then_inc(stored, 1)


def alibi_heads(nc, C, I, name, b, xnT, V, dist, slopes, X):
    NS = 2 * TPB
    SLOTS = 4
    SCHEDULE = []
    for t in range(TPB):
        SCHEDULE += [("S", 2 * t, 0), ("S", 2 * t + 1, 0), ("X", t, 0), ("T", (t - 1) % TPB, int(t == 0))]
        SCHEDULE += {0: [("V", 3, 1), ("Y", 0, 1), ("R", 0, 1)],
                     1: [("V", 4, 1), ("P", 0, 0)],
                     2: [("V", 5, 1), ("L", 0, 0), ("o", 0, 1)],
                     3: [("V", 6, 1), ("P", 1, 0)],
                     4: [("V", 7, 1), ("Y", 1, 1), ("L", 1, 0)],
                     5: [("V", 0, 0), ("o", 1, 1)],
                     6: [("V", 1, 0)],
                     7: [("V", 2, 0)]}[t]

    with Stage(nc, name) as S:
        wqk = [S.sb(f"wqk{k}", [P, 2 * AD]) for k in range(SLOTS)]
        wo = [S.sb(f"wo{k}", [P, D]) for k in range(SLOTS)]
        sums = [S.sb(f"sums{k}", [P, TPB]) for k in range(SLOTS)]
        recip = [S.sb(f"recip{k}", [P, TPB]) for k in range(SLOTS)]
        q1 = [S.sb(f"q1_{k}", [P, SEQ], F32R) for k in range(2)]
        k1 = [S.sb(f"k1_{k}", [P, SEQ], F32R) for k in range(2)]
        k2 = [S.sb(f"k2_{k}", [AD, SEQ], F32R) for k in range(2)]
        bias = [S.sb(f"bias{k}", [P, DIST0 + SEQ]) for k in range(2)]
        vals = [S.sb(f"vals{k}", [P, TPB, AD]) for k in range(2)]
        slope = S.sb("slope", [P, 1])
        start, zero = S.sb("start", [1, NS]), C.zeros[0:1, 0:1]
        half_max = S.sb("half_max", [P, TPB, 2])
        neg_max = S.sb("neg_max", [P, TPB])
        weights = [S.sb(f"weights{k}", [P, SEQ]) for k in range(2)]
        turned = [S.sb(f"turned{c}", [P, TPB, CH]) for c in range(2)]
        y = [S.sb(f"y{c}", [P, CH]) for c in range(2)]
        p_p = S.ps("p_p", [P, CH])
        p_s = [S.ps(f"p_s{k}", [P, CH]) for k in range(2)]
        p_t = [S.ps(f"p_t{k}", [P, CH]) for k in range(2)]
        p_y = [S.ps(f"p_y{c}", [P, CH]) for c in range(2)]
        p_x = S.ps("p_x", [P, CH])
        loaded = [S.sem(f"loaded{k}") for k in range(SLOTS)]
        sloped, bias_ready, vals_ready = S.sem("sloped"), S.sem("bias_ready"), S.sem("vals_ready")
        p_ready, high_done, low_done = S.sem("p_ready"), S.sem("high_done"), S.sem("low_done")
        s_ready, s_read, max_done, x_done = S.sem("s_ready"), S.sem("s_read"), S.sem("max_done"), S.sem("x_done")
        t_ready = [S.sem(f"t_ready{h}") for h in range(2)]
        t_stored = [S.sem(f"t_stored{h}") for h in range(2)]
        v_done, y_copied, r_done = S.sem("v_done"), S.sem("y_copied"), S.sem("r_done")
        o_ready, o_added = S.sem("o_ready"), S.sem("o_added")

        def steps(eng, step):
            step(0, 0)
            with eng.Fori(0, AH // SLOTS - 1) as i:
                for k in range(1, SLOTS + 1):
                    step(Count(i, SLOTS, k), k % SLOTS)
            for u in range(AH - SLOTS + 1, AH):
                step(u, u % SLOTS)

        def exists(u, ahead):
            return not isinstance(u, int) or 0 <= u + ahead < AH

        def entries(u, k):
            for what, n, before in SCHEDULE:
                if what in "PL":
                    if exists(u, 1):
                        yield what, n, u + 1, (k + 1) % SLOTS
                elif exists(u, -before):
                    yield what, n, u - before, (k - before) % SLOTS

        LEFT = [(what, n) for what, n, before in SCHEDULE if before]

        with nc.Block() as block:

            @block.sync
            def _(sp):
                def fetch(u, k):
                    head = ds(at_turn(u * AD), AD)
                    for half, W in enumerate((I["L2_attn_Wq"], I["L2_attn_Wk"])):
                        cols = slice(half * AD, (half + 1) * AD)
                        sp.dma_start(wqk[k][:, cols], W[:, head]).then_inc(loaded[k], 16)
                        sp.dma_start(wo[k][cols, :], I["L2_attn_Wo"][head, :]).then_inc(loaded[k], 16)

                def step(u, k):
                    if exists(u, 3):
                        wait(sp, o_added, u * 2)
                        fetch(u + 3, (k + 3) % SLOTS)

                for u in range(3):
                    fetch(u, u)
                steps(sp, step)

            @block.gpsimd
            def _(pool):
                def prepare(u, k):
                    pool.tensor_copy(slope[:, :], slopes[:, ds(at_turn(u), 1)]).then_inc(sloped, 1)
                    wait(pool, sloped, u + 1)
                    wait(pool, s_read, (u - 1) * NS)
                    pool.tensor_tensor(bias[k % 2][:, :], dist[:, :], slope[:, 0:1].to_broadcast([P, DIST0 + SEQ]), ALU.mult
                                       ).then_inc(bias_ready, 1)
                    wait(pool, bias_ready, u + 1)
                    wait(pool, v_done, (u - 1) * TPB)
                    pool.tensor_copy(vals[k % 2][:, :, :], V[:, ds(at_turn(u), 1), :, :].rearrange("p u t d -> p (u t) d")
                                     ).then_inc(vals_ready, 1)

                def step(u, k):
                    if exists(u, 1):
                        prepare(u + 1, k + 1)

                prepare(0, 0)
                steps(pool, step)

            @block.tensor
            def _(pe):
                def project(u, k, c):
                    if c == 0:
                        wait(pe, loaded[k], (u - k) * (64 // SLOTS) + 64)
                    wait(pe, low_done, u * 2 + c)
                    at = b * SEQ + c * CH
                    pe.matmul(p_p[:, :], wqk[k][:, :], xnT[:, at:at + CH], start=True, stop=True).then_inc(p_ready, 1)

                def scores(u, k, g):
                    t, c = g // 2, g % 2
                    if g == 0:
                        wait(pe, low_done, u * 2 + 2)
                    wait(pe, s_read, u * NS + g - 1)
                    keys = slice(c * CH, (c + 1) * CH)
                    queries = slice(t * P, (t + 1) * P)
                    pe.matmul(p_s[c][:, :], q1[k % 2][:, queries], k1[k % 2][:, keys], start=True, stop=False)
                    pe.matmul(p_s[c][:, :], q1[k % 2][0:AD, queries], k2[k % 2][:, keys], start=False, stop=True
                              ).then_inc(s_ready, 1)

                def turn(u, t):
                    wait(pe, x_done, u * TPB + t + 1)
                    for h in range(2):
                        wait(pe, t_stored[h], u * TPB + t)
                        for j in range(TPC):
                            at = (h * TPC + j) * P
                            mm = pe.transpose(p_t[h][:, j * P:(j + 1) * P], weights[t % 2][:, at:at + P], C.ident[:, :])
                        mm.then_inc(t_ready[h], 1)

                def times_values(u, k, n):
                    c, pair = n // 4, n % 4
                    if pair == 0:
                        for h in range(2):
                            wait(pe, t_stored[h], u * TPB + (c + 1) * TPC)
                        wait(pe, vals_ready, u + 1)
                        wait(pe, y_copied, u * 2 + c - 1)
                    for half in range(2):
                        j = pair * 2 + half
                        mm = pe.matmul(p_y[c][half * AD:(half + 1) * AD, :], vals[k % 2][:, j, :], turned[c][:, j, :],
                                       start=(pair == 0), stop=(pair == 3), skip_group_check=True,
                                       tile_position=(0, half * AD))
                    mm.then_inc(v_done, 1)

                def output(u, k, c):
                    wait(pe, y_copied, u * 2 + c + 1)
                    wait(pe, o_added, u * 2 + c)
                    for t in range(TPC):
                        mm = pe.matmul(p_x[:, t * P:(t + 1) * P], y[c][:, t * P:(t + 1) * P], wo[k][:, :],
                                       start=True, stop=True)
                    mm.then_inc(o_ready, 1)

                def do(what, n, u, k):
                    if what == "S":
                        scores(u, k, n)
                    elif what == "T":
                        turn(u, n)
                    elif what == "V":
                        times_values(u, k, n)
                    elif what == "P":
                        project(u, k, n)
                    elif what == "o":
                        output(u, k, n)

                def step(u, k):
                    for entry in entries(u, k):
                        do(*entry)

                for c in range(2):
                    project(0, 0, c)
                steps(pe, step)
                for what, n in LEFT:
                    do(what, n, AH - 1, (AH - 1) % SLOTS)

            @block.scalar
            def _(act):
                def high_parts(u, k, half):
                    c = slice(half * CH, (half + 1) * CH)
                    wait(act, p_ready, u * 2 + half + 1)
                    if half == 0:
                        wait(act, s_ready, (u - 1) * NS)
                    act.activation(q1[k % 2][0:AD, c], p_p[0:AD, :], ACT.Copy, scale=AD ** -0.5)
                    act.copy(k1[k % 2][AD:P, c], p_p[AD:P, :])
                    act.copy(k1[k % 2][0:AD, c], p_p[AD:P, :]).then_inc(high_done, 1)

                def exp_tile(u, k, t):
                    wait(act, max_done, u * TPB + t + 1)
                    act.activation(weights[t % 2][:, :], weights[t % 2][:, :], ACT.Exp, bias=neg_max[:, t:t + 1],
                                   accum_out=sums[k][:, t:t + 1]).then_inc(x_done, 1)

                def store_turned(u, t):
                    c, at = t // TPC, t % TPC * P
                    if at == 0:
                        wait(act, v_done, (u - 1) * TPB + (c + 1) * 4)
                    wait(act, t_ready[0], u * TPB + t + 1)
                    act.copy(turned[c][:, 0:TPC, at:at + P], p_t[0][:, :].rearrange("p (t a) -> p t a", a=P)
                             ).then_inc(t_stored[0], 1)

                def copy_result(u, c):
                    wait(act, v_done, u * TPB + c * 4 + 4)
                    wait(act, o_ready, u * 2)
                    act.copy(y[c][:, :], p_y[c][:, :]).then_inc(y_copied, 1)

                def do(what, n, u, k):
                    if what == "P":
                        high_parts(u, k, n)
                    elif what == "X":
                        exp_tile(u, k, n)
                    elif what == "T":
                        store_turned(u, n)
                    elif what == "Y":
                        copy_result(u, n)

                def step(u, k):
                    for entry in entries(u, k):
                        do(*entry)

                for c in range(2):
                    high_parts(0, 0, c)
                steps(act, step)
                for what, n in LEFT:
                    do(what, n, AH - 1, (AH - 1) % SLOTS)

            @block.vector
            def _(dve):
                def low_parts(u, k, half):
                    c = slice(half * CH, (half + 1) * CH)
                    wait(dve, high_done, u * 2 + half + 1)
                    if half == 0:
                        wait(dve, s_ready, (u - 1) * NS)
                    dve.scalar_tensor_tensor(out=q1[k % 2][AD:P, c], in0=p_p[0:AD, :], scalar=AD ** -0.5,
                                             in1=q1[k % 2][0:AD, c].bitcast(F32), op0=ALU.mult, op1=ALU.subtract)
                    dve.tensor_tensor(k2[k % 2][:, c], p_p[AD:P, :], k1[k % 2][AD:P, c].bitcast(F32), ALU.subtract
                                      ).then_inc(low_done, 1)

                def max_of(u, k, g):
                    t, c = g // 2, g % 2
                    if g == 0:
                        wait(dve, bias_ready, u + 1)
                    if c == 0:
                        wait(dve, t_ready[1], u * TPB + t - 1)
                    wait(dve, s_ready, u * NS + g + 1)
                    dve.tensor_copy(start[:, g:g + 1], zero[:, :])
                    at = DIST0 - t * P + c * CH
                    dve.tensor_tensor_reduce(weights[t % 2][:, c * CH:(c + 1) * CH], p_s[c][:, :],
                                             bias[k % 2][:, at:at + CH], 1.0, -3.0e38, ALU.add, ALU.max,
                                             half_max[:, t, c:c + 1]).then_inc(s_read, 1)
                    if c == 1:
                        wait(dve, s_read, u * NS + g + 1)
                        dve.tensor_reduce(neg_max[:, t:t + 1], half_max[:, t, :], AX, ALU.max, negate=True
                                          ).then_inc(max_done, 1)

                def store_turned(u, t):
                    c, at = t // TPC, t % TPC * P
                    if at == 0:
                        wait(dve, v_done, (u - 1) * TPB + (c + 1) * 4)
                    wait(dve, t_ready[1], u * TPB + t + 1)
                    dve.tensor_copy(turned[c][:, TPC:TPB, at:at + P], p_t[1][:, :].rearrange("p (t a) -> p t a", a=P)
                                    ).then_inc(t_stored[1], 1)

                def reciprocals(u, k):
                    wait(dve, x_done, (u + 1) * TPB)
                    dve.reciprocal(recip[k][:, :], sums[k][:, :]).then_inc(r_done, 1)

                def add_output(u, k, c):
                    wait(dve, r_done, u + 1)
                    wait(dve, o_ready, u * 2 + c + 1)
                    wait(dve, o_added, u * 2 + c)
                    for t in range(TPC):
                        tile = b * TPB + c * TPC + t
                        added = dve.scalar_tensor_tensor(out=X[:, tile, :], in0=p_x[:, t * P:(t + 1) * P],
                                                         scalar=recip[k][:, c * TPC + t:c * TPC + t + 1],
                                                         in1=X[:, tile, :], op0=ALU.mult, op1=ALU.add)
                    added.then_inc(o_added, 1)

                def do(what, n, u, k):
                    if what == "S":
                        max_of(u, k, n)
                    elif what == "T":
                        store_turned(u, n)
                    elif what == "L":
                        low_parts(u, k, n)
                    elif what == "R":
                        reciprocals(u, k)
                    elif what == "o":
                        add_output(u, k, n)

                def step(u, k):
                    for entry in entries(u, k):
                        do(*entry)

                for c in range(2):
                    low_parts(0, 0, c)
                steps(dve, step)
                for what, n in LEFT:
                    do(what, n, AH - 1, (AH - 1) % SLOTS)


def add_turned(nc, C, name, X, outT):
    with Stage(nc, name) as S:
        p = S.ps("p", [P, NCH, CH])
        ready = S.sem("ready")
        with nc.Block() as block:

            @block.tensor
            def _(pe):
                for g in range(NCH):
                    for k in range(TPC):
                        t = g * TPC + k
                        mm = pe.transpose(p[:, g, k * P:(k + 1) * P], outT[:, t * P:(t + 1) * P], C.ident[:, :])
                    mm.then_inc(ready, 1)

            @block.vector
            def _(dve):
                for g in range(NCH):
                    t = slice(g * TPC, (g + 1) * TPC)
                    dve.wait_ge(ready, g + 1)
                    dve.tensor_tensor(X[:, t, :], X[:, t, :], p[:, g, :].rearrange("p (t d) -> p t d", d=D), ALU.add)


TWO_PI = (6.28125, 0.0019350051879882812, 3.0199159819567e-07)
ROUND = 1.5 * 2.0 ** 23


def resonant_mixer(nc, C, X, xn):
    with Stage(nc, "mix3") as S:
        lmlg, theta, last = (C.row["L3_attn_" + r] for r in ("lmlg", "theta", "last_conv_init"))
        gamma = S.sb("gamma", [P, D])
        turns = S.sb("turns", [P, D])
        angle = S.sb("angle", [P, D])
        re_c = S.sb("re_c", [P, D])
        past0 = S.sb("past0", [P, D])
        past1 = S.sb("past1", [P, D])
        y0 = S.sb("y0", [P, TPB, D])
        y1 = S.sb("y1", [P, TPB, D])
        own, own_act, own_pool = S.sem("own"), S.sem("own_act"), S.sem("own_pool")
        decayed, reduced, cos_done, past_done = S.sem("decayed"), S.sem("reduced"), S.sem("cos_done"), S.sem("past_done")
        x0, x1 = xn[:, 0:TPB, :], xn[:, TPB:NT, :]
        with nc.Block() as block:

            @block.scalar
            def _(act):
                chain = Chain(act, own_act)
                chain.step(act.activation(gamma[:, :], lmlg, ACT.Exp))
                act.activation(gamma[:, :], gamma[:, :], ACT.Exp, scale=-1.0).then_inc(decayed, 1)
                act.wait_ge(reduced, 1)
                act.activation(re_c[:, :], angle[:, :], ACT.Sin).then_inc(cos_done, 1)

            @block.vector
            def _(dve):
                chain = Chain(dve, own)
                chain.step(dve.tensor_scalar(turns[:, :], theta, float(1.0 / (2 * np.pi)), None, ALU.mult))
                chain.step(dve.tensor_scalar(turns[:, :], turns[:, :], ROUND, None, ALU.add))
                chain.step(dve.tensor_scalar(turns[:, :], turns[:, :], -ROUND, None, ALU.add))
                chain.step(dve.tensor_copy(angle[:, :], theta))
                for part in TWO_PI:
                    chain.step(dve.scalar_tensor_tensor(out=angle[:, :], in0=turns[:, :], scalar=-part, in1=angle[:, :],
                                                        op0=ALU.mult, op1=ALU.add))
                chain.step(dve.tensor_scalar(turns[:, :], angle[:, :], -1.0, None, ALU.mult))
                chain.step(dve.tensor_tensor(angle[:, :], angle[:, :], turns[:, :], ALU.max))
                dve.tensor_scalar(angle[:, :], angle[:, :], -1.0, float(np.pi / 2), ALU.mult, ALU.add).then_inc(reduced, 1)
                dve.wait_ge(decayed, 1)
                dve.wait_ge(cos_done, 1)
                chain.step(dve.tensor_tensor(re_c[:, :], re_c[:, :], gamma[:, :], ALU.mult))
                chain.step(dve.tensor_tensor(past0[:, :], re_c[:, :], last, ALU.mult))
                chain.step(dve.tensor_tensor(past1[:, :], re_c[:, :], re_c[:, :], ALU.mult))
                chain.step(dve.tensor_tensor(gamma[:, :], gamma[:, :], gamma[:, :], ALU.mult))
                chain.step(dve.scalar_tensor_tensor(out=past1[:, :], in0=past1[:, :], scalar=2.0, in1=gamma[:, :],
                                                    op0=ALU.mult, op1=ALU.subtract))
                dve.tensor_tensor(past1[:, :], past1[:, :], last, ALU.mult).then_inc(past_done, 1)
                dve.wait_ge(past_done, 1)
                chain.step(dve.tensor_tensor(y1[:, :, :], x0, per_feature(re_c[:, :], TPB), ALU.mult))
                chain.step(dve.tensor_tensor(y1[:, :, :], y1[:, :, :], per_feature(past1[:, :], TPB), ALU.add))
                chain.step(dve.tensor_tensor(y1[:, :, :], y1[:, :, :], x1, ALU.add))
                chain.step(dve.tensor_tensor(y1[:, :, :], y1[:, :, :], x1, ALU.mult))
                dve.tensor_tensor(X[:, TPB:NT, :], X[:, TPB:NT, :], y1[:, :, :], ALU.add)

            @block.gpsimd
            def _(pool):
                chain = Chain(pool, own_pool)
                pool.wait_ge(past_done, 1)
                chain.step(pool.tensor_tensor(y0[:, :, :], x0, per_feature(past0[:, :], TPB), ALU.add))
                chain.step(pool.tensor_tensor(y0[:, :, :], y0[:, :, :], x0, ALU.mult))
                pool.tensor_tensor(X[:, 0:TPB, :], X[:, 0:TPB, :], y0[:, :, :], ALU.add)


SE = 16
SLOT = 64
NSLOT = SE * SLOT
ST = NSLOT // P
SFF = 256
MSF = SFF // P


def slot_directions(nc, C, I, se_parts):
    with Stage(nc, "slots") as S:
        raw = S.sb("raw", [P, ST, D])
        gamma, beta = S.sb("gamma", [P, D]), S.sb("beta", [P, D])
        load(nc, "slots_load", [(raw[:, :, :], I["L3_ffn_slot_embeds"].rearrange("e s d -> (e s) d").rearrange(
                                    "(t p) d -> p t d", p=P))])
        with nc.Block() as block:

            @block.vector
            def _(dve):
                dve.tensor_scalar(gamma[:, :], C.row["L3_ffn_slot_g"], C.scale[:, 0:1], None, ALU.mult)
                dve.tensor_scalar(beta[:, :], C.row["L3_ffn_slot_b"], C.scale[:, 0:1], None, ALU.mult)

        seT = S.sb("seT", [P, NSLOT])
        high_done = S.sem("high_done")
        normalise(nc, C, "slots_norm", raw, raw, seT, gamma=gamma[:, :], beta=beta[:, :], tiles=ST)
        with nc.Block() as block:

            @block.scalar
            def _(act):
                act.copy(se_parts[0][:, :], seT[:, :]).then_inc(high_done, 1)

            @block.vector
            def _(dve):
                dve.wait_ge(high_done, 1)
                dve.tensor_tensor(se_parts[1][:, :], seT[:, :], se_parts[0][:, :].bitcast(F32), ALU.subtract)


def soft_moe_ffn(nc, C, I, name, X, xn, xnT, se_parts):
    with Stage(nc, name) as M:
        slotsT = M.sb("slotsT", [P, SE, BATCH, SLOT])
        eout = M.sb("eout", [P, BATCH, ST, D])
        outT = M.sb("outT", [P, TOK])
        normalise(nc, C, name + "_norm", xn, xn, xnT, gamma=C.row["L3_ffn_norm_g"], beta=C.row["L3_ffn_norm_b"])
        x_parts = [M.sb(f"x_{part}", [P, TOK], F32R) for part in ("high", "low")]

        def half(x, b):
            return x[:, b * SEQ:(b + 1) * SEQ]

        def halves(b):
            return [half(x, b) for x in x_parts]

        def slots(b):
            return se_parts

        softmax_apply(nc, C, name + "_in", slots, halves, lambda b: xn[:, b * TPB:(b + 1) * TPB, :],
                      lambda b: slotsT[:, :, b, :], 1.0, lambda b: (half(xnT, b), *halves(b)))
        slot_experts(nc, C, I, name + "_exp", slotsT, eout)
        softmax_apply(nc, C, name + "_out", halves, slots, lambda b: eout[:, b, :, :],
                      lambda b: half(outT, b).rearrange("p (e s) -> p e s", s=SLOT), 0.5, None)
        add_turned(nc, C, name + "_add", X, outT)


def softmax_apply(nc, C, name, A, B, W, dst, factor, x_split):
    GT = TPC
    TILES = BATCH * TPB
    GROUPS = TILES // GT
    PASSES = ((0, 0), (0, 1), (1, 0))
    with Stage(nc, name) as S:
        w_parts = [[S.sb(f"w{b}_{part}", [P, TPB, D], F32R) for part in ("high", "low")] for b in range(BATCH)]
        neg_max = [S.sb(f"neg_max{k}", [P, 1]) for k in range(2)]
        total = [S.sb(f"total{k}", [P, 1]) for k in range(2)]
        recip = [S.sb(f"recip{k}", [P, 1]) for k in range(2)]
        e = [S.sb(f"e{k}", [P, SEQ]) for k in range(2)]
        turned = [[S.sb(f"turned{k}_{part}", [P, TPB, CH], F32R) for part in ("high", "low")] for k in range(2)]
        p_s = [S.ps(f"p_s{k}", [P, SEQ]) for k in range(2)]
        p_t = [S.ps(f"p_t{k}", [P, CH]) for k in range(2)]
        p_w = S.ps("p_w", [P, CH])
        s_ready, max_done, exp_done = S.sem("s_ready"), S.sem("max_done"), S.sem("exp_done")
        recip_done, e_ready = S.sem("recip_done"), S.sem("e_ready")
        t_ready = [S.sem(f"t_ready{h}") for h in range(2)]
        t_high = [S.sem(f"t_high{h}") for h in range(2)]
        t_stored = [S.sem(f"t_stored{h}") for h in range(2)]
        w_ready, w_stored = S.sem("w_ready"), S.sem("w_stored")
        split_high, split_done = S.sem("split_high"), S.sem("split_done")

        SPLITS, scores_need, weights_need = [], [], []
        for b in range(BATCH):
            if x_split:
                SPLITS.append((-1 if b == 0 else TPB - 4, *x_split(b)))
            scores_need.append(len(SPLITS) if x_split else 0)
            SPLITS.append((1 if b == 0 else TPB - 2, W(b), *(x[:, :, :] for x in w_parts[b])))
            weights_need.append(len(SPLITS))

        def place(i, h, part):
            return turned[i // GT % 2][part][:, h * 4:h * 4 + 4, i % GT * P:(i % GT + 1) * P]

        with nc.Block() as block:

            @block.tensor
            def _(pe):
                def scores(i):
                    if i >= TILES:
                        return
                    b, t = i // TPB, i % TPB
                    wait(pe, split_done, scores_need[b])
                    wait(pe, exp_done, i - 1)
                    for c in range(2):
                        for x, y in PASSES:
                            mm = pe.matmul(p_s[i % 2][:, c * CH:(c + 1) * CH], A(b)[x][:, t * P:(t + 1) * P],
                                           B(b)[y][:, c * CH:(c + 1) * CH], start=(x + y == 0), stop=(x == 1))
                    mm.then_inc(s_ready, 1)

                def turn(i):
                    wait(pe, e_ready, i + 1)
                    for h in range(2):
                        wait(pe, t_stored[h], i)
                        for j in range(4):
                            at = (h * 4 + j) * P
                            mm = pe.transpose(p_t[h][:, j * P:(j + 1) * P], e[i % 2][:, at:at + P], C.ident[:, :])
                        mm.then_inc(t_ready[h], 1)

                def weigh(g, piece):
                    b = g * GT // TPB
                    if piece == 0:
                        wait(pe, split_done, weights_need[b])
                        wait(pe, w_stored, g)
                        for h in range(2):
                            wait(pe, t_stored[h], (g + 1) * GT)
                    for k in (2 * piece, 2 * piece + 1):
                        for x, y in PASSES:
                            mm = pe.matmul(p_w[:, :], w_parts[b][x][:, k, :], turned[g % 2][y][:, k, :],
                                           start=(k + x + y == 0), stop=(k == TPB - 1 and x == 1))
                    if piece == GT - 1:
                        mm.then_inc(w_ready, 1)

                scores(0)
                scores(1)
                for i in range(TILES):
                    turn(i)
                    scores(i + 2)
                    if i >= GT:
                        weigh(i // GT - 1, i % GT)
                for piece in range(GT):
                    weigh(GROUPS - 1, piece)

            @block.scalar
            def _(act):
                def split(i):
                    for when, src, high, low in SPLITS:
                        if when == i:
                            act.copy(high, src).then_inc(split_high, 1)

                def exp(i):
                    if i < TILES:
                        wait(act, max_done, i + 1)
                        wait(act, t_ready[1], i - 1)
                        act.activation(e[i % 2][:, :], p_s[i % 2][:, :], ACT.Exp, bias=neg_max[i % 2][:, 0:1],
                                       accum_out=total[i % 2][:, 0:1]).then_inc(exp_done, 1)

                split(-1)
                exp(0)
                for i in range(TILES):
                    for h in range(2):
                        wait(act, t_ready[h], i + 1)
                        wait(act, w_ready, i // GT - 1)
                        act.copy(place(i, h, 0), p_t[h][:, :].rearrange("p (t a) -> p t a", a=P)).then_inc(t_high[h], 1)
                    exp(i + 1)
                    split(i)

            @block.vector
            def _(dve):
                def split(i):
                    for n, (when, src, high, low) in enumerate(SPLITS):
                        if when == i:
                            wait(dve, split_high, n + 1)
                            dve.tensor_tensor(low, src, high.bitcast(F32), ALU.subtract).then_inc(split_done, 1)

                def maximum(i):
                    if i < TILES:
                        wait(dve, s_ready, i + 1)
                        dve.tensor_reduce(neg_max[i % 2][:, 0:1], p_s[i % 2][:, :], AX, ALU.max, negate=True
                                          ).then_inc(max_done, 1)

                def store(g):
                    wait(dve, w_ready, g + 1)
                    b, half = g * GT // TPB, g % (TPB // GT)
                    dve.tensor_copy(dst(b)[:, half * 8:(half + 1) * 8, :], p_w[:, :].rearrange("p (e s) -> p e s", s=SLOT)
                                    ).then_inc(w_stored, 1)

                def divide(i):
                    if i < TILES:
                        wait(dve, exp_done, i + 1)
                        dve.reciprocal(recip[i % 2][:, 0:1], total[i % 2][:, 0:1]).then_inc(recip_done, 1)
                        wait(dve, recip_done, i + 1)
                        dve.tensor_scalar(e[i % 2][:, :], e[i % 2][:, :], recip[i % 2][:, 0:1], factor, ALU.mult, ALU.mult
                                          ).then_inc(e_ready, 1)

                split(-1)
                maximum(0)
                maximum(1)
                divide(0)
                for i in range(TILES):
                    for h in range(2):
                        wait(dve, t_high[h], i + 1)
                        dve.tensor_tensor(place(i, h, 1), p_t[h][:, :].rearrange("p (t a) -> p t a", a=P),
                                          place(i, h, 0).bitcast(F32), ALU.subtract).then_inc(t_stored[h], 1)
                    divide(i + 1)
                    split(i)
                    if i >= GT and i % GT == GT - 1:
                        store(i // GT - 1)
                    maximum(i + 2)
                store(GROUPS - 1)


def slot_experts(nc, C, I, name, slotsT, eout):
    K = 4
    with Stage(nc, name) as S:
        wg = [S.sb(f"wg{k}", [P, SFF]) for k in range(K)]
        wu = [S.sb(f"wu{k}", [P, SFF]) for k in range(K)]
        wd = [S.sb(f"wd{k}", [P, MSF, D]) for k in range(K)]
        b_rows = S.sb("b_rows", [2 * SE * MSF, P])
        b_cols = S.sb("b_cols", [P, 2, SE * MSF])
        bias = [S.sb(f"bias{k}", [P, 2, MSF]) for k in range(2)]
        bd = S.sb("bd", [P, ST, D])
        gate = [S.sb(f"gate{k}", [P, MSF, P]) for k in range(2)]
        hidden = [S.sb(f"hidden{k}", [P, MSF, P]) for k in range(2)]
        p_up = [S.ps(f"p_up{k}", [P, 2, MSF, P]) for k in range(2)]
        p_out = [S.ps(f"p_out{k}", [P, BATCH, CH // 2]) for k in range(2)]
        p_b = S.ps("p_b", [P, CH])
        loaded = [S.sem(f"loaded{k}") for k in range(K)]
        b_loaded, b_turned, b_stored = S.sem("b_loaded"), S.sem("b_turned"), S.sem("b_stored")
        b_set, up_ready, gate_done, hidden_done = S.sem("b_set"), S.sem("up_ready"), S.sem("gate_done"), S.sem("hidden_done")
        down_done, stored = S.sem("down_done"), S.sem("stored")
        with nc.Block() as block:

            @block.sync
            def _(sp):
                def fetch(e, k):
                    sp.dma_start(wg[k][:, :], I["L3_ffn_Wg"][ds(e, 1)].rearrange("e d f -> d (e f)")).then_inc(loaded[k], 16)
                    sp.dma_start(wu[k][:, :], I["L3_ffn_Wu"][ds(e, 1)].rearrange("e d f -> d (e f)")).then_inc(loaded[k], 16)
                    sp.dma_start(wd[k][:, :, :], I["L3_ffn_Wd"][ds(e, 1)].rearrange("e (m p) d -> p (e m) d", p=P)
                                 ).then_inc(loaded[k], 16)

                sp.dma_start(b_rows[0:SE * MSF, :], I["L3_ffn_bg"].rearrange("e (m p) -> (e m) p", p=P)).then_inc(b_loaded, 16)
                sp.dma_start(b_rows[SE * MSF:, :], I["L3_ffn_bu"].rearrange("e (m p) -> (e m) p", p=P)).then_inc(b_loaded, 16)
                for h in range(2):
                    sp.dma_start(bd[h * SLOT:(h + 1) * SLOT, :, :],
                                 I["L3_ffn_bd"].rearrange("(t h) d -> h t d", h=2)[h].partition_broadcast(SLOT)
                                 ).then_inc(b_loaded, 16)
                for k in range(K):
                    fetch(k, k)
                with sp.Fori(0, SE // K - 1) as i:
                    for k in range(K):
                        sp.wait_ge(down_done, i * K + k + 1)
                        fetch(i * K + K + k, k)

            @block.tensor
            def _(pe):
                def up(i, k):
                    e = i * K + k
                    pe.wait_ge(loaded[k], i * 48 + 48)
                    pe.wait_ge(hidden_done, e - 1 if k > 1 else i * K)
                    for j, w in enumerate((wg, wu)):
                        for m in range(MSF):
                            mm = pe.matmul(p_up[k % 2][:, j, m, :], w[k][:, m * P:(m + 1) * P], slotsT[:, ds(e, 1), :, :],
                                           start=True, stop=True)
                    mm.then_inc(up_ready, 1)

                def down(i, k):
                    pe.wait_ge(hidden_done, i * K + k + 1)
                    if k % 2 == 0:
                        pe.wait_ge(stored, i * 2 + k // 2 - 1 if k // 2 > 1 else i * 2)
                    h = slice(k % 2 * SLOT, (k % 2 + 1) * SLOT)
                    for b in range(BATCH):
                        for m in range(MSF):
                            mm = pe.matmul(p_out[k // 2][h, b, 0:D], hidden[k % 2][:, m, b * SLOT:(b + 1) * SLOT],
                                           wd[k][:, m, :], start=(m == 0), stop=(m == MSF - 1),
                                           tile_position=(0, k % 2 * SLOT))
                    mm.then_inc(down_done, 1)

                pe.wait_ge(b_loaded, 64)
                pe.transpose(p_b[:, 0:2 * SE * MSF], b_rows[:, :], C.ident[0:2 * SE * MSF, 0:2 * SE * MSF]
                             ).then_inc(b_turned, 1)
                with pe.Fori(0, SE // K) as i:
                    up(i, 0)
                    for k in range(K):
                        if k + 1 < K:
                            up(i, k + 1)
                        down(i, k)

            @block.scalar
            def _(act):
                with act.Fori(0, SE // K) as i:
                    for k in range(K):
                        e = i * K + k
                        act.wait_ge(b_set, e + 1)
                        act.wait_ge(up_ready, e + 1)
                        for m in range(MSF):
                            ins = act.activation(gate[k % 2][:, m, :], p_up[k % 2][:, 0, m, :], ACT.Gelu,
                                                 bias=bias[k % 2][:, 0, m:m + 1])
                        ins.then_inc(gate_done, 1)

            @block.vector
            def _(dve):
                dve.wait_ge(b_turned, 1)
                dve.tensor_copy(b_cols[:, :, :], p_b[:, 0:2 * SE * MSF].rearrange("p (j c) -> p j c", j=2)
                                ).then_inc(b_stored, 1)
                dve.wait_ge(b_stored, 1)
                with dve.Fori(0, SE // K) as i:
                    def set_bias(k):
                        e = i * K + k
                        dve.wait_ge(hidden_done, e - 1 if k > 1 else i * K)
                        dve.tensor_copy(bias[k % 2][:, :, :], b_cols[:, :, ds(e * MSF, MSF)]).then_inc(b_set, 1)

                    set_bias(0)
                    for k in range(K):
                        e = i * K + k
                        if k + 1 < K:
                            set_bias(k + 1)
                        dve.wait_ge(gate_done, e + 1)
                        dve.wait_ge(b_set, e + 1)
                        dve.wait_ge(down_done, e - 1 if k > 1 else i * K)
                        for m in range(MSF):
                            ins = dve.scalar_tensor_tensor(out=hidden[k % 2][:, m, :], in0=p_up[k % 2][:, 1, m, :],
                                                           scalar=bias[k % 2][:, 1, m:m + 1], in1=gate[k % 2][:, m, :],
                                                           op0=ALU.add, op1=ALU.mult)
                        ins.then_inc(hidden_done, 1)
                        if k % 2:
                            dve.wait_ge(down_done, e + 1)
                            t = i * 2 + k // 2
                            for b in range(BATCH):
                                ins = dve.tensor_tensor(eout[:, b, ds(t, 1), :], p_out[k // 2][:, b, 0:D].unsqueeze(1), bd[:, ds(t, 1), :],
                                                        ALU.add)
                            ins.then_inc(stored, 1)


def build_program(nc, I, out):
    with ExitStack() as stack:
        class C:
            pass

        def sb(name, shape, dt=F32):
            return stack.enter_context(nc.sbuf_tensor(name, shape, dt))

        C.ident = sb("ident", [P, P])
        C.ones = sb("ones", [P, P])
        C.zeros = sb("zeros", [P, P])
        C.half = sb("half", [P, NT])
        C.neg_half = sb("neg_half", [P, NT])
        C.rms_eps = sb("rms_eps", [P, NT])
        C.neg_one = sb("neg_one", [P, NT])
        X = sb("X", [P, NT, D])
        xn = sb("xn", [P, NT, D])
        xnT = sb("xnT", [P, TOK])
        constants(nc, C)
        ROWS = ("L2_attn_ln_gamma", "L2_attn_ln_beta", "L3_ffn_norm_g", "L3_ffn_norm_b", "L3_ffn_slot_g",
                "L3_ffn_slot_b", "L3_attn_lmlg", "L3_attn_theta", "L3_attn_last_conv_init")
        C.rows = sb("rows", [P, len(ROWS), D])
        C.row = {r: C.rows[:, n, :] for n, r in enumerate(ROWS)}
        b1, b2 = sb("ffn0_b1", [P, MFF]), sb("ffn0_b2", [D, 1])
        C.scale = sb("scale", [P, 1])
        load(nc, "load", [(X[:, b * TPB:(b + 1) * TPB, :], I["L0_attn_x"][b].rearrange("(t p) d -> p t d", p=P))
                          for b in range(BATCH)]
             + [(b1[:, :], I["L0_ffn_b1"].rearrange("(m p) -> p m", p=P)), (b2[:, :], I["L0_ffn_b2"].unsqueeze(1)),
                (C.scale[:, :], I["L3_ffn_scale"].partition_broadcast(P))]
             + [(C.row[r], I[r].partition_broadcast(P)) for r in ROWS])

        def layer_norm(name):
            normalise(nc, C, name, X, xn, xnT)

        with Stage(nc, "ffn0") as S:
            up, down = S.sb("up", [P, DFF], F32R), S.sb("down", [P, MFF, D], F32R)
            ternary_weights(nc, C, "ffn0_w", I["L0_ffn_W1"], I["L0_ffn_W2"], 1e-8, up, down)
            layer_norm("ln0a")
            ffn(nc, C, "ffn0a", X, xnT, up, down, b1, b2[:, 0:1])
            layer_norm("ln0b")
            gated_scan_mixer(nc, C, I, X, xn, xnT)
            layer_norm("ln0c")
            ffn(nc, C, "ffn0b", X, xnT, up, down, b1, b2[:, 0:1])
        layer_norm("ln1a")
        moe_ffn(nc, C, I, "moe_a", X, xnT)
        layer_norm("ln1b")
        stacked_attention_mixer(nc, C, I, X, xn, xnT)
        layer_norm("ln1c")
        moe_ffn(nc, C, I, "moe_b", X, xnT)
        with Stage(nc, "ffn2") as S:
            up, down = S.sb("up", [P, DFF], F32R), S.sb("down", [P, MFF, D], F32R)
            ternary_weights(nc, C, "ffn2_w", I["L2_ffn_w_up"], I["L2_ffn_w_down"], 0.0, up, down)
            layer_norm("ln2a")
            normalise(nc, C, "ln2a_rms", xn, xn, xnT, kind="rms")
            ffn(nc, C, "ffn2a", X, xnT, up, down, rms=True)
            layer_norm("ln2b")
            alibi_attention_mixer(nc, C, I, X, xn, xnT)
            layer_norm("ln2c")
            normalise(nc, C, "ln2c_rms", xn, xn, xnT, kind="rms")
            ffn(nc, C, "ffn2b", X, xnT, up, down, rms=True)
        with Stage(nc, "ffn3") as S:
            se_parts = [S.sb(f"se_{part}", [P, NSLOT], F32R) for part in ("high", "low")]
            slot_directions(nc, C, I, se_parts)
            layer_norm("ln3a")
            soft_moe_ffn(nc, C, I, "ffn3a", X, xn, xnT, se_parts)
            layer_norm("ln3b")
            resonant_mixer(nc, C, X, xn)
            layer_norm("ln3c")
            soft_moe_ffn(nc, C, I, "ffn3b", X, xn, xnT, se_parts)
        store_outputs(nc, X, out)


def load(nc, name, pairs):
    with Stage(nc, name) as S:
        loaded = S.sem("loaded")
        with nc.Block() as block:

            @block.sync
            def _(sp):
                for dst, src in pairs:
                    sp.dma_start(dst, src, allow_slow_non_contiguous=True).then_inc(loaded, 16)
                sp.wait_ge(loaded, 16 * len(pairs))


def store_outputs(nc, X, out):
    with Stage(nc, "store_x") as S:
        stored = S.sem("stored")
        with nc.Block() as block:

            @block.sync
            def _(sp):
                for b in range(BATCH):
                    sp.dma_start(out[b].rearrange("(t p) d -> p t d", p=P),
                                 X[:, b * TPB:(b + 1) * TPB, :]).then_inc(stored, 16)
                sp.wait_ge(stored, 16 * BATCH)


_INS = ['L0_attn_x', 'L0_attn_Wq', 'L0_attn_Wk', 'L0_attn_Wv', 'L0_attn_Wf', 'L0_attn_bf', 'L0_attn_Wg',
        'L0_attn_Wout', 'L0_attn_gamma', 'L0_attn_beta', 'L0_ffn_W1', 'L0_ffn_b1', 'L0_ffn_W2', 'L0_ffn_b2',
        'L1_attn_W_attn', 'L1_attn_b_attn', 'L1_attn_W_k2', 'L1_attn_b_k2', 'L1_attn_W_proj', 'L1_attn_b_proj',
        'L1_ffn_Wr', 'L1_ffn_br', 'L1_ffn_W1', 'L1_ffn_b1', 'L1_ffn_W2', 'L1_ffn_b2', 'L2_attn_ln_gamma',
        'L2_attn_ln_beta', 'L2_attn_Wq', 'L2_attn_Wk', 'L2_attn_Wv', 'L2_attn_Wo', 'L2_ffn_w_up', 'L2_ffn_w_down',
        'L3_attn_lmlg', 'L3_attn_theta', 'L3_attn_last_conv_init', 'L3_ffn_norm_g', 'L3_ffn_norm_b',
        'L3_ffn_slot_g', 'L3_ffn_slot_b', 'L3_ffn_scale', 'L3_ffn_slot_embeds', 'L3_ffn_Wg', 'L3_ffn_bg',
        'L3_ffn_Wu', 'L3_ffn_bu', 'L3_ffn_Wd', 'L3_ffn_bd']


def kernel(**inputs):
    import numpy as _np
    import concourse.bacc as _bacc
    from concourse import mybir as _mybir
    from concourse.bass_utils import run_bass_kernel_spmd as _run

    nc = _bacc.Bacc("TRN2", target_bir_lowering=False, num_devices=1)
    arrays, ins = {}, {}
    for name in _INS:
        a = _np.ascontiguousarray(inputs[name])
        arrays[f"in_{name}_dram"] = a
        ins[name] = nc.dram_tensor(f"in_{name}_dram", a.shape, _mybir.dt.from_np(a.dtype), kind="ExternalInput").ap()
    out = nc.dram_tensor("out_0_dram", (BATCH, SEQ, D), _mybir.dt.float32, kind="ExternalOutput").ap()
    build_program(nc, ins, out)
    r = _run(nc, [arrays], core_ids=[0])
    return r.results[0]["out_0_dram"]
```
